# Optimizing a Trainium2 kernel written in Bass

```python
import numpy as np
import jax
import jax.numpy as jnp

def _softmax(x, axis=-1):
    return jax.nn.softmax(x, axis=axis)

def _gelu(x):
    return jax.nn.gelu(x, approximate=True)

def _silu(x):
    return jax.nn.silu(x)

def _sigmoid(x):
    return jax.nn.sigmoid(x)

def _layernorm(x, axis=-1, eps=1e-05):
    m = jnp.mean(x, axis=axis, keepdims=True)
    v = jnp.var(x, axis=axis, keepdims=True)
    return (x - m) / jnp.sqrt(v + eps)

def _scatter_add(tgt, idx, src, axis=0):
    return tgt.at[idx].add(src)

def _segment_sum(src, seg, n):
    return jax.ops.segment_sum(src, seg, n)
kernel_name = 'mk_gnn_preln_d2_gnn_r64_f3a61f'

def setup_inputs(seed: int=0):
    np.random.seed(seed)
    _w = jnp.asarray

    def _rec_inputs():
        import jax
        import jax.numpy as jnp
        _gk = jax.random.key(seed)
        x = -5.025e-05 + 0.9999 * jax.random.normal(jax.random.fold_in(_gk, 1), (100000, 64), jnp.float32)
        src = jax.random.randint(jax.random.fold_in(_gk, 2), (50000,), 0, 100000, jnp.int32)
        dst = jnp.minimum((100000 * jax.random.uniform(jax.random.fold_in(_gk, 3), (50000,)) ** 2.0).astype(jnp.int32), 99999)
        _o = jnp.argsort(dst, stable=True)
        src = src[_o]
        dst = dst[_o]
        edge_attr_64 = -2.25437e-05 + 0.999858 * jax.random.normal(jax.random.fold_in(_gk, 12), (50000, 64), jnp.float32)
        edge_type_32 = jax.random.randint(jax.random.fold_in(_gk, 14), (50000,), 0, 32, jnp.int32)
        return (x, src, dst, edge_attr_64, edge_type_32)
    x, src, dst, edge_attr_64, edge_type_32 = _rec_inputs()

    def _L0_gnn_setup():
        import jax, jax.numpy as jnp
        import numpy as np
        N = 15625
        IN, HID, OUT = (64, 128, 64)

        def _gcn_layer(x, W, b, src, dst, n):
            h = x @ W
            deg = jnp.zeros((n,), x.dtype).at[dst].add(1.0) + 1.0
            dinv = jax.lax.rsqrt(deg)
            norm = dinv[src] * dinv[dst]
            agg = jnp.zeros((n, h.shape[1]), h.dtype).at[dst].add(h[src] * norm[:, None])
            return agg + h * (dinv * dinv)[:, None] + b
        key = jax.random.key(seed)
        k1, k2, k3 = jax.random.split(key, 3)
        x = jax.random.normal(k1, (N, IN), jnp.float32)
        i = jnp.arange(N - 1)
        edge_index = jnp.stack([jnp.concatenate([i, i + 1]), jnp.concatenate([i + 1, i])]).astype(jnp.int64)
        W1 = jax.random.normal(k2, (IN, HID), jnp.float32) * (1.0 / np.sqrt(IN))
        b1 = jnp.zeros((HID,), jnp.float32)
        W2 = jax.random.normal(k3, (HID, OUT), jnp.float32) * (1.0 / np.sqrt(HID))
        b2 = jnp.zeros((OUT,), jnp.float32)
        return {'x': x, 'edge_index': edge_index, 'W1': W1, 'b1': b1, 'W2': W2, 'b2': b2}
    _L0_gnn_all = _L0_gnn_setup()
    _L0_gnn_in = {k: v for k, v in _L0_gnn_all.items() if k in ('W1', 'b1', 'W2', 'b2')}
    del _L0_gnn_all

    def _L1_gnn_setup():
        import jax, jax.numpy as jnp
        import numpy as np
        NEG_SLOPE = 0.01
        N, E, D, R = (100000, 15625, 64, 32)
        key = jax.random.key(seed)
        ks = jax.random.split(key, 8)
        return {'nfeat': jax.random.normal(ks[0], (N, D), dtype=jnp.float32), 'efeat': jax.random.normal(ks[1], (E, D), dtype=jnp.float32), 'src': jax.random.randint(ks[2], (E,), 0, N, dtype=jnp.int32), 'dst': jax.random.randint(ks[3], (E,), 0, N, dtype=jnp.int32), 'etype': jax.random.randint(ks[4], (E,), 0, R, dtype=jnp.int32), 'relation_weight': jax.random.normal(ks[5], (R, D, D), dtype=jnp.float32) * 0.05, 'res_w1': jax.random.normal(ks[6], (D, D), dtype=jnp.float32) * 0.05, 'res_w2': jax.random.normal(ks[7], (D, D), dtype=jnp.float32) * 0.05}
    _L1_gnn_all = _L1_gnn_setup()
    _L1_gnn_in = {k: v for k, v in _L1_gnn_all.items() if k in ('relation_weight', 'res_w1', 'res_w2')}
    del _L1_gnn_all
    return {'x': x, 'src': src, 'dst': dst, 'edge_attr_64': edge_attr_64, 'edge_type_32': edge_type_32, 'L0_gnn_W1': _L0_gnn_in['W1'], 'L0_gnn_b1': _L0_gnn_in['b1'], 'L0_gnn_W2': _L0_gnn_in['W2'], 'L0_gnn_b2': _L0_gnn_in['b2'], 'L1_gnn_relation_weight': _L1_gnn_in['relation_weight'], 'L1_gnn_res_w1': _L1_gnn_in['res_w1'], 'L1_gnn_res_w2': _L1_gnn_in['res_w2']}

def reference(x, src, dst, edge_attr_64, edge_type_32, L0_gnn_W1, L0_gnn_b1, L0_gnn_W2, L0_gnn_b2, L1_gnn_relation_weight, L1_gnn_res_w1, L1_gnn_res_w2):
    import jax
    import jax.numpy as jnp

    def _L0_gnn_ref(x, edge_index, W1, b1, W2, b2):
        import jax, jax.numpy as jnp
        import numpy as np
        N = 15625
        IN, HID, OUT = (64, 128, 64)

        def _gcn_layer(x, W, b, src, dst, n):
            h = x @ W
            deg = jnp.zeros((n,), x.dtype).at[dst].add(1.0) + 1.0
            dinv = jax.lax.rsqrt(deg)
            norm = dinv[src] * dinv[dst]
            agg = jnp.zeros((n, h.shape[1]), h.dtype).at[dst].add(h[src] * norm[:, None])
            return agg + h * (dinv * dinv)[:, None] + b
        src, dst = (edge_index[0], edge_index[1])
        n = x.shape[0]
        h = _gcn_layer(x, W1, b1, src, dst, n)
        h = jax.nn.relu(h)
        out = _gcn_layer(h, W2, b2, src, dst, n)
        return out

    def _L1_gnn_ref(nfeat, efeat, src, dst, etype, relation_weight, res_w1, res_w2):
        import jax, jax.numpy as jnp
        import numpy as np
        NEG_SLOPE = 0.01
        N, D = nfeat.shape
        h = nfeat
        h_proj = jnp.einsum('nd,rde->rne', h, relation_weight)
        t_r = h_proj[etype, src]
        h_r = h_proj[etype, dst]
        att = jnp.sum(t_r * jnp.tanh(h_r + efeat), axis=-1)
        seg_max = jax.lax.stop_gradient(jax.ops.segment_max(att, dst, num_segments=N))
        att_exp = jnp.exp(att - seg_max[dst])
        denom = jax.ops.segment_sum(att_exp, dst, num_segments=N)
        a = att_exp / denom[dst]
        msg = h[src] * a[:, None]
        h_nb = jax.ops.segment_sum(msg, dst, num_segments=N)
        out = jax.nn.leaky_relu((h + h_nb) @ res_w1.T, NEG_SLOPE) + jax.nn.leaky_relu(h * h_nb @ res_w2.T, NEG_SLOPE)
        return out
    edge_index = jnp.stack([src, dst])
    h = jnp.maximum(_layernorm(x, axis=-1), 0.0)
    x = x + _L0_gnn_ref(h, edge_index, L0_gnn_W1, L0_gnn_b1, L0_gnn_W2, L0_gnn_b2)
    h = jnp.maximum(_layernorm(x, axis=-1), 0.0)
    x = x + _L1_gnn_ref(h, edge_attr_64, src, dst, edge_type_32, L1_gnn_relation_weight, L1_gnn_res_w1, L1_gnn_res_w2)
    return x

_drawn_inputs = setup_inputs


def setup_inputs(seed=0):
    import zlib

    import numpy as np

    out = dict(_drawn_inputs(seed))
    spreads = {'L0_gnn_b1': (0.0, 0.1), 'L0_gnn_b2': (0.0, 0.1)}
    factors = {}
    for name, (base, spread) in spreads.items():
        noise = np.random.default_rng([zlib.crc32(name.encode()), seed]).standard_normal(out[name].shape)
        drawn = base * np.exp(spread * noise) if base else spread * noise
        out[name] = jnp.asarray(drawn.astype(out[name].dtype))
    for name, factor in factors.items():
        out[name] = (out[name] * factor).astype(out[name].dtype)
    return out
```

```python
from contextlib import ExitStack

import concourse.bass as bass
from concourse import mybir

ALU = mybir.AluOpType
ACT = mybir.ActivationFunctionType
AX = mybir.AxisListType
F32 = mybir.dt.float32
F16 = mybir.dt.float16
I32 = mybir.dt.int32

P = 128
N = 100000
E = 50000
D = 64
HID = 128
R = 32
EPS = 1e-5

CB = 32
BROWS = P * CB
NB = -(-N // BROWS)
NPAD = NB * BROWS
KN = NB * CB
BW = CB * D
TAIL_P = (N - (NB - 1) * BROWS) // CB
TAIL_SPLIT = TAIL_P // 16 * 16

KE = 392
EFULL = E // KE
ETAIL = E - EFULL * KE
GT = 14
GE = KE // GT
EPAD = P * KE
ESPLIT = 112

KS = 424
GS = 4
NGS = KS // GS
RW = D + 3
MW = D + 1
HW = 2 * D + 1

KEY_PAD = 1 << 20
SKIP = 1 << 20
SLOT_SKIP = 1 << 23
ROW_SKIP = 1 << 21
FAR = 1e30
MM = 512


def after(eng, sem, value):
    if isinstance(value, int) and value <= 0:
        return
    eng.wait_ge(sem, value)


class Order:

    def __init__(self, eng, sem):
        self.eng, self.sem, self.n = eng, sem, 0

    def did(self, ins):
        ins.then_inc(self.sem, 1)
        self.n += 1

    def wait(self):
        self.eng.wait_ge(self.sem, self.n)


def build(nc, x, src, dst, eattr, etype, w1, b1, w2, b2, relw, rw1, rw2, out):
    with ExitStack() as ctx:
        def sb(name, shape, dt=F32):
            return ctx.enter_context(nc.sbuf_tensor(name, shape, dt))

        def sem(name):
            return ctx.enter_context(nc.semaphore(name))

        def sem2(name):
            return [sem(name + "_even"), sem(name + "_odd")]

        g0_t = nc.dram_tensor("g0_table", (NPAD, D), F32).ap()
        g1_t = nc.dram_tensor("g1_table", (NPAD, D), F32).ap()
        agg_t = nc.dram_tensor("agg_table", (NPAD, D), F32).ap()
        x1_t = nc.dram_tensor("x1_table", (NPAD, D), F32).ap()
        h_t = nc.dram_tensor("h_table", (NPAD, D), F32).ap()
        slot_t = nc.dram_tensor("slot_table", (P * KS, RW), F32).ap()
        edge_t = nc.dram_tensor("edge_table", (1 + EPAD, MW), F32).ap()

        ident = sb("ident", [P, P])
        upper = sb("upper", [P, P])
        ones = sb("ones", [P, P])
        dsti = sb("dsti", [P, KE + 1], I32)
        srci = sb("srci", [P, KE], I32)
        relf = sb("relf", [P, KE])
        eidi = sb("eidi", [P, KE], I32)
        meta = sb("meta", [P, KE, 3], I32)
        key = sb("key", [P, KE + 1])
        same = sb("same", [P, KE + 1])
        head = sb("head", [P, KE])
        outi = sb("outi", [P, KE], I32)
        slot_row = sb("slot_row", [P, KE], I32)
        tmp_a = sb("tmp_a", [P, KE + 1])
        tmp_b = sb("tmp_b", [P, KE + 1])
        tmp_i = sb("tmp_i", [P, KE], I32)
        tmp_j = sb("tmp_j", [P, KE], I32)
        lo_key = sb("lo_key", [P, KE])
        hi_key = sb("hi_key", [P, KE])
        pos = sb("pos", [P, KE])
        onesk = sb("onesk", [P, KE])
        cnt = sb("cnt", [P, 6, R])
        cnti = sb("cnti", [P, 2, R], I32)
        base = sb("base", [P, R])
        diag = sb("diag", [P, P])
        first_row = sb("first_row", [P, P])
        carry = sb("carry", [P, P])
        fix_i = sb("fix_i", [P, 1], I32)
        fix_f = sb("fix_f", [P, 2])
        dinv = sb("dinv", [P, KN])
        tile_rel = sb("tile_rel", [1, 2, KS])
        tile_reli = sb("tile_reli", [1, KS], I32)
        w1_sb = sb("w1_sb", [P, HID])
        w2_sb = sb("w2_sb", [P, D])
        b1_sb = sb("b1_sb", [P, 1])
        b2_sb = sb("b2_sb", [P, D])
        rel_sb = sb("rel_sb", [P, R, P])
        res_in = sb("res_in", [P, P])
        res_sb = sb("res_sb", [P, P])
        stat = sb("stat", [P, 2, 6, CB])
        gbuf = sb("gbuf", [P, 2, GT, MW])
        rbuf = sb("rbuf", [P, 2, GT, MW])
        sbuf = sb("sbuf", [P, 2, GT, D])
        rden = sb("rden", [P, 2, 2, GT])
        hsum = sb("hsum", [P, MW])
        fixrow = sb("fixrow", [P, MW])
        fixden = sb("fixden", [P, 2])
        fixout = sb("fixout", [P, D])
        src_idx = sb("src_idx", [P, 2, GT], I32)
        out_idx = sb("out_idx", [P, 2, GT], I32)
        slot_e = sb("slot_e", [P, 2, 2, GS])
        slot_idx = sb("slot_idx", [P, 2, GS], I32)
        smax = sb("smax", [P, 2])
        diag_max = sb("diag_max", [P, 2, P])
        seen = sb("seen", [P, 2 * P])
        perm_buf = sb("perm_buf", [P, 2, GT, RW])
        arena = sb("arena", [P, KE * MW])

        def part(buffer, at, shape, dt=F32):
            n = 1
            for k in shape:
                n *= k
            flat = buffer if len(buffer.shape) == 2 else buffer[:].rearrange("p a b c -> p (a b c)")
            words = flat[:, at:at + (n + 1) // 2] if dt == F16 else flat[:, at:at + n]
            words = words if dt == F32 else words.bitcast(dt)
            if len(shape) == 1:
                return words
            if len(shape) == 2:
                return words.rearrange("p (a b) -> p a b", b=shape[1])
            return words.rearrange("p (a b c) -> p a b c", b=shape[1], c=shape[2])

        iota_h = part(arena, 8 * BW, [KN], F16)
        lo_hot = part(arena, 8 * BW + KN // 2, [4, P], F16)
        hi_hot = part(arena, 8 * BW + KN // 2 + 2 * P, [4, KN], F16)
        degs = part(arena, 8 * BW + KN // 2 + 2 * P + 2 * KN, [2, KN])
        zero = part(arena, 10 * BW, [KS * RW // 8])
        iota_i = part(arena, 10 * BW + KS * RW // 8, [KN], I32)
        slot_in = part(perm_buf, 0, [2, GS, RW])
        slot_ht = part(gbuf, 0, [2, GS, P])
        slot_h = part(rbuf, 0, [2, GS, HW])
        slot_z = part(sbuf, 0, [2, GS, D])
        slot_th = part(sbuf, 2 * GS * D, [2, GS, D])
        slot_q = part(sbuf, 4 * GS * D, [2, GS, D])
        turned3 = part(gbuf, 0, [2, MM])
        low3 = part(rbuf, 0, [2, MM])
        leaky3 = part(sbuf, 0, [2, MM])
        halves3 = part(sbuf, 2 * MM, [2, 4, D])
        block_at = [arena[:, k * BW:(k + 1) * BW] for k in range(KE * MW // BW)]
        banks = ctx.enter_context(nc.psum_tensor("banks", [P, 8, MM], F32))

        def cols(ap):
            return ap.rearrange("p (c f) -> p c f", f=D)

        def bank(k, n=1):
            return banks[:, k:k + n, :].rearrange("p a b -> p (a b)")

        filled, loaded, consts = sem("filled"), sem("inputs_loaded"), sem("pool_constants")
        prep, prep_pe, prep_ready = sem("prep_steps"), sem("prep_products"), sem("indices_ready")
        slots_zeroed, agg_zeroed, pads_zeroed = sem("slots_zeroed"), sem("agg_zeroed"), sem("edge_pads_zeroed")
        perm_loaded, perm_meta, perm_sent = sem2("perm_loaded"), sem2("perm_meta"), sem2("perm_sent")
        perm_tail, waits_over = sem("perm_tail"), sem("waits_over")
        hot_made, hot_used, deg_read = sem("one_hots_made"), sem("one_hots_used"), sem("degree_read")
        deg_root, dinv_ready = sem("degree_root"), sem("dinv_ready")

        def rows(table, b, parts=P, first=0):
            if isinstance(b, int):
                at = b * BROWS + first * CB
                return table[at:at + parts * CB, :].rearrange("(p c) f -> p (c f)", c=CB)
            return table[bass.ds(b * BROWS, BROWS), :].rearrange("(p c) f -> p (c f)", c=CB)

        def move_block(eng, dram, slot, b, signal, store):
            if isinstance(b, int) and b == NB - 1 and dram.shape[0] == N:
                parts = [(0, TAIL_SPLIT), (TAIL_SPLIT, TAIL_P)]
            else:
                parts = [(0, P)]
            for lo, hi in parts:
                there, here = rows(dram, b, hi - lo, lo), slot[lo:hi, :]
                eng.dma_start(there if store else here, here if store else there).then_inc(signal, 16)

        def blocks(eng, step):
            step(0, 0, 0)
            step(1, 1, 0)
            with eng.Fori(1, NB // 2) as i:
                step(2 * i, 0, i)
                step(2 * i + 1, 1, i)
            step(NB - 1, 0, NB // 2)

        pass0 = {k: sem("p0_" + k) for k in
                 ("sum", "mean", "centered", "square", "var", "vare", "std", "rstd", "coef", "g")}
        x_in0, g0_out = sem2("p0_x_loaded"), sem2("p0_g0_stored")
        pass1 = {k: sem("p1_" + k) for k in ("sum", "a", "turned", "at", "h", "relu", "u", "g")}
        agg_in1, g_in1, g1_out = sem2("p1_agg_loaded"), sem2("p1_g0_loaded"), sem2("p1_g1_stored")
        pass2 = {k: sem("p2_" + k) for k in
                 ("xb", "sum", "scaled", "x1", "rowsum", "mean", "centered", "square", "var", "vare", "std", "rstd", "h")}
        in2 = sem2("p2_loaded")
        x1_out, h_out = sem2("p2_x1_stored"), sem2("p2_h_stored")
        pass3 = {k: sem("p3_" + k) for k in ("sum", "prod", "turned", "t", "o", "low", "leaky", "res", "out")}
        in3, out3 = sem2("p3_loaded"), sem2("p3_stored")

        def edge_sems(name):
            return {
                "src_idx": sem2(name + "_src_idx"), "out_idx": sem2(name + "_out_idx"),
                "got": sem2(name + "_rows_here"), "run": sem(name + "_run"), "head": sem(name + "_head"),
                "sent": sem2(name + "_sums_sent"), "carry": sem(name + "_carry"), "fix": sem(name + "_fix"),
                "fixed": sem(name + "_fixed"), "norm": sem(name + "_norm"), "fixsteps": sem(name + "_fix_steps"),
                "clear": sem(name + "_cleared"),
            }
        e1, e2, e3 = edge_sems("e1"), edge_sems("e2"), edge_sems("e3")
        rel = {k: sem("rel_" + k) for k in ("pad", "idx", "turned", "ht", "tr", "z", "th", "q", "att")}
        rel_in, rel_got, rel_sent = sem2("rel_loaded"), sem2("rel_rows_here"), sem2("rel_sent")
        edges_in, soft, soft_pe, soft_exp = sem("edges_loaded"), sem("softmax_steps"), sem("softmax_rows"), sem("weights_ready")

        seg_max, weighted, quotient = sem("segment_maxima"), sem("rows_weighted"), sem("quotient_steps")
        at_step = {}

        PERM_DONE = 16 * GT * (GE // 2)
        SUMS_DONE = 16 * GT * (GE // 2)
        REL_DONE = 16 * GS * (NGS // 2)
        N_LOADS = 18 + 2 + 1
        stored_all = [NB // 2 + 1, NB // 2]

        block = ctx.enter_context(nc.Block())

        @block.sync
        def _(sp):
            count = [0]

            def load(to, of):
                sp.dma_start(to, of).then_inc(loaded, 16)
                count[0] += 1

            def load_edges(tile, vec):
                full = vec[0:EFULL * KE].rearrange("(p t) -> p t", t=KE)
                load(tile[0:ESPLIT, 0:KE], full[0:ESPLIT, :])
                load(tile[ESPLIT:EFULL, 0:KE], full[ESPLIT:EFULL, :])
                load(tile[EFULL:P, 0:ETAIL], vec[EFULL * KE:E].unsqueeze(0))

            sp.wait_ge(filled, 1)
            load_edges(dsti, dst)
            load_edges(tmp_j, etype)
            load_edges(srci, src)
            ctx.enter_context(nc.allow_non_contiguous_dma(reason="one number in each partition"))
            later = dst[KE:EFULL * KE].rearrange("(p t) -> p t", t=KE)
            load(dsti[0:ESPLIT, KE:KE + 1], later[0:ESPLIT, 0:1])
            load(dsti[ESPLIT:EFULL - 1, KE:KE + 1], later[ESPLIT:EFULL - 1, 0:1])
            load(dsti[EFULL - 1:EFULL, KE:KE + 1], dst[EFULL * KE:EFULL * KE + 1].unsqueeze(0))
            load(w1_sb[0:D, :], w1)
            load(w1_sb[D:P, :], w1)
            load(w2_sb[:], w2)
            load(b1_sb[:], b1.unsqueeze(1))
            load(b2_sb[:], b2.partition_broadcast(P))
            load(res_in[0:D, 0:D], rw1)
            load(res_in[D:P, D:P], rw2)
            load(rel_sb[0:D, :, 0:D], relw.rearrange("r d e -> d r e"))
            load(rel_sb[D:P, :, D:P], relw.rearrange("r d e -> d r e"))
            assert count[0] == N_LOADS, count[0]
            wide = KS * RW // 8
            lanes = slot_t.rearrange("(l s) w -> l (s w)", l=P)
            for k in range(8):
                sp.dma_start(lanes[:, k * wide:(k + 1) * wide], zero).then_inc(slots_zeroed, 16)
            flat = agg_t.rearrange("(l s) w -> l (s w)", l=P)
            aw = KN * D // 16
            for k in range(16):
                sp.dma_start(flat[:, k * aw:(k + 1) * aw], zero[:, 0:aw]).then_inc(agg_zeroed, 16)
            pads = edge_t[E + 1:EPAD + 1, :].rearrange("(l s) w -> l (s w)", s=2)
            sp.dma_start(pads, zero[0:(EPAD - E) // 2, 0:2 * MW]).then_inc(pads_zeroed, 16)

            def load0(b, q, u):
                after(sp, pass0["centered"], b - 1)
                move_block(sp, x, block_at[q], b, x_in0[q], store=False)

            def store0(b, q, u):
                sp.wait_ge(pass0["g"], b + 1)
                move_block(sp, g0_t, block_at[6 + q], b, g0_out[q], store=True)

            def two_ahead(load, store):
                def step(b, q, u):
                    if not (isinstance(b, int) and b == NB - 1):
                        load(b + 1, 1 - q, u + q)
                    store(b, q, u)
                load(0, 0, 0)
                step(0, 0, 0)
                step(1, 1, 0)
                with sp.Fori(1, NB // 2 - 1) as i:
                    step(2 * i, 0, i)
                    step(2 * i + 1, 1, i)
                step(NB - 3, 0, NB // 2 - 1)
                step(NB - 2, 1, NB // 2 - 1)
                step(NB - 1, 0, NB // 2)

            two_ahead(load0, store0)

            for q in range(2):
                sp.wait_ge(e1["sent"][q], SUMS_DONE)
            sp.wait_ge(e1["fixed"], 16)

            def load1(b, q, u):
                after(sp, pass1["turned"], 4 * (b - 1))
                move_block(sp, agg_t, block_at[q], b, agg_in1[q], store=False)
                move_block(sp, g0_t, block_at[2 + q], b, g_in1[q], store=False)

            def store1(b, q, u):
                sp.wait_ge(pass1["g"], 4 * (b + 1))
                move_block(sp, g1_t, block_at[4 + q], b, g1_out[q], store=True)

            two_ahead(load1, store1)

            for q in range(2):
                sp.wait_ge(e2["sent"][q], SUMS_DONE)
            sp.wait_ge(e2["fixed"], 16)

            def load2(b, q, u):
                after(sp, pass2["h"], b - 1)
                move_block(sp, x, block_at[q], b, in2[q], store=False)
                move_block(sp, agg_t, block_at[2 + q], b, in2[q], store=False)
                move_block(sp, g1_t, block_at[4 + q], b, in2[q], store=False)

            def store2(b, q, u):
                sp.wait_ge(pass2["x1"], b + 1)
                move_block(sp, x1_t, block_at[8 + q], b, x1_out[q], store=True)
                sp.wait_ge(pass2["h"], b + 1)
                move_block(sp, h_t, block_at[10 + q], b, h_out[q], store=True)

            two_ahead(load2, store2)

            for q in range(2):
                sp.wait_ge(perm_sent[q], PERM_DONE)

            def load_slots(j, q, u):
                after(sp, rel["z"], j - 1)
                by_lane = slot_t.rearrange("(l s) w -> l s w", l=P)
                sp.dma_start(slot_in[:, q], by_lane[:, bass.ds(j * GS, GS), :]).then_inc(rel_in[q], 16)

            for j in range(2):
                load_slots(j, j, 0)
            with sp.Fori(1, NGS // 2) as i:
                load_slots(2 * i, 0, i)
                load_slots(2 * i + 1, 1, i)

            for q in range(2):
                sp.wait_ge(rel_sent[q], REL_DONE)
            sp.wait_ge(pads_zeroed, 16)
            by_edge = edge_t[1:EPAD + 1, :].rearrange("(p t) w -> p (t w)", p=P)
            half = KE // 2 * MW
            for k in range(2):
                sp.dma_start(arena[:, k * half:(k + 1) * half],
                             by_edge[:, k * half:(k + 1) * half]).then_inc(edges_in, 16)

            for q in range(2):
                sp.wait_ge(e3["sent"][q], SUMS_DONE)
            sp.wait_ge(e3["fixed"], 16)

            def load3(b, q, u):
                after(sp, pass3["out"], 8 * (b - 1))
                move_block(sp, h_t, block_at[q], b, in3[q], store=False)
                move_block(sp, agg_t, block_at[2 + q], b, in3[q], store=False)
                move_block(sp, x1_t, block_at[4 + q], b, in3[q], store=False)

            def store3(b, q, u):
                sp.wait_ge(pass3["out"], 8 * (b + 1))
                move_block(sp, out, block_at[10 + q], b, out3[q], store=True)

            two_ahead(load3, store3)
            sp.wait_ge(out3[0], 16 * (stored_all[0] + 1))
            sp.wait_ge(out3[1], 16 * stored_all[1])

        @block.gpsimd
        def _(pool):
            pool.iota(iota_i, pattern=[[1, KN]], base=0, channel_multiplier=0).then_inc(consts, 1)
            pool.iota(eidi[:], pattern=[[1, KE]], base=1, channel_multiplier=KE).then_inc(consts, 1)
            pool.wait_ge(filled, 1)
            pool.affine_select(out=ident[:], in_=ones[:], compare_op=ALU.is_equal, fill=0.0, base=0,
                               pattern=[[1, P]], channel_multiplier=-1).then_inc(consts, 1)
            pool.affine_select(out=upper[:], in_=ones[:], compare_op=ALU.is_gt, fill=0.0, base=0,
                               pattern=[[1, P]], channel_multiplier=-1).then_inc(consts, 1)

            def alone():
                pool.sem_inc(waits_over, 1)

            def scatter(table, idx, of, bound, signal):
                pool.indirect_dma_start(out=table[:, :], out_offset=bass.IndirectOffsetOnAxis(ap=idx, axis=0),
                                        in_=of, in_offset=None, bounds_check=bound,
                                        oob_is_err=False).then_inc(signal, 16)

            def gather(to, table, idx, signal):
                pool.indirect_dma_start(out=to, out_offset=None, in_=table[:, :],
                                        in_offset=bass.IndirectOffsetOnAxis(ap=idx, axis=0)).then_inc(signal, 16)

            pool.wait_ge(prep_ready, 1)
            pool.wait_ge(slots_zeroed, 16 * 8)
            eat = eattr[0:EFULL * KE, :].rearrange("(p t) f -> p t f", t=KE)

            def perm_load(g, q, u, kind):
                after(pool, perm_sent[q], 16 * GT * u)
                alone()
                if kind == "whole":
                    for lo, hi in ((0, ESPLIT), (ESPLIT, EFULL)):
                        pool.dma_start(perm_buf[lo:hi, q, :, 0:D], eat[lo:hi, bass.ds(g * GT, GT), :]).then_inc(perm_loaded[q], 16)
                    pool.dma_start(perm_buf[EFULL:P, q, :, 0:D],
                                   eattr[bass.ds(g * GT + EFULL * KE, GT), :].unsqueeze(0)).then_inc(perm_loaded[q], 16)
                else:
                    for lo, hi in ((0, ESPLIT), (ESPLIT, EFULL)):
                        pool.dma_start(perm_buf[lo:hi, q, :, 0:D], eat[lo:hi, bass.ds(g * GT, GT), :]).then_inc(perm_loaded[q], 16)
                    if kind == "part":
                        left = ETAIL - g * GT
                        pool.dma_start(perm_buf[EFULL:P, q, 0:left, 0:D], eattr[E - left:E, :].unsqueeze(0)).then_inc(perm_tail, 16)
                pool.tensor_copy(perm_buf[:].bitcast(I32)[:, q, :, D:RW], meta[:, bass.ds(g * GT, GT), :]).then_inc(perm_meta[q], 1)
                pool.tensor_copy(out_idx[:, q, :], slot_row[:, bass.ds(g * GT, GT)]).then_inc(perm_meta[q], 1)

            def perm_send(g, q, u, loads):
                pool.wait_ge(perm_loaded[q], loads)
                pool.wait_ge(perm_meta[q], 2 * (u + 1))
                alone()
                for k in range(GT):
                    scatter(slot_t, out_idx[:, q, k:k + 1], perm_buf[:, q, k, :], P * KS - 1, perm_sent[q])

            whole = ETAIL // GT
            assert whole % 2 == 1 and whole < GE
            def perm(g, q, u, kind):
                perm_load(g, q, u, kind)
                w = (whole + 1) // 2 if q == 0 else whole // 2
                after_whole = 48 * w
                loads = 48 * (u + 1) if kind == "whole" else after_whole + 32 * (u + 1 - w)
                perm_send(g, q, u, loads)

            perm(0, 0, 0, "whole")
            perm(1, 1, 0, "whole")
            with pool.Fori(1, whole // 2) as i:
                perm(2 * i, 0, i, "whole")
                perm(2 * i + 1, 1, i, "whole")
            perm(whole - 1, 0, whole // 2, "whole")
            perm_load(whole, 1, whole // 2, "part")
            pool.wait_ge(perm_tail, 16)
            perm_send(whole, 1, whole // 2, 48 * (whole // 2) + 32)
            with pool.Fori((whole + 1) // 2, GE // 2) as i:
                perm(2 * i, 0, i, "none")
                perm(2 * i + 1, 1, i, "none")
            for q in range(2):
                pool.wait_ge(perm_sent[q], PERM_DONE)

            def send_sums(s, g, q, u, made, of):
                pool.wait_ge(s["out_idx"][q], u + 1)
                pool.wait_ge(made, g + 1 if made is s["norm"] else GT * (g + 1))
                alone()
                for k in range(GT):
                    scatter(agg_t, out_idx[:, q, k:k + 1], of(q, k), N - 1, s["sent"][q])

            def edge_phase(s, table):
                def get(g, q, u):
                    pool.wait_ge(s["src_idx"][q], u + 1)
                    after(pool, s["head"], GT * (g - 1))
                    alone()
                    for k in range(GT):
                        gather(gbuf[:, q, k, 0:D], table, src_idx[:, q, k:k + 1], s["got"][q])

                def send(g, q, u):
                    send_sums(s, g, q, u, s["head"], lambda q, k: rbuf[:, q, k, 0:D])

                get(0, 0, 0)
                get(1, 1, 0)
                send(0, 0, 0)
                with pool.Fori(1, GE // 2) as i:
                    get(2 * i, 0, i)
                    send(2 * i - 1, 1, i - 1)
                    get(2 * i + 1, 1, i)
                    send(2 * i, 0, i)
                send(GE - 1, 1, GE // 2 - 1)
                fix(s, fixrow[:, 0:D])

            def fix(s, row):
                pool.wait_ge(s["fix"], 1)
                scatter(agg_t, fix_i[:, 0:1], row, N - 1, s["fixed"])

            for q in range(2):
                pool.wait_ge(g0_out[q], 16 * stored_all[q])
            pool.wait_ge(agg_zeroed, 16 * 16)
            edge_phase(e1, g0_t)
            for q in range(2):
                pool.wait_ge(g1_out[q], 16 * stored_all[q])
            edge_phase(e2, g1_t)

            def share2(b, q, u):
                pool.wait_ge(in2[q], 48 * (u + 1) + (16 if isinstance(b, int) and b == NB - 1 else 0))
                pool.tensor_tensor(cols(block_at[q]), cols(block_at[q]),
                                   b2_sb[:].unsqueeze(1).to_broadcast([P, CB, D]), ALU.add).then_inc(pass2["xb"], 1)
                pool.tensor_tensor(block_at[2 + q], block_at[2 + q], block_at[4 + q], ALU.add).then_inc(pass2["sum"], 1)

            blocks(pool, share2)

            for q in range(2):
                pool.wait_ge(h_out[q], 16 * stored_all[q])

            def rel_get(j, q, u):
                pool.wait_ge(rel_in[q], 16 * (u + 1))
                after(pool, rel_sent[q], 16 * GS * u)
                alone()
                for k in range(GS):
                    idx = slot_in[:, q, k, :].bitcast(I32)
                    gather(slot_h[:, q, k, 0:D], h_t, idx[:, D + 1:D + 2], rel_got[q])
                    gather(slot_h[:, q, k, D:2 * D], h_t, idx[:, D:D + 1], rel_got[q])

            def rel_send(j, q, u):
                pool.wait_ge(rel["idx"], j + 1)
                pool.wait_ge(rel["att"], j + 1)
                alone()
                for k in range(GS):
                    scatter(edge_t, slot_idx[:, q, k:k + 1], slot_h[:, q, k, D:HW], EPAD, rel_sent[q])

            rel_get(0, 0, 0)
            rel_get(1, 1, 0)
            rel_send(0, 0, 0)
            with pool.Fori(1, NGS // 2) as i:
                rel_get(2 * i, 0, i)
                rel_send(2 * i - 1, 1, i - 1)
                rel_get(2 * i + 1, 1, i)
                rel_send(2 * i, 0, i)
            rel_send(NGS - 1, 1, NGS // 2 - 1)

            def send3(g, q, u):
                send_sums(e3, g, q, u, e3["norm"], lambda q, k: sbuf[:, q, k, :])

            send3(0, 0, 0)
            send3(1, 1, 0)
            with pool.Fori(1, GE // 2) as i:
                send3(2 * i, 0, i)
                send3(2 * i + 1, 1, i)
            fix(e3, fixout[:])

            def share3(b, q, u):
                pool.wait_ge(in3[q], 48 * (u + 1))
                after(pool, pass3["turned"], 8 * (b - 1))
                both = arena[:, (6 + 2 * q) * BW:(8 + 2 * q) * BW].rearrange("p (c f) -> p c f", f=P)
                pool.tensor_tensor(both[:, :, D:P], cols(block_at[q]), cols(block_at[2 + q]),
                                   ALU.mult).then_inc(pass3["prod"], 1)

            blocks(pool, share3)

        @block.vector
        def _(dve):
            v = nc.vector
            o = Order(dve, prep)
            o.did(v.memset(dsti[:], KEY_PAD))
            o.did(v.memset(srci[:], 0))
            o.did(v.memset(tmp_j[:], R))
            o.did(v.memset(ones[:], 1.0))
            o.did(v.memset(onesk[:], 1.0))
            o.did(v.memset(zero, 0.0))
            o.did(v.memset(res_in[:], 0.0))
            o.did(v.memset(rel_sb[:], 0.0))
            o.did(v.memset(pos[:], float(SLOT_SKIP)))
            o.did(v.memset(same[:], 0.0))
            o.did(v.memset(tile_rel[:], 0.0))
            o.wait()
            v.memset(tmp_b[:], 0.0).then_inc(filled, 1)
            dve.wait_ge(loaded, 16 * N_LOADS)
            dve.wait_ge(consts, 4)
            dve.wait_ge(filled, 1)
            o.did(v.tensor_copy(key[:], dsti[:]))
            o.did(v.tensor_copy(relf[:], tmp_j[:]))
            o.wait()
            for r in range(R):
                o.did(v.tensor_scalar(tmp_a[:, 0:KE], relf[:], float(r), None, ALU.is_equal, ALU.add,
                                      accum_out=cnt[:, 0, r:r + 1]))
                o.wait()
            at_step["counts"] = o.n
            dve.wait_ge(prep_pe, 1)
            totals, before = bank(0)[:, 0:R], bank(0)[:, R:2 * R]
            o.did(v.tensor_copy(cnti[:, 0, :], totals))
            o.wait()
            o.did(v.tensor_scalar(cnti[:, 1, :], cnti[:, 0, :], P - 1, None, ALU.add))
            o.wait()
            o.did(v.tensor_scalar(cnti[:, 0, :], cnti[:, 1, :], 7, None, ALU.logical_shift_right))
            o.wait()
            o.did(v.tensor_copy(cnt[:, 1, :], cnti[:, 0, :]))
            o.wait()
            o.did(v.tensor_tensor_scan(out=cnt[:, 2, :], data0=onesk[:, 0:R], data1=cnt[:, 1, :],
                                       initial=0.0, op0=ALU.mult, op1=ALU.add))
            o.wait()
            o.did(v.tensor_tensor(cnt[:, 3, :], cnt[:, 2, :], cnt[:, 1, :], ALU.subtract))
            o.wait()
            o.did(v.scalar_tensor_tensor(out=base[:], in0=cnt[:, 3, :], scalar=float(P), in1=before,
                                         op0=ALU.mult, op1=ALU.add))
            o.wait()
            o.did(v.tensor_scalar(cnt[:, 4, :], base[:], -1.0, None, ALU.add))
            o.wait()
            for r in range(R):
                o.did(v.tensor_scalar(tmp_i[:], relf[:], float(r), None, ALU.is_equal))
                o.wait()
                o.did(v.tensor_tensor_scan(out=tmp_a[:, 0:KE], data0=onesk[:], data1=tmp_i[:],
                                           initial=cnt[:, 4, r:r + 1], op0=ALU.mult, op1=ALU.add))
                o.wait()
                o.did(v.copy_predicated(pos[:], tmp_i[:], tmp_a[:, 0:KE]))
                o.wait()
            o.did(v.tensor_copy(tmp_i[:], pos[:]))
            o.wait()
            o.did(v.tensor_scalar(tmp_j[:], tmp_i[:], P - 1, None, ALU.bitwise_and))
            o.did(v.tensor_scalar(outi[:], tmp_i[:], 7, None, ALU.logical_shift_right))
            o.wait()
            o.did(v.scalar_tensor_tensor(out=slot_row[:], in0=tmp_j[:], scalar=float(KS), in1=outi[:],
                                         op0=ALU.mult, op1=ALU.add))
            o.did(v.tensor_copy(meta[:, :, 0], srci[:]))
            o.did(v.tensor_copy(meta[:, :, 1], dsti[:, 0:KE]))
            o.wait()
            v.tensor_copy(meta[:, :, 2], eidi[:]).then_inc(prep_ready, 1)
            dve.wait_ge(prep_ready, 1)
            o.did(v.tensor_tensor(same[:, 1:KE], key[:, 1:KE], key[:, 0:KE - 1], ALU.is_equal))
            o.did(v.tensor_scalar(head[:], key[:, 0:KE], key[:, 0:1], None, ALU.is_equal))
            o.did(v.tensor_tensor(tmp_a[:, 0:KE], key[:, 1:KE + 1], key[:, 0:KE], ALU.is_equal))
            o.wait()
            o.did(v.tensor_tensor(tmp_b[:, 0:KE], tmp_a[:, 0:KE], head[:], ALU.max))
            o.wait()
            o.did(v.scalar_tensor_tensor(out=outi[:], in0=tmp_b[:, 0:KE], scalar=float(SKIP), in1=key[:, 0:KE],
                                         op0=ALU.mult, op1=ALU.add))
            o.did(v.tensor_tensor(fix_f[:, 0:1], key[:, KE:KE + 1], key[:, 0:1], ALU.is_equal))
            o.did(v.tensor_scalar(diag[:], ident[:], key[:, 0:1], None, ALU.mult))
            at_step["first keys"] = o.n
            o.wait()
            o.did(v.scalar_tensor_tensor(out=fix_i[:], in0=fix_f[:, 0:1], scalar=float(SKIP), in1=key[:, 0:1],
                                         op0=ALU.mult, op1=ALU.add))
            dve.wait_ge(prep_pe, 2)
            o.did(v.tensor_copy(first_row[:], bank(1)[:, 0:P]))
            o.did(v.tensor_copy(res_sb[:], bank(1)[:, P:2 * P]))
            o.wait()
            o.did(v.scalar_tensor_tensor(out=carry[:], in0=first_row[:], scalar=key[:, KE - 1:KE], in1=upper[:],
                                         op0=ALU.is_equal, op1=ALU.mult))
            o.did(v.tensor_copy(tile_rel[0:1, 0, :], iota_i[0:1, 0:KS]))
            o.wait()
            for r in range(R - 1):
                o.did(v.scalar_tensor_tensor(out=tile_rel[0:1, 1, :], in0=tile_rel[0:1, 0, :],
                                             scalar=cnt[0:1, 2, r:r + 1], in1=tile_rel[0:1, 1, :],
                                             op0=ALU.is_ge, op1=ALU.add))
                o.wait()
            o.did(v.tensor_copy(tile_reli[:], tile_rel[0:1, 1, :]))
            o.did(v.tensor_scalar(tmp_i[:], dsti[:, 0:KE], 5, P - 1, ALU.logical_shift_right, ALU.bitwise_and))
            o.did(v.tensor_scalar(tmp_j[:], dsti[:, 0:KE], CB - 1, None, ALU.bitwise_and))
            o.did(v.tensor_copy(iota_h, iota_i))
            o.wait()
            o.did(v.tensor_copy(lo_key[:], tmp_i[:]))
            o.wait()
            o.did(v.tensor_scalar(tmp_i[:], dsti[:, 0:KE], 12, None, ALU.logical_shift_right))
            o.wait()
            o.did(v.scalar_tensor_tensor(out=hi_key[:], in0=tmp_i[:], scalar=float(CB), in1=tmp_j[:],
                                         op0=ALU.mult, op1=ALU.add))
            o.wait()

            def hot(t, k):
                after(dve, hot_used, t - 3)
                v.tensor_scalar(lo_hot[:, k % 4, :], iota_h[:, 0:P], lo_key[:, bass.ds(t, 1)], None,
                                ALU.is_equal).then_inc(hot_made, 1)
                v.tensor_scalar(hi_hot[:, k % 4, :], iota_h, hi_key[:, bass.ds(t, 1)], None,
                                ALU.is_equal).then_inc(hot_made, 1)

            for k in range(8):
                hot(k, k)
            with dve.Fori(1, KE // 8) as i:
                for k in range(8):
                    hot(8 * i + k, k)
            dve.wait_ge(hot_used, KE)
            v.tensor_scalar(degs[:, 0, :].rearrange("p (a c) -> p a c", a=2), banks[:, 0:2, 0:KN // 2], 1.0, None,
                            ALU.add).then_inc(deg_read, 1)
            dve.wait_ge(deg_root, 1)
            v.reciprocal(dinv[:], degs[:, 1, :]).then_inc(dinv_ready, 1)
            dve.wait_ge(dinv_ready, 1)

            def scale_of(b):
                return dinv[:, bass.ds(b * CB, CB)].unsqueeze(2).to_broadcast([P, CB, D])

            def spread(ap):
                return ap.unsqueeze(2).to_broadcast([P, CB, D])

            def centre(s, b, q, sums, xin, xc):
                v.tensor_reduce(stat[:, q, 0, :], cols(xin), AX.X, ALU.add).then_inc(s[sums], 1)
                dve.wait_ge(s[sums], b + 1)
                v.tensor_scalar(stat[:, q, 1, :], stat[:, q, 0, :], 1.0 / D, None, ALU.mult).then_inc(s["mean"], 1)
                dve.wait_ge(s["mean"], b + 1)
                v.tensor_tensor(cols(xc), cols(xin), spread(stat[:, q, 1, :]), ALU.subtract).then_inc(s["centered"], 1)

            def deviation(s, b, q, sq):
                dve.wait_ge(s["square"], b + 1)
                v.tensor_reduce(stat[:, q, 5, :], cols(sq), AX.X, ALU.add).then_inc(s["var"], 1)
                dve.wait_ge(s["var"], b + 1)
                v.tensor_scalar(stat[:, q, 2, :], stat[:, q, 5, :], 1.0 / D, EPS, ALU.mult, ALU.add).then_inc(s["vare"], 1)
                dve.wait_ge(s["std"], b + 1)
                v.reciprocal(stat[:, q, 4, :], stat[:, q, 3, :]).then_inc(s["rstd"], 1)
                dve.wait_ge(s["rstd"], b + 1)

            def centre0(b, q, u):
                last = isinstance(b, int) and b == NB - 1
                dve.wait_ge(x_in0[q], 16 * (u + 1) + (16 if last else 0))
                after(dve, pass0["g"], b - 1)
                centre(pass0, b, q, "sum", block_at[q], block_at[2 + q])

            def finish0(b, q, u):
                deviation(pass0, b, q, block_at[4 + q])
                v.tensor_tensor(stat[:, q, 5, :], stat[:, q, 4, :], dinv[:, bass.ds(b * CB, CB)],
                                ALU.mult).then_inc(pass0["coef"], 1)
                dve.wait_ge(pass0["coef"], b + 1)
                after(dve, g0_out[q], 16 * u)
                v.scalar_tensor_tensor(out=cols(block_at[6 + q]), in0=cols(block_at[2 + q]), scalar=0.0,
                                       in1=spread(stat[:, q, 5, :]), op0=ALU.max, op1=ALU.mult).then_inc(pass0["g"], 1)

            def staggered(first, second):
                def step(b, q, u):
                    first(b + 1, 1 - q, u + q)
                    second(b, q, u)
                first(0, 0, 0)
                step(0, 0, 0)
                step(1, 1, 0)
                with dve.Fori(1, NB // 2 - 1) as i:
                    step(2 * i, 0, i)
                    step(2 * i + 1, 1, i)
                step(NB - 3, 0, NB // 2 - 1)
                step(NB - 2, 1, NB // 2 - 1)
                second(NB - 1, 0, NB // 2)

            staggered(centre0, finish0)

            def sum_group(s, g, q, rows_of, width):
                for k in range(GT):
                    t = g * GT + k
                    former = rbuf[:, q, k - 1, 0:width] if k else rbuf[:, 1 - q, GT - 1, 0:width]
                    after(dve, s["run"], t)
                    v.scalar_tensor_tensor(out=rbuf[:, q, k, 0:width], in0=former, scalar=same[:, bass.ds(t, 1)],
                                           in1=rows_of(q, k), op0=ALU.mult, op1=ALU.add).then_inc(s["run"], 1)
                    after(dve, s["head"], t)
                    v.scalar_tensor_tensor(out=hsum[:, 0:width], in0=rows_of(q, k), scalar=head[:, bass.ds(t, 1)],
                                           in1=hsum[:, 0:width], op0=ALU.mult, op1=ALU.add).then_inc(s["head"], 1)

            def clear(s):
                v.memset(rbuf[:, 1, GT - 1, :], 0.0).then_inc(s["clear"], 1)
                v.memset(hsum[:], 0.0).then_inc(s["clear"], 1)
                dve.wait_ge(s["clear"], 2)

            def over_groups(eng, step):
                step(0, 0, 0)
                step(1, 1, 0)
                with eng.Fori(1, GE // 2) as i:
                    step(2 * i, 0, i)
                    step(2 * i + 1, 1, i)

            def edge_sums(s):
                clear(s)

                def step(g, q, u):
                    dve.wait_ge(s["got"][q], 16 * GT * (u + 1))
                    after(dve, s["sent"][q], 16 * GT * u)
                    sum_group(s, g, q, lambda q, k: gbuf[:, q, k, 0:D], D)

                over_groups(dve, step)
                dve.wait_ge(s["carry"], 1)
                dve.wait_ge(s["head"], KE)
                v.tensor_tensor(fixrow[:, 0:D], bank(0)[:, 0:D], hsum[:, 0:D], ALU.add).then_inc(s["fix"], 1)

            edge_sums(e1)

            def sum1(b, q, u):
                dve.wait_ge(agg_in1[q], 16 * (u + 1))
                dve.wait_ge(g_in1[q], 16 * (u + 1))
                v.tensor_tensor(block_at[q], block_at[q], block_at[2 + q], ALU.add).then_inc(pass1["sum"], 1)
                dve.wait_ge(pass1["sum"], b + 1)
                v.tensor_tensor(cols(block_at[q]), cols(block_at[q]), scale_of(b), ALU.mult).then_inc(pass1["a"], 1)

            def out1(b, q, u):
                after(dve, g1_out[q], 16 * u)
                for z in range(4):
                    n = 4 * b + z
                    dve.wait_ge(pass1["u"], n + 1)
                    v.tensor_tensor(cols(block_at[4 + q])[:, 8 * z:8 * z + 8, :],
                                    bank(6 + z % 2).rearrange("p (c f) -> p c f", f=D),
                                    dinv[:, bass.ds(b * CB + 8 * z, 8)].unsqueeze(2).to_broadcast([P, 8, D]),
                                    ALU.mult).then_inc(pass1["g"], 1)

            staggered(sum1, out1)
            edge_sums(e2)

            def centre2(b, q, u):
                dve.wait_ge(pass2["sum"], b + 1)
                after(dve, x1_out[q], 16 * u)
                v.tensor_tensor(cols(block_at[2 + q]), cols(block_at[2 + q]), scale_of(b), ALU.mult).then_inc(pass2["scaled"], 1)
                dve.wait_ge(pass2["scaled"], b + 1)
                v.tensor_tensor(block_at[8 + q], block_at[2 + q], block_at[q], ALU.add).then_inc(pass2["x1"], 1)
                dve.wait_ge(pass2["x1"], b + 1)
                centre(pass2, b, q, "rowsum", block_at[8 + q], block_at[4 + q])

            def finish2(b, q, u):
                deviation(pass2, b, q, block_at[2 + q])
                after(dve, h_out[q], 16 * u)
                v.scalar_tensor_tensor(out=cols(block_at[10 + q]), in0=cols(block_at[4 + q]), scalar=0.0,
                                       in1=spread(stat[:, q, 4, :]), op0=ALU.max, op1=ALU.mult).then_inc(pass2["h"], 1)

            staggered(centre2, finish2)

            def rel_index(j, q, u):
                dve.wait_ge(rel_in[q], 16 * (u + 1))
                after(dve, rel_sent[q], 16 * GS * u)
                number = slot_in.bitcast(I32)[:, q, :, D + 2]
                v.tensor_scalar(slot_e[:, q, 0, :], number, 0.0, float(ROW_SKIP), ALU.is_equal, ALU.mult).then_inc(rel["pad"], 1)
                dve.wait_ge(rel["pad"], j + 1)
                v.tensor_tensor(slot_idx[:, q, :], slot_e[:, q, 0, :], number, ALU.add).then_inc(rel["idx"], 1)

            def rel_work(j, q, u):
                rel_index(j, q, u)
                made = bank(2 + q).rearrange("p (k f) -> p k f", f=P)
                dve.wait_ge(rel["tr"], j + 1)
                dve.wait_ge(rel["idx"], j + 1)
                v.tensor_tensor(slot_z[:, q], made[:, :, 0:D], slot_in[:, q, :, 0:D], ALU.add).then_inc(rel["z"], 1)
                dve.wait_ge(rel["th"], j + 1)
                v.tensor_tensor(slot_q[:, q], slot_th[:, q], made[:, :, D:P], ALU.mult).then_inc(rel["q"], 1)
                dve.wait_ge(rel["q"], j + 1)
                v.tensor_reduce(slot_h[:, q, :, 2 * D], slot_q[:, q], AX.X, ALU.add).then_inc(rel["att"], 1)

            for j in range(2):
                rel_work(j, j, 0)
            with dve.Fori(1, NGS // 2) as i:
                rel_work(2 * i, 0, i)
                rel_work(2 * i + 1, 1, i)

            o = Order(dve, soft)
            dve.wait_ge(edges_in, 32)
            edge_rows = arena[:].rearrange("p (t w) -> p t w", w=MW)
            att, bwd, pen, mx = lo_key, hi_key, tmp_a, pos
            o.did(v.tensor_copy(att[:], edge_rows[:, :, D]))
            o.did(v.tensor_scalar(pen[:], same[:], -1.0, FAR, ALU.add, ALU.mult))
            o.wait()
            o.did(v.memset(edge_rows[:, :, D], 1.0))
            o.did(v.tensor_tensor_scan(out=tmp_b[:, 0:KE], data0=pen[:, 0:KE], data1=att[:], initial=-FAR,
                                       op0=ALU.add, op1=ALU.max))
            o.wait()
            o.did(v.tensor_tensor_scan(out=bwd[:][:, ::-1], data0=pen[:, 1:KE + 1][:, ::-1], data1=tmp_b[:, 0:KE][:, ::-1],
                                       initial=-FAR, op0=ALU.add, op1=ALU.max))
            o.wait()
            o.did(v.tensor_scalar(diag[:], ident[:], key[:, KE - 1:KE], None, ALU.mult))
            o.did(v.tensor_scalar(diag_max[:, 0, :], ident[:], tmp_b[:, KE - 1:KE], None, ALU.mult))
            o.did(v.tensor_scalar(diag_max[:, 1, :], ident[:], bwd[:, 0:1], None, ALU.mult))
            at_step["last segments"] = o.n
            dve.wait_ge(soft_pe, 1)
            lk, fm, hm = (bank(0)[:, k * P:(k + 1) * P] for k in range(3))
            both = seen
            for n, k in enumerate((0, KE - 1)):
                o.did(v.tensor_scalar(both[:, 0:P], lk, key[:, k:k + 1], -1.0, ALU.is_equal, ALU.add))
                o.did(v.tensor_scalar(both[:, P:2 * P], first_row[:], key[:, k:k + 1], -1.0, ALU.is_equal, ALU.add))
                o.wait()
                o.did(v.scalar_tensor_tensor(out=both[:, 0:2 * P], in0=both[:, 0:2 * P], scalar=FAR,
                                             in1=bank(0)[:, P:3 * P], op0=ALU.mult, op1=ALU.add))
                o.wait()
                o.did(v.tensor_reduce(smax[:, n:n + 1], both[:, 0:2 * P], AX.X, ALU.max))
                o.wait()
            for n, k in enumerate((0, KE - 1)):
                v.tensor_scalar(tmp_b[:, 0:KE], key[:, 0:KE], key[:, k:k + 1], -1.0, ALU.is_equal, ALU.add).then_inc(seg_max, 1)
                dve.wait_ge(seg_max, 3 * n + 1)
                v.tensor_scalar(tmp_b[:, 0:KE], tmp_b[:, 0:KE], FAR, smax[:, n:n + 1], ALU.mult, ALU.add).then_inc(seg_max, 1)
                dve.wait_ge(seg_max, 3 * n + 2)
                v.tensor_tensor(mx[:], tmp_b[:, 0:KE], bwd[:] if n == 0 else mx[:], ALU.max).then_inc(seg_max, 1)
                dve.wait_ge(seg_max, 3 * n + 3)
            o.did(v.tensor_tensor(tmp_b[:, 0:KE], att[:], mx[:], ALU.subtract))
            at_step["exponents"] = o.n
            dve.wait_ge(soft_exp, 1)

            clear(e3)

            def soft_group(g, q, u):
                after(dve, e3["head"], GT * g)
                v.tensor_tensor(gbuf[:, q], edge_rows[:, bass.ds(g * GT, GT), :],
                                tmp_a[:, bass.ds(g * GT, GT)].unsqueeze(2).to_broadcast([P, GT, MW]),
                                ALU.mult).then_inc(weighted, 1)
                dve.wait_ge(weighted, g + 1)
                sum_group(e3, g, q, lambda q, k: gbuf[:, q, k, :], MW)
                dve.wait_ge(e3["run"], GT * (g + 1))
                v.tensor_scalar(rden[:, q, 0, :], rbuf[:, q, :, D], 1e-30, None, ALU.max).then_inc(quotient, 1)
                dve.wait_ge(quotient, 2 * g + 1)
                v.reciprocal(rden[:, q, 1, :], rden[:, q, 0, :]).then_inc(quotient, 1)
                dve.wait_ge(quotient, 2 * g + 2)
                after(dve, e3["sent"][q], 16 * GT * u)
                v.tensor_tensor(sbuf[:, q], rbuf[:, q, :, 0:D], rden[:, q, 1, :].unsqueeze(2).to_broadcast([P, GT, D]),
                                ALU.mult).then_inc(e3["norm"], 1)

            over_groups(dve, soft_group)
            dve.wait_ge(e3["carry"], 1)
            dve.wait_ge(e3["head"], KE)
            o2 = Order(dve, e3["fixsteps"])
            o2.did(v.tensor_tensor(fixrow[:], bank(0)[:, 0:MW], hsum[:], ALU.add))
            o2.wait()
            o2.did(v.tensor_scalar(fixden[:, 0:1], fixrow[:, D:MW], 1e-30, None, ALU.max))
            o2.wait()
            o2.did(v.reciprocal(fixden[:, 1:2], fixden[:, 0:1]))
            o2.wait()
            v.tensor_scalar(fixout[:], fixrow[:, 0:D], fixden[:, 1:2], None, ALU.mult).then_inc(e3["fix"], 1)

            def sum3(b, q, u):
                dve.wait_ge(in3[q], 48 * (u + 1))
                after(dve, pass3["turned"], 8 * (b - 1))
                two = arena[:, (6 + 2 * q) * BW:(8 + 2 * q) * BW].rearrange("p (c f) -> p c f", f=P)
                v.tensor_tensor(two[:, :, 0:D], cols(block_at[q]), cols(block_at[2 + q]), ALU.add).then_inc(pass3["sum"], 1)

            def outblock3(b, q, u):
                after(dve, out3[q], 16 * u)
                for z in range(8):
                    n = 8 * b + z
                    dve.wait_ge(pass3["low"], n + 1)
                    v.tensor_tensor(leaky3[:, z % 2, :], bank(2 + z % 2), low3[:, z % 2, :], ALU.max).then_inc(pass3["leaky"], 1)
                    dve.wait_ge(pass3["leaky"], n + 1)
                    y = leaky3[:, z % 2, :].rearrange("p (c f) -> p c f", f=P)
                    v.tensor_tensor(halves3[:, z % 2], y[:, :, 0:D], y[:, :, D:P], ALU.add).then_inc(pass3["res"], 1)
                    dve.wait_ge(pass3["res"], n + 1)
                    v.tensor_tensor(cols(block_at[10 + q])[:, 4 * z:4 * z + 4, :], halves3[:, z % 2],
                                    cols(block_at[4 + q])[:, 4 * z:4 * z + 4, :], ALU.add).then_inc(pass3["out"], 1)

            staggered(sum3, outblock3)

        @block.scalar
        def _(act):
            act.wait_ge(deg_read, 1)
            nc.scalar.activation(degs[:, 1, :], degs[:, 0, :], ACT.Sqrt).then_inc(deg_root, 1)

            def norm_part(s, xc, sq):
                def square(b, q):
                    act.wait_ge(s["centered"], b + 1)
                    after(act, s["var"], b - 1)
                    nc.scalar.activation(sq(q), xc(q), ACT.Square).then_inc(s["square"], 1)

                def root(b, q):
                    act.wait_ge(s["vare"], b + 1)
                    after(act, s["rstd"], b - 1)
                    nc.scalar.activation(stat[:, q, 3, :], stat[:, q, 2, :], ACT.Sqrt).then_inc(s["std"], 1)

                square(0, 0)
                square(1, 1)
                root(0, 0)
                with act.Fori(1, NB // 2) as i:
                    square(2 * i, 0)
                    root(2 * i - 1, 1)
                    square(2 * i + 1, 1)
                    root(2 * i, 0)
                square(NB - 1, 0)
                root(NB - 2, 1)
                root(NB - 1, 0)

            norm_part(pass0, lambda q: block_at[2 + q], lambda q: block_at[4 + q])

            def indices(s, sources):
                def src_part(g, q, u):
                    after(act, s["got"][q], 16 * GT * u)
                    nc.scalar.copy(src_idx[:, q, :], srci[:, bass.ds(g * GT, GT)]).then_inc(s["src_idx"][q], 1)

                def out_part(g, q, u):
                    after(act, s["sent"][q], 16 * GT * u)
                    nc.scalar.copy(out_idx[:, q, :], outi[:, bass.ds(g * GT, GT)]).then_inc(s["out_idx"][q], 1)

                if not sources:
                    out_part(0, 0, 0)
                    out_part(1, 1, 0)
                    with act.Fori(1, GE // 2) as i:
                        out_part(2 * i, 0, i)
                        out_part(2 * i + 1, 1, i)
                    return
                src_part(0, 0, 0)
                src_part(1, 1, 0)
                out_part(0, 0, 0)
                src_part(2, 0, 1)
                out_part(1, 1, 0)
                src_part(3, 1, 1)
                with act.Fori(1, GE // 2 - 1) as i:
                    out_part(2 * i, 0, i)
                    src_part(2 * i + 2, 0, i + 1)
                    out_part(2 * i + 1, 1, i)
                    src_part(2 * i + 3, 1, i + 1)
                out_part(GE - 2, 0, GE // 2 - 1)
                out_part(GE - 1, 1, GE // 2 - 1)

            for q in range(2):
                act.wait_ge(perm_sent[q], PERM_DONE)
            indices(e1, True)

            def turn1(n, z):
                q = z % 2
                act.wait_ge(pass1["turned"], n + 1)
                after(act, pass1["h"], n - 1)
                nc.scalar.copy(arena[:, 6 * BW + q * MM:6 * BW + (q + 1) * MM], bank(q)).then_inc(pass1["at"], 1)

            def relu1(n, z):
                q = z % 2
                act.wait_ge(pass1["h"], n + 1)
                after(act, pass1["u"], n - 1)
                nc.scalar.activation(arena[:, 7 * BW + q * 2 * MM:7 * BW + (q + 1) * 2 * MM], bank(2 + 2 * q, 2),
                                     ACT.Relu, bias=b1_sb[:, 0:1]).then_inc(pass1["relu"], 1)

            def step1(b, q, u):
                for z in range(4):
                    n = 4 * b + z
                    if not (isinstance(n, int) and n == 4 * NB - 1):
                        turn1(n + 1, z + 1)
                    relu1(n, z)

            turn1(0, 0)
            blocks(act, step1)
            indices(e2, True)
            norm_part(pass2, lambda q: block_at[4 + q], lambda q: block_at[2 + q])

            def rel_turn(j, q):
                act.wait_ge(rel["turned"], j + 1)
                after(act, rel["tr"], j - 1)
                nc.scalar.copy(slot_ht[:, q], bank(q).rearrange("p (k s) -> p k s", s=P)).then_inc(rel["ht"], 1)

            def rel_tanh(j, q):
                act.wait_ge(rel["z"], j + 1)
                after(act, rel["q"], j - 1)
                nc.scalar.activation(slot_th[:, q], slot_z[:, q], ACT.Tanh).then_inc(rel["th"], 1)

            for j in range(2):
                rel_turn(j, j)
                rel_tanh(j, j)
            with act.Fori(1, NGS // 2) as i:
                for q in range(2):
                    rel_turn(2 * i + q, q)
                    rel_tanh(2 * i + q, q)

            act.wait_ge(soft, at_step["exponents"])
            nc.scalar.activation(tmp_a[:, 0:KE], tmp_b[:, 0:KE], ACT.Exp).then_inc(soft_exp, 1)
            indices(e3, False)

            def turn3(n, z):
                q = z % 2
                act.wait_ge(pass3["turned"], n + 1)
                after(act, pass3["o"], n - 1)
                nc.scalar.copy(turned3[:, q, :], bank(q)).then_inc(pass3["t"], 1)

            def lower3(n, z):
                q = z % 2
                act.wait_ge(pass3["o"], n + 1)
                after(act, pass3["leaky"], n - 1)
                nc.scalar.mul(low3[:, q, :], bank(2 + q), 0.01).then_inc(pass3["low"], 1)

            def step3(b, q, u):
                for z in range(8):
                    n = 8 * b + z
                    if not (isinstance(n, int) and n == 8 * NB - 1):
                        turn3(n + 1, z + 1)
                    lower3(n, z)

            turn3(0, 0)
            blocks(act, step3)

        @block.tensor
        def _(pe):
            pe.wait_ge(consts, 4)
            pe.wait_ge(prep, at_step["counts"])
            nc.tensor.matmul(bank(0)[:, 0:R], ones[:], cnt[:, 0, :], start=True, stop=True)
            nc.tensor.matmul(bank(0)[:, R:2 * R], upper[:], cnt[:, 0, :], start=True, stop=True).then_inc(prep_pe, 1)
            pe.wait_ge(prep, at_step["first keys"])
            nc.tensor.matmul(bank(1)[:, 0:P], ones[:], diag[:], start=True, stop=True)
            nc.tensor.transpose(bank(1)[:, P:2 * P], res_in[:], ident[:]).then_inc(prep_pe, 1)

            def count(t, k):
                pe.wait_ge(hot_made, 2 * (t + 1))
                first, last = isinstance(t, int) and t == 0, isinstance(t, int) and t == KE - 1
                nc.tensor.matmul(banks[:, 0, 0:KN // 2], lo_hot[:, k % 4, :], hi_hot[:, k % 4, 0:KN // 2],
                                 start=first, stop=last, skip_group_check=True)
                nc.tensor.matmul(banks[:, 1, 0:KN // 2], lo_hot[:, k % 4, :], hi_hot[:, k % 4, KN // 2:KN],
                                 start=first, stop=last, skip_group_check=True).then_inc(hot_used, 1)

            for k in range(8):
                count(k, k)
            with pe.Fori(1, KE // 8 - 1) as i:
                for k in range(8):
                    count(8 * i + k, k)
            for k in range(8):
                count(KE - 8 + k, k)

            def carried(s, width):
                pe.wait_ge(s["run"], KE)
                nc.tensor.matmul(bank(0)[:, 0:width], carry[:], rbuf[:, 1, GT - 1, 0:width],
                                 start=True, stop=True).then_inc(s["carry"], 1)

            carried(e1, D)

            def turn1(n, z):
                b, zz = (n // 4, n % 4) if isinstance(n, int) else n
                at = 4 * b + zz
                pe.wait_ge(pass1["a"], b + 1)
                after(pe, pass1["at"], at - 1)
                for k in range(4):
                    c = (8 * zz + 2 * k) * D
                    ins = nc.tensor.transpose(bank(zz % 2)[:, k * P:(k + 1) * P], block_at[z][:, c:c + P], ident[:])
                ins.then_inc(pass1["turned"], 1)

            def hidden1(n, q):
                pe.wait_ge(pass1["at"], n + 1)
                after(pe, pass1["relu"], n - 1)
                at = arena[:, 6 * BW + q * MM:6 * BW + (q + 1) * MM]
                nc.tensor.matmul(bank(2 + 2 * q), w1_sb[0:D, :], at[0:D, :], start=True, stop=True)
                nc.tensor.matmul(bank(3 + 2 * q), w1_sb[D:P, :], at[D:P, :], start=True, stop=True).then_inc(pass1["h"], 1)

            def output1(n, q):
                pe.wait_ge(pass1["relu"], n + 1)
                after(pe, pass1["g"], n - 1)
                hs = arena[:, 7 * BW + q * 2 * MM:7 * BW + (q + 1) * 2 * MM]
                for k in range(8):
                    pair, half = k // 2, k % 2
                    ins = nc.tensor.matmul(bank(6 + q)[:, k * D:(k + 1) * D],
                                           hs[:, half * MM + pair * P:half * MM + (pair + 1) * P], w2_sb[:],
                                           start=True, stop=True)
                ins.then_inc(pass1["u"], 1)

            def step1(b, q, u):
                final = isinstance(b, int) and b == NB - 1
                for z in range(4):
                    n = 4 * b + z
                    if z < 3:
                        turn1((b, z + 1), q)
                    elif not final:
                        turn1((b + 1, 0), 1 - q)
                    hidden1(n, z % 2)
                    if not (isinstance(n, int) and n == 0):
                        output1(n - 1, 1 - z % 2)

            turn1((0, 0), 0)
            blocks(pe, step1)
            output1(4 * NB - 1, 1)
            carried(e2, D)

            def rel_turn(j, q, u):
                pe.wait_ge(rel_got[q], 16 * 2 * GS * (u + 1))
                after(pe, rel["ht"], j - 1)
                for k in range(GS):
                    ins = nc.tensor.transpose(bank(q)[:, k * P:(k + 1) * P], slot_h[:, q, k, 0:P], ident[:])
                ins.then_inc(rel["turned"], 1)

            def rel_project(j, q, u):
                pe.wait_ge(rel["ht"], j + 1)
                after(pe, rel["q"], j - 1)
                flat = rel_sb[:].rearrange("p r f -> p (r f)")
                for k in range(GS):
                    r = pe.value_load(tile_reli[0:1, bass.ds(j * GS + k, 1)], min_val=0, max_val=R - 1)
                    ins = nc.tensor.matmul(bank(2 + q)[:, k * P:(k + 1) * P], slot_ht[:, q, k, :],
                                           flat[:, bass.ds(r * P, P)], start=True, stop=True)
                ins.then_inc(rel["tr"], 1)

            for j in range(2):
                rel_turn(j, j, 0)
                rel_project(j, j, 0)
            with pe.Fori(1, NGS // 2) as i:
                for q in range(2):
                    rel_turn(2 * i + q, q, i)
                    rel_project(2 * i + q, q, i)

            pe.wait_ge(soft, at_step["last segments"])
            for k, d in enumerate((diag[:], diag_max[:, 0, :], diag_max[:, 1, :])):
                ins = nc.tensor.matmul(bank(0)[:, k * P:(k + 1) * P], ones[:], d, start=True, stop=True)
            ins.then_inc(soft_pe, 1)
            carried(e3, MW)

            def turn3(b, zz, q):
                at = 8 * b + zz
                pe.wait_ge(pass3["sum"], b + 1)
                pe.wait_ge(pass3["prod"], b + 1)
                after(pe, pass3["t"], at - 1)
                two = arena[:, (6 + 2 * q) * BW:(8 + 2 * q) * BW]
                for k in range(4):
                    c = (4 * zz + k) * P
                    ins = nc.tensor.transpose(bank(zz % 2)[:, k * P:(k + 1) * P], two[:, c:c + P], ident[:])
                ins.then_inc(pass3["turned"], 1)

            def res3(n, q):
                pe.wait_ge(pass3["t"], n + 1)
                after(pe, pass3["leaky"], n - 1)
                for k in range(4):
                    ins = nc.tensor.matmul(bank(2 + q)[:, k * P:(k + 1) * P], turned3[:, q, :][:, k * P:(k + 1) * P], res_sb[:],
                                           start=True, stop=True)
                ins.then_inc(pass3["o"], 1)

            def step3(b, q, u):
                final = isinstance(b, int) and b == NB - 1
                for z in range(8):
                    if z < 7:
                        turn3(b, z + 1, q)
                    elif not final:
                        turn3(b + 1, 0, 1 - q)
                    res3(8 * b + z, z % 2)

            turn3(0, 0, 0)
            blocks(pe, step3)


_INS = ["x", "src", "dst", "edge_attr_64", "edge_type_32", "L0_gnn_W1", "L0_gnn_b1", "L0_gnn_W2", "L0_gnn_b2",
        "L1_gnn_relation_weight", "L1_gnn_res_w1", "L1_gnn_res_w2"]


def kernel(**inputs):
    import numpy as _np
    import concourse.bacc as _bacc
    from concourse import mybir as _mybir
    from concourse.bass_utils import run_bass_kernel_spmd as _run

    nc = _bacc.Bacc("TRN2", target_bir_lowering=False, num_devices=1)
    arrays, args = {}, []
    for name in _INS:
        a = _np.ascontiguousarray(inputs[name])
        arrays[f"in_{name}"] = a
        args.append(nc.dram_tensor(f"in_{name}", a.shape, _mybir.dt.from_np(a.dtype), kind="ExternalInput").ap())
    args.append(nc.dram_tensor("result", (N, D), F32, kind="ExternalOutput").ap())
    build(nc, *args)
    return _run(nc, [arrays], core_ids=[0]).results[0]["result"]
```

```python
from contextlib import ExitStack

import concourse.bass as bass
from concourse import mybir

ALU = mybir.AluOpType
ACT = mybir.ActivationFunctionType
AX = mybir.AxisListType
F32 = mybir.dt.float32
F16 = mybir.dt.float16
I32 = mybir.dt.int32

P = 128
N = 100000
E = 50000
D = 64
HID = 128
R = 32
EPS = 1e-5

CB = 32
BROWS = P * CB
NB = -(-N // BROWS)
NPAD = NB * BROWS
KN = NB * CB
BW = CB * D
TAIL_P = (N - (NB - 1) * BROWS) // CB
TAIL_SPLIT = TAIL_P // 16 * 16

KE = 392
EFULL = E // KE
ETAIL = E - EFULL * KE
GT = 14
GE = KE // GT
EPAD = P * KE
ESPLIT = 112

KS = 424
GS = 4
NGS = KS // GS
SB = 4
RW = 2 * D + 2
MW = D + 1
WW = RW + MW

KEY_PAD = 1 << 20
SKIP = 1 << 20
SLOT_SKIP = 1 << 23
ROW_SKIP = 1 << 21
FAR = 1e30
TINY = 1e-30
MM = 512
GW = GT * D


def after(eng, sem, value):
    if isinstance(value, int) and value <= 0:
        return
    eng.wait_ge(sem, value)


def known(value, at_least, below):
    return not isinstance(value, int) or at_least <= value < below


class Order:

    def __init__(self, eng, sem):
        self.eng, self.sem, self.n = eng, sem, 0

    def did(self, ins):
        ins.then_inc(self.sem, 1)
        self.n += 1

    def wait(self):
        self.eng.wait_ge(self.sem, self.n)

    def do(self, ins):
        self.did(ins)
        self.wait()


def build(nc, x, src, dst, eattr, etype, w1, b1, w2, b2, relw, rw1, rw2, out):
    with ExitStack() as ctx:
        def sb(name, shape, dt=F32):
            return ctx.enter_context(nc.sbuf_tensor(name, shape, dt))

        def sem(name):
            return ctx.enter_context(nc.semaphore(name))

        def sem2(name):
            return [sem(name + "_even"), sem(name + "_odd")]

        def sems(prefix, names):
            return {k: sem(f"{prefix}_{k}") for k in names.split()}

        g0_t = nc.dram_tensor("g0_by_node", (NPAD, D), F32).ap()
        g1_t = nc.dram_tensor("g1_by_node", (NPAD, D), F32).ap()
        x1_t = nc.dram_tensor("x1_by_node", (NPAD, D), F32).ap()
        h_t = nc.dram_tensor("h_by_node", (NPAD, D), F32).ap()
        xd_t = nc.dram_tensor("x_of_destination", (EPAD, D), F32).ap()
        g1d_t = nc.dram_tensor("g1_of_destination", (EPAD, D), F32).ap()
        x1d_t = nc.dram_tensor("x1_of_destination", (EPAD, D), F32).ap()
        hd_t = nc.dram_tensor("h_of_destination", (EPAD, D), F32).ap()
        slot_t = nc.dram_tensor("slot_rows", (P * KS, RW), F32).ap()
        edge_t = nc.dram_tensor("edge_rows", (1 + EPAD, MW), F32).ap()

        ident = sb("ident", [P, P])
        upper = sb("upper", [P, P])
        ones = sb("ones", [P, P])
        diag = sb("diag", [P, P])
        first_row = sb("first_row", [P, P])
        carry = sb("carry", [P, P])
        dsti = sb("dsti", [P, KE + 1], I32)
        dsafe = sb("dsafe", [P, KE], I32)
        meta = sb("meta", [P, KE, 2], I32)
        relf = sb("relf", [P, KE])
        key = sb("key", [P, KE + 1])
        same = sb("same", [P, KE + 1])
        head = sb("head", [P, KE])
        outi = sb("outi", [P, KE], I32)
        slot_row = sb("slot_row", [P, KE], I32)
        dinv_e = sb("dinv_e", [P, KE])
        dinv2_e = sb("dinv2_e", [P, KE])
        tmp_a = sb("tmp_a", [P, KE + 1])
        tmp_b = sb("tmp_b", [P, KE + 1])
        tmp_i = sb("tmp_i", [P, KE], I32)
        tmp_j = sb("tmp_j", [P, KE], I32)
        lo_key = sb("lo_key", [P, KE])
        hi_key = sb("hi_key", [P, KE])
        pos = sb("pos", [P, KE])
        onesk = sb("onesk", [P, KE])
        cnt = sb("cnt", [P, 6, R])
        cnti = sb("cnti", [P, 2, R], I32)
        rel_no = sb("rel_no", [P, R])
        tile_no = sb("tile_no", [1, KS])
        tile_reli = sb("tile_reli", [1, KS], I32)
        w1_sb = sb("w1_sb", [P, HID])
        w2_sb = sb("w2_sb", [P, D])
        b1_sb = sb("b1_sb", [P, 1])
        b2_sb = sb("b2_sb", [P, D])
        res_in = sb("res_in", [P, P])
        res_sb = sb("res_sb", [P, P])
        res1_sb = sb("res1_sb", [P, P])
        stat = sb("stat", [P, 2, 6, CB])
        estat = sb("estat", [P, 6, GT])
        rden = sb("rden", [P, 2, GT])
        smax = sb("smax", [P, 2])
        src_idx = sb("src_idx", [P, 2, GT], I32)
        out_idx = sb("out_idx", [P, 2, GT], I32)
        slot_idx = sb("slot_idx", [P, SB, GS], I32)
        slot_e = sb("slot_e", [P, SB, GS])
        fix_i = sb("fix_i", [P, 1], I32)
        fix_s = sb("fix_s", [P, 12])
        hd_i = sb("hd_i", [P, 1], I32)
        last_i = sb("last_i", [P, 1], I32)
        hsum = sb("hsum", [P, MW])
        fix_sum = sb("fix_sum", [P, MW])
        fix_x = sb("fix_x", [P, D])
        fix_c = sb("fix_c", [P, D])
        fix_q = sb("fix_q", [P, D])
        fix_g1 = sb("fix_g1", [P, D])
        fix_x1 = sb("fix_x1", [P, D])
        fix_h = sb("fix_h", [P, D])
        fix_two = sb("fix_two", [P, P])
        fix_t = sb("fix_t", [P, P])
        fix_hid = sb("fix_hid", [P, P])
        fix_low = sb("fix_low", [P, P])
        fix_out = sb("fix_out", [P, D])
        h_last = sb("h_last", [P, D])
        gbuf = sb("gbuf", [P, 2 * GT * MW])
        rbuf = sb("rbuf", [P, 2 * GT * MW])
        ebuf = sb("ebuf", [P, 9 * GW])
        chain = sb("chain", [P, 6 * MM])
        halves = sb("halves", [P, 2, 4, D])
        arena = sb("arena", [P, KE * MW])
        banks = ctx.enter_context(nc.psum_tensor("banks", [P, 8, MM], F32))

        def part(buffer, at, shape, dt=F32):
            n = 1
            for k in shape:
                n *= k
            words = buffer[:, at:at + (n + 1) // 2] if dt == F16 else buffer[:, at:at + n]
            words = words if dt == F32 else words.bitcast(dt)
            if len(shape) == 1:
                return words
            if len(shape) == 2:
                return words.rearrange("p (a b) -> p a b", b=shape[1])
            return words.rearrange("p (a b c) -> p a b c", b=shape[1], c=shape[2])

        iota_h = part(arena, 8 * BW, [KN], F16)
        lo_hot = part(arena, 8 * BW + KN // 2, [4, P], F16)
        hi_hot = part(arena, 8 * BW + KN // 2 + 2 * P, [4, KN], F16)
        degs = part(arena, 8 * BW + KN // 2 + 2 * P + 2 * KN, [2, KN])
        ZW = KS * RW // 16
        zero = part(arena, 10 * BW, [ZW])
        iota_i = part(arena, 10 * BW + ZW, [KN], I32)
        eidi = part(arena, 10 * BW + ZW + KN, [KE], I32)
        rows_e = part(rbuf, 0, [2, GT, MW])
        rows_g = part(gbuf, 0, [2, GT, MW])
        perm_rows = part(arena, 0, [2, GT, RW])
        slot_w = part(arena, 2 * GT * RW, [SB, GS, WW])
        srci = part(ebuf, 3 * GW, [KE], I32)
        dinv = part(ebuf, 2 * GW, [KN])
        rel_sb = part(arena, 2 * GT * RW + SB * GS * WW, [R, P])
        tile_rel = part(ebuf, 3 * GW, [2, KS])
        slot_ht = part(ebuf, 0, [2, GS, P])
        slot_z = part(ebuf, 2 * GS * P, [2, GS, D])
        slot_th = part(ebuf, 3 * GS * P, [2, GS, D])
        slot_q = part(ebuf, 4 * GS * P, [2, GS, D])
        diag_max = part(chain, 0, [2, P])
        seen = part(chain, 2 * P, [2 * P])

        def slot(k):
            return arena[:, k * BW:(k + 1) * BW]

        def eslot(k, n=1):
            return ebuf[:, k * GW:(k + n) * GW]

        def cols(ap):
            return ap.rearrange("p (c f) -> p c f", f=D)

        def bank(k, n=1):
            return banks[:, k:k + n, :].rearrange("p a b -> p (a b)")

        def wide(ap, c, f=D):
            return ap.unsqueeze(2).to_broadcast([P, c, f])

        def b2_over(c):
            return b2_sb[:].unsqueeze(1).to_broadcast([P, c, D])

        filled, loaded, consts = sem("filled"), sem("inputs_loaded"), sem("pool_constants")
        prep, prep_pe, prep_act = sem("prep_steps"), sem("prep_products"), sem("prep_roots")
        zeroed, cleared = sem("zeros_stored"), sem("sums_cleared")
        waits_over = {e: sem("waits_over_" + e) for e in ("pool", "sp", "dve")}
        x_idx, x_got, x_kept = sem("xd_idx"), sem2("xd_here"), sem2("xd_stored")
        hot_made, hot_used, deg_read = sem("one_hots_made"), sem("one_hots_used"), sem("degree_read")
        deg_root, out_idx_ready = sem("degree_root"), sem("out_idx_ready")
        A = sems("a", "rows centered square std g turned at h relu u g1 xu x1")
        a_in, a_g0, a_g1, a_x1 = sem2("a_x_loaded"), sem2("a_g0_stored"), sem2("a_g1_stored"), sem2("a_x1_stored")
        B = sems("b", "rows centered square std h turned t o low leaky out")
        b_in, b_h, b_out = sem2("b_x1_loaded"), sem2("b_h_stored"), sem2("b_out_stored")
        e1 = sems("e1", "rows centered square std run head a turned at h relu u g1")
        e1_src = sem("e1_src_idx")
        e1_x, e1_got, e1_sent, e1_kept = (sem2("e1_" + k) for k in ("xd_loaded", "rows_here", "rows_sent", "g1d_stored"))
        e2 = sems("e2", "run head rows centered square std h")
        e2_src = sem("e2_src_idx")
        e2_in, e2_got, e2_sent, e2_kept = (sem2("e2_" + k) for k in ("loaded", "rows_here", "rows_sent", "stored"))
        sort = sem("sort_steps")
        rel_cleared, rel_weights = sem("relation_weights_cleared"), sem("relation_weights_loaded")
        c_last = sem("last_rows_here")
        c = sems("perm", "tmp hf")
        c_meta = sem("perm_meta")
        c_ef, c_hd, c_sent = (sem2("perm_" + k) for k in ("features", "hd_loaded", "sent"))
        rel = sems("rel", "idx turned ht tr z th q att")
        rel_in, rel_got, rel_sent = ([sem(f"rel_{k}_{n}") for n in range(SB)] for k in ("loaded", "rows_here", "sent"))
        edges_in, soft, soft_pe, soft_exp = sem("edges_loaded"), sem("softmax_steps"), sem("softmax_rows"), sem("weights_ready")
        f = sems("f", "weighted run head rows two turned t o low leaky half out")
        f_in, f_sent = sem2("f_loaded"), sem2("f_sent")
        fix_in = sem("fix_loaded")
        fix = sems("fix", "ve act pe sent")
        for s, steps, first in ((A, 6, 0), (B, 5, 0), (e1, 8, 0), (e2, 9, 4)):
            s["steps"], s["first"] = steps, first
        at_step = {}
        ALL = 16 * GT * (GE // 2)
        STORES = [16 * (NB // 2 + 1), 16 * (NB // 2)]
        FIX_1_STEPS = 13
        N_LOADS = 9 + 3 + 9

        block = ctx.enter_context(nc.Block())

        def row_steps(s, n, k):
            return s["steps"] * n + s["first"] + k

        def over_groups(eng, step):
            step(0, 0, 0)
            step(1, 1, 0)
            with eng.Fori(1, GE // 2) as i:
                step(2 * i, 0, i)
                step(2 * i + 1, 1, i)

        def over_blocks(eng, step):
            step(0, 0, 0)
            step(1, 1, 0)
            with eng.Fori(1, NB // 2) as i:
                step(2 * i, 0, i)
                step(2 * i + 1, 1, i)
            step(NB - 1, 0, NB // 2)
            step(NB, 1, NB // 2)

        def over_both(eng, step):
            step(0, 0, 0)
            step(1, 1, 0)
            with eng.Fori(1, NB // 2) as i:
                step(2 * i, 0, i)
                step(2 * i + 1, 1, i)
            for g in range(NB - 1, GE + 1):
                step(g, g % 2, g // 2)

        def over_slots(step, eng):
            for j in range(SB):
                step(j, j, j % 2, 0)
            with eng.Fori(1, NGS // SB) as i:
                for s in range(SB):
                    step(SB * i + s, s, s % 2, i)
            for j in range(NGS // SB * SB, NGS):
                step(j, j % SB, j % 2, j // SB)

        def over_perm(eng, step):
            whole = ETAIL // GT
            s0 = GE - 1 - whole
            assert s0 % 2 == 0
            step(0, 0, 0, "none")
            step(1, 1, 0, "none")
            with eng.Fori(1, s0 // 2) as i:
                step(2 * i, 0, i, "none")
                step(2 * i + 1, 1, i, "none")
            step(s0, 0, s0 // 2, "part")
            step(s0 + 1, 1, s0 // 2, "whole")
            with eng.Fori(s0 // 2 + 1, GE // 2) as i:
                step(2 * i, 0, i, "whole")
                step(2 * i + 1, 1, i, "whole")

        def features_in(u, kind):
            u0 = (GE - 1 - ETAIL // GT) // 2
            return 32 * (u + 1) if kind == "none" else 32 * u0 + 48 * (u + 1 - u0)

        def group(table, g):
            return table.rearrange("(p t) f -> p (t f)", p=P)[:, bass.ds(g * GW, GW)]

        def rows(table, b, parts=P, first=0):
            if isinstance(b, int):
                at = b * BROWS + first * CB
                return table[at:at + parts * CB, :].rearrange("(p c) f -> p (c f)", c=CB)
            return table[bass.ds(b * BROWS, BROWS), :].rearrange("(p c) f -> p (c f)", c=CB)

        def move_block(eng, dram, here, b, signal, store):
            parts = [(0, P)]
            if isinstance(b, int) and b == NB - 1 and dram.shape[0] == N:
                parts = [(0, TAIL_SPLIT), (TAIL_SPLIT, TAIL_P)]
            for lo, hi in parts:
                there, mine = rows(dram, b, hi - lo, lo), here[lo:hi, :]
                eng.dma_start(there if store else mine, mine if store else there).then_inc(signal, 16)

        def all_landed(eng, signals, counts):
            for q in range(2):
                eng.wait_ge(signals[q], counts[q] if isinstance(counts, list) else counts)

        @block.sync
        def _(sp):
            count = [0]

            def load(to, of):
                sp.dma_start(to, of).then_inc(loaded, 16)
                count[0] += 1

            def load_edges(tile, vec):
                full = vec[0:EFULL * KE].rearrange("(p t) -> p t", t=KE)
                load(tile[0:ESPLIT, 0:KE], full[0:ESPLIT, :])
                load(tile[ESPLIT:EFULL, 0:KE], full[ESPLIT:EFULL, :])
                load(tile[EFULL:P, 0:ETAIL], vec[EFULL * KE:E].unsqueeze(0))

            sp.wait_ge(filled, 1)
            load_edges(dsti, dst)
            load_edges(tmp_j, etype)
            load_edges(srci, src)
            ctx.enter_context(nc.allow_non_contiguous_dma(reason="one number in each partition"))
            later = dst[KE:EFULL * KE].rearrange("(p t) -> p t", t=KE)
            load(dsti[0:ESPLIT, KE:KE + 1], later[0:ESPLIT, 0:1])
            load(dsti[ESPLIT:EFULL - 1, KE:KE + 1], later[ESPLIT:EFULL - 1, 0:1])
            load(dsti[EFULL - 1:EFULL, KE:KE + 1], dst[EFULL * KE:EFULL * KE + 1].unsqueeze(0))
            load(w1_sb[0:D, :], w1)
            load(w1_sb[D:P, :], w1)
            load(w2_sb[:], w2)
            load(b1_sb[:], b1.unsqueeze(1))
            load(b2_sb[:], b2.partition_broadcast(P))
            load(res_in[0:D, 0:D], rw1)
            load(res_in[D:P, D:P], rw2)
            load(fix_two[0:D, 0:D], rw1)
            load(fix_two[D:P, D:P], rw1)
            assert count[0] == N_LOADS, count[0]
            lanes = slot_t.rearrange("(l s) w -> l (s w)", l=P)
            for k in range(16):
                sp.dma_start(lanes[:, k * ZW:(k + 1) * ZW], zero).then_inc(zeroed, 16)
            pads = edge_t[E + 1:EPAD + 1, :].rearrange("(l s) w -> l (s w)", s=2)
            sp.dma_start(pads, zero[0:(EPAD - E) // 2, 0:2 * MW]).then_inc(zeroed, 16)
            sp.wait_ge(zeroed, 16 * 17)

            def load_a(b, q):
                after(sp, A["x1"], 2 * (b - 1))
                move_block(sp, x, slot(q), b, a_in[q], store=False)

            def step_a(b, q, u):
                if known(b, 0, NB - 1):
                    load_a(b + 1, 1 - q)
                if known(b, 0, NB):
                    sp.wait_ge(A["g"], b + 1)
                    move_block(sp, g0_t, slot(6 + q), b, a_g0[q], store=True)
                if known(b, 1, NB + 1):
                    sp.wait_ge(A["g1"], 4 * b)
                    move_block(sp, g1_t, slot(9 - q), b - 1, a_g1[1 - q], store=True)
                    sp.wait_ge(A["x1"], 2 * b)
                    move_block(sp, x1_t, slot(11 - q), b - 1, a_x1[1 - q], store=True)

            def over_a():
                step_a(0, 0, 0)
                step_a(1, 1, 0)
                with sp.Fori(1, NB // 2 - 1) as i:
                    step_a(2 * i, 0, i)
                    step_a(2 * i + 1, 1, i)
                for b in range(NB - 3, NB + 1):
                    step_a(b, b % 2, b // 2)

            load_a(0, 0)
            over_a()
            all_landed(sp, a_g0, STORES)
            all_landed(sp, a_g1, STORES)
            all_landed(sp, a_x1, STORES)
            all_landed(sp, x_kept, 16 * (GE // 2))

            def load_e1(g, q):
                after(sp, e1["centered"], g - 1)
                sp.dma_start(eslot(q), group(xd_t, g)).then_inc(e1_x[q], 16)

            def load_b(b, q):
                after(sp, B["out"], 4 * (b - 1))
                move_block(sp, x1_t, slot(q), b, b_in[q], store=False)

            def step_e1(g, q, u):
                if known(g, 0, GE - 1):
                    load_e1(g + 1, 1 - q)
                if known(g, 0, NB - 1):
                    load_b(g + 1, 1 - q)
                if known(g, 0, NB):
                    sp.wait_ge(B["h"], g + 1)
                    move_block(sp, h_t, slot(6 + q), g, b_h[q], store=True)
                if known(g, 1, GE + 1):
                    sp.wait_ge(e1["g1"], 2 * g)
                    sp.dma_start(group(g1d_t, g - 1), eslot(8 - q)).then_inc(e1_kept[1 - q], 16)
                if known(g, 1, NB + 1):
                    sp.wait_ge(B["out"], 4 * g)
                    move_block(sp, out, slot(9 - q), g - 1, b_out[1 - q], store=True)

            load_e1(0, 0)
            load_b(0, 0)
            sp.dma_start(fix_x[:], xd_t.rearrange("(p t) f -> p (t f)", p=P)[:, 0:D]).then_inc(fix_in, 16)
            over_both(sp, step_e1)
            all_landed(sp, e1_kept, 16 * (GE // 2))

            sp.wait_ge(fix["ve"], FIX_1_STEPS)

            sp.wait_ge(rel_cleared, 1)
            sp.dma_start(rel_sb[0:D, :, 0:D], relw.rearrange("r d e -> d r e")).then_inc(rel_weights, 16)
            sp.dma_start(rel_sb[D:P, :, D:P], relw.rearrange("r d e -> d r e")).then_inc(rel_weights, 16)

            def load_e2(g, q):
                after(sp, e2["h"], g - 1)
                sp.dma_start(eslot(q), group(xd_t, g)).then_inc(e2_in[q], 16)
                sp.dma_start(eslot(2 + q), group(g1d_t, g)).then_inc(e2_in[q], 16)

            def step_e2(g, q, u):
                if known(g, 0, GE - 1):
                    load_e2(g + 1, 1 - q)
                sp.wait_ge(e2["h"], g + 1)
                sp.dma_start(group(x1d_t, g), eslot(4 + q)).then_inc(e2_kept[q], 16)
                sp.dma_start(group(hd_t, g), eslot(6 + q)).then_inc(e2_kept[q], 16)

            load_e2(0, 0)
            step_e2(0, 0, 0)
            step_e2(1, 1, 0)
            with sp.Fori(1, GE // 2 - 1) as i:
                step_e2(2 * i, 0, i)
                step_e2(2 * i + 1, 1, i)
            step_e2(GE - 2, 0, GE // 2 - 1)
            step_e2(GE - 1, 1, GE // 2 - 1)
            all_landed(sp, e2_kept, 32 * (GE // 2))

            sp.wait_ge(fix["sent"], 48)

            by_edge = eattr[0:EFULL * KE, :].rearrange("(p t) f -> p t f", t=KE)

            def load_perm(s, q, u, kind):
                g = GE - 1 - s
                after(sp, c["tmp"], s - 1)
                sp.sem_inc(waits_over["sp"], 1)
                sp.dma_start(eslot(q), group(hd_t, g)).then_inc(c_hd[q], 16)
                after(sp, c_sent[q], 16 * GT * u)
                for lo, hi in ((0, ESPLIT), (ESPLIT, EFULL)):
                    sp.dma_start(perm_rows[lo:hi, q, :, 0:D], by_edge[lo:hi, bass.ds(g * GT, GT), :]).then_inc(c_ef[q], 16)
                if kind == "whole":
                    sp.dma_start(perm_rows[EFULL:P, q, :, 0:D],
                                 eattr[bass.ds(g * GT + EFULL * KE, GT), :].unsqueeze(0)).then_inc(c_ef[q], 16)
                if kind == "part":
                    left = ETAIL % GT
                    sp.dma_start(perm_rows[EFULL:P, q, 0:left, 0:D], eattr[E - left:E, :].unsqueeze(0)).then_inc(c_ef[q], 16)

            over_perm(sp, load_perm)
            all_landed(sp, c_sent, ALL)

            def load_slots(j, s, q, u):
                after(sp, rel_sent[s], 16 * GS * u)
                by_lane = slot_t.rearrange("(l s) w -> l s w", l=P)
                sp.dma_start(slot_w[:, s, :, 0:RW], by_lane[:, bass.ds(j * GS, GS), :]).then_inc(rel_in[s], 16)

            over_slots(load_slots, sp)

            for s in range(SB):
                sp.wait_ge(rel_sent[s], 16 * GS * ((NGS - s + SB - 1) // SB))
            all_landed(sp, b_out, [STORES[0] + 16, STORES[1]])
            edge_view = edge_t[1:EPAD + 1, :].rearrange("(p t) w -> p (t w)", p=P)
            half = KE // 2 * MW
            for k in range(2):
                sp.dma_start(arena[:, k * half:(k + 1) * half],
                             edge_view[:, k * half:(k + 1) * half]).then_inc(edges_in, 16)

            def load_f(g, q, u):
                after(sp, f["out"], 4 * (g - 1))
                sp.dma_start(eslot(q), group(hd_t, g)).then_inc(f_in[q], 16)
                sp.dma_start(eslot(2 + q), group(x1d_t, g)).then_inc(f_in[q], 16)

            over_groups(sp, load_f)

        @block.vector
        def _(dve):
            v = nc.vector
            tt, ts, stt = v.tensor_tensor, v.tensor_scalar, v.scalar_tensor_tensor

            def link(ins, signal, n):
                ins.then_inc(signal, 1)
                dve.wait_ge(signal, n)

            o = Order(dve, prep)
            o.did(v.memset(dsti[:], KEY_PAD))
            o.did(v.memset(srci, 0))
            o.did(v.memset(tmp_j[:], R))
            o.did(v.memset(ones[:], 1.0))
            o.did(v.memset(zero, 0.0))
            o.did(v.memset(res_in[:], 0.0))
            o.did(v.memset(fix_two[:], 0.0))
            o.wait()
            v.memset(tmp_b[:], 0.0).then_inc(filled, 1)
            o.did(v.memset(onesk[:], 1.0))
            o.did(v.memset(same[:], 0.0))
            dve.wait_ge(loaded, 16 * N_LOADS)
            dve.wait_ge(consts, 4)
            o.do(v.tensor_copy(key[:], dsti[:]))
            o.do(ts(dsafe[:], key[:, 0:KE], float(N - 1), None, ALU.min))
            at_step["safe destinations"] = o.n
            o.did(ts(tmp_i[:], dsti[:, 0:KE], 5, P - 1, ALU.logical_shift_right, ALU.bitwise_and))
            o.did(ts(outi[:], dsti[:, 0:KE], CB - 1, None, ALU.bitwise_and))
            o.did(ts(slot_row[:], dsti[:, 0:KE], 12, None, ALU.logical_shift_right))
            o.did(v.tensor_copy(iota_h, iota_i))
            o.did(v.tensor_copy(relf[:], tmp_j[:]))
            o.did(v.tensor_copy(rel_no[:], iota_i[:, 0:R]))
            o.did(v.tensor_copy(tile_no[:], iota_i[0:1, 0:KS]))
            o.did(v.tensor_copy(meta[:, :, 0], srci))
            o.did(v.tensor_copy(meta[:, :, 1], eidi))
            o.wait()
            o.did(v.tensor_copy(lo_key[:], tmp_i[:]))
            o.do(stt(out=hi_key[:], in0=slot_row[:], scalar=float(CB), in1=outi[:], op0=ALU.mult, op1=ALU.add))

            def hot(t, k):
                after(dve, hot_used, t - 3)
                ts(lo_hot[:, k % 4, :], iota_h[:, 0:P], lo_key[:, bass.ds(t, 1)], None,
                   ALU.is_equal).then_inc(hot_made, 1)
                ts(hi_hot[:, k % 4, :], iota_h, hi_key[:, bass.ds(t, 1)], None,
                   ALU.is_equal).then_inc(hot_made, 1)

            for k in range(8):
                hot(k, k)
            with dve.Fori(1, KE // 8) as i:
                for k in range(8):
                    hot(8 * i + k, k)
            dve.wait_ge(hot_used, KE)
            ts(degs[:, 0, :].rearrange("p (a c) -> p a c", a=2), banks[:, 0:2, 0:KN // 2], 1.0, None,
               ALU.add).then_inc(deg_read, 1)
            dve.wait_ge(deg_root, 1)
            o.do(v.reciprocal(dinv, degs[:, 1, :]))

            def centre(s, n, st, c, xin, xc):
                link(v.tensor_reduce(st[:, 0, :], cols(xin), AX.X, ALU.add), s["rows"], row_steps(s, n, 1))
                link(ts(st[:, 1, :], st[:, 0, :], 1.0 / D, None, ALU.mult), s["rows"], row_steps(s, n, 2))
                tt(cols(xc), cols(xin), wide(st[:, 1, :], c), ALU.subtract).then_inc(s["centered"], 1)

            def deviation(s, n, st, sq):
                dve.wait_ge(s["square"], n + 1)
                link(v.tensor_reduce(st[:, 5, :], cols(sq), AX.X, ALU.add), s["rows"], row_steps(s, n, 3))
                ts(st[:, 2, :], st[:, 5, :], 1.0 / D, EPS, ALU.mult, ALU.add).then_inc(s["rows"], 1)
                dve.wait_ge(s["std"], n + 1)
                link(v.reciprocal(st[:, 4, :], st[:, 3, :]), s["rows"], row_steps(s, n, 5))

            def relu_times(to, xc, factor, c):
                return stt(out=cols(to), in0=cols(xc), scalar=0.0, in1=wide(factor, c), op0=ALU.max, op1=ALU.mult)

            def half_a(b, q, u, z):
                at = slice(z * CB // 2, (z + 1) * CB // 2)
                dve.wait_ge(A["g1"], 4 * b + 2 * z + 2)
                if z == 0:
                    after(dve, a_x1[q], 16 * u)
                x1 = cols(slot(10 + q))[:, at, :]
                link(tt(x1, cols(slot(8 + q))[:, at, :], cols(slot(q))[:, at, :], ALU.add), A["xu"], 2 * b + z + 1)
                tt(x1, x1, b2_over(CB // 2), ALU.add).then_inc(A["x1"], 1)

            def step_a(b, q, u):
                st = stat[:, q]
                if known(b, 0, NB):
                    dve.wait_ge(a_in[q], 16 * (u + 1) + (16 if isinstance(b, int) and b == NB - 1 else 0))
                    centre(A, b, st, CB, slot(q), slot(2 + q))
                if known(b, 1, NB + 1):
                    half_a(b - 1, 1 - q, u - (1 - q), 0)
                if known(b, 0, NB):
                    deviation(A, b, st, slot(4 + q))
                    link(tt(st[:, 5, :], st[:, 4, :], dinv[:, bass.ds(b * CB, CB)], ALU.mult), A["rows"], row_steps(A, b, 6))
                    after(dve, a_g0[q], 16 * u)
                    relu_times(slot(6 + q), slot(2 + q), st[:, 5, :], CB).then_inc(A["g"], 1)
                if known(b, 1, NB + 1):
                    half_a(b - 1, 1 - q, u - (1 - q), 1)

            over_blocks(dve, step_a)

            o.did(tt(same[:, 1:KE], key[:, 1:KE], key[:, 0:KE - 1], ALU.is_equal))
            o.did(ts(head[:], key[:, 0:KE], key[:, 0:1], None, ALU.is_equal))
            o.did(tt(tmp_a[:, 0:KE], key[:, 1:KE + 1], key[:, 0:KE], ALU.is_equal))
            o.did(ts(diag[:], ident[:], key[:, 0:1], None, ALU.mult))
            at_step["first keys"] = o.n
            o.wait()
            o.do(tt(tmp_b[:, 0:KE], tmp_a[:, 0:KE], head[:], ALU.max))
            o.did(stt(out=outi[:], in0=tmp_b[:, 0:KE], scalar=float(SKIP), in1=key[:, 0:KE], op0=ALU.mult, op1=ALU.add))
            o.do(tt(fix_s[:, 0:1], key[:, KE:KE + 1], key[:, 0:1], ALU.is_equal))
            o.did(stt(out=fix_i[:], in0=fix_s[:, 0:1], scalar=float(SKIP), in1=key[:, 0:1], op0=ALU.mult, op1=ALU.add))
            o.did(ts(last_i[:], key[:, KE - 1:KE], float(N - 1), None, ALU.min))
            o.do(v.tensor_tensor_scan(out=tmp_a[:, 0:KE], data0=same[:, 0:KE], data1=onesk[:], initial=0.0,
                                      op0=ALU.mult, op1=ALU.add))
            o.do(v.tensor_copy(fix_s[:, 2:3], tmp_a[:, KE - 1:KE]))
            o.do(ts(tmp_a[:, 0:KE], tmp_a[:, 0:KE], 1.0, None, ALU.add))
            at_step["edge degrees"] = o.n
            o.do(v.tensor_reduce(fix_s[:, 3:4], head[:], AX.X, ALU.add))
            o.did(stt(out=hd_i[:], in0=fix_s[:, 3:4], scalar=-2.0, in1=meta[:, 0:1, 1], op0=ALU.add, op1=ALU.add))
            dve.wait_ge(prep_pe, 1)
            o.did(v.tensor_copy(first_row[:], bank(0)[:, 0:P]))
            o.did(v.tensor_copy(res_sb[:], bank(0)[:, P:2 * P]))
            o.did(v.tensor_copy(res1_sb[:], bank(0)[:, 2 * P:3 * P]))
            o.wait()
            o.do(stt(out=carry[:], in0=first_row[:], scalar=key[:, KE - 1:KE], in1=upper[:], op0=ALU.is_equal, op1=ALU.mult))
            at_step["carry"] = o.n
            dve.wait_ge(prep_act, 1)
            o.do(v.reciprocal(dinv_e[:], tmp_b[:, 0:KE]))
            o.do(tt(dinv2_e[:], dinv_e[:], dinv_e[:], ALU.mult))
            dve.wait_ge(prep_pe, 2)
            o.do(tt(fix_s[:, 4:5], bank(0)[:, 0:1], fix_s[:, 3:4], ALU.add))
            o.do(ts(fix_s[:, 5:6], fix_s[:, 4:5], 1.0, None, ALU.add))
            at_step["fix degrees"] = o.n
            dve.wait_ge(prep_act, 2)
            o.do(v.reciprocal(fix_s[:, 7:8], fix_s[:, 6:7]))

            def sum_group(s, g, q, width):
                for k in range(GT):
                    t = g * GT + k
                    former = rows_e[:, q, k - 1, 0:width] if k else rows_e[:, 1 - q, GT - 1, 0:width]
                    after(dve, s["run"], t)
                    stt(out=rows_e[:, q, k, 0:width], in0=former, scalar=same[:, bass.ds(t, 1)],
                        in1=rows_g[:, q, k, 0:width], op0=ALU.mult, op1=ALU.add).then_inc(s["run"], 1)
                    after(dve, s["head"], t)
                    stt(out=hsum[:, 0:width], in0=rows_g[:, q, k, 0:width], scalar=head[:, bass.ds(t, 1)],
                        in1=hsum[:, 0:width], op0=ALU.mult, op1=ALU.add).then_inc(s["head"], 1)

            def clear(n):
                v.memset(rows_e[:, 1, GT - 1, :], 0.0).then_inc(cleared, 1)
                v.memset(hsum[:], 0.0).then_inc(cleared, 1)
                dve.wait_ge(cleared, 2 * n)

            clear(1)

            def e1_part(g, q, u):
                after(dve, e1["turned"], 2 * (g - 1))
                dve.wait_ge(e1_got[q], 16 * GT * (u + 1))
                sum_group(e1, g, q, D)
                dve.wait_ge(e1["run"], GT * (g + 1))
                link(tt(cols(eslot(5 + q)), rows_e[:, q, :, 0:D], wide(dinv_e[:, bass.ds(g * GT, GT)], GT), ALU.mult),
                     e1["rows"], row_steps(e1, g, 8))
                tt(eslot(5 + q), eslot(5 + q), eslot(4), ALU.add).then_inc(e1["a"], 1)

            def e1_keep(g, q, u, c):
                n, w = 2 * g + c, 8 - 2 * c
                dve.wait_ge(e1["u"], n + 1)
                if c == 0:
                    after(dve, e1_sent[q], 16 * GT * u)
                    after(dve, e1_kept[q], 16 * u)
                tt(cols(eslot(7 + q))[:, 8 * c:8 * c + w, :], cols(bank(6)[:, 0:w * D]),
                   wide(dinv_e[:, bass.ds(g * GT + 8 * c, w)], w), ALU.mult).then_inc(e1["g1"], 1)

            def quad_b(b, q, u, z):
                n = 4 * b + z
                at = slice(8 * z, 8 * z + 8)
                low, leaky = part(arena, 10 * BW + (2 + z % 2) * MM, [MM]), part(arena, 11 * BW + z % 2 * MM, [MM])
                dve.wait_ge(B["low"], n + 1)
                if z == 0:
                    after(dve, b_out[q], 16 * u)
                link(tt(leaky, bank(4 + z % 2), low, ALU.max), B["leaky"], n + 1)
                tt(cols(slot(8 + q))[:, at, :], cols(leaky), cols(slot(q))[:, at, :], ALU.add).then_inc(B["out"], 1)

            def step_e1(g, q, u):
                st = stat[:, q]
                if known(g, 0, GE):
                    dve.wait_ge(e1_x[q], 16 * (u + 1))
                    centre(e1, g, estat[:], GT, eslot(q), eslot(2))
                if known(g, 0, NB):
                    dve.wait_ge(b_in[q], 16 * (u + 1))
                    centre(B, g, st, CB, slot(q), slot(2 + q))
                if known(g, 0, GE):
                    deviation(e1, g, estat[:], eslot(3))
                    link(tt(estat[:, 5, :], estat[:, 4, :], dinv2_e[:, bass.ds(g * GT, GT)], ALU.mult), e1["rows"], row_steps(e1, g, 6))
                    relu_times(eslot(4), eslot(2), estat[:, 5, :], GT).then_inc(e1["rows"], 1)
                if known(g, 0, NB):
                    deviation(B, g, st, slot(4 + q))
                    after(dve, b_h[q], 16 * u)
                    relu_times(slot(6 + q), slot(2 + q), st[:, 4, :], CB).then_inc(B["h"], 1)
                if known(g, 0, GE):
                    dve.wait_ge(e1["rows"], row_steps(e1, g, 7))
                    e1_part(g, q, u)
                before = (g - 1, 1 - q, u - (1 - q))
                if known(g, 1, GE + 1):
                    e1_keep(*before, 0)
                if known(g, 1, NB + 1):
                    quad_b(*before, 0)
                    quad_b(*before, 1)
                if known(g, 1, GE + 1):
                    e1_keep(*before, 1)
                if known(g, 1, NB + 1):
                    quad_b(*before, 2)
                    quad_b(*before, 3)

            over_both(dve, step_e1)
            dve.wait_ge(B["square"], NB)
            v.memset(rel_sb, 0.0).then_inc(rel_cleared, 1)

            fo = Order(dve, fix["ve"])

            def fix_norm(n, xin):
                fo.do(v.tensor_reduce(fix_s[:, 8:9], xin[:], AX.X, ALU.add))
                fo.do(ts(fix_s[:, 9:10], fix_s[:, 8:9], 1.0 / D, None, ALU.mult))
                fo.do(ts(fix_c[:], xin[:], fix_s[:, 9:10], None, ALU.subtract))
                fo.do(tt(fix_q[:], fix_c[:], fix_c[:], ALU.mult))
                fo.do(v.tensor_reduce(fix_s[:, 8:9], fix_q[:], AX.X, ALU.add))
                fo.do(ts(fix_s[:, 9:10], fix_s[:, 8:9], 1.0 / D, EPS, ALU.mult, ALU.add))
                at_step[f"variance {n}"] = fo.n
                dve.wait_ge(fix["act"], 3 * n + 1)
                fo.do(v.reciprocal(fix_s[:, 11:12], fix_s[:, 10:11]))

            dve.wait_ge(fix_in, 16)
            dve.wait_ge(fix["pe"], 1)
            dve.wait_ge(e1["head"], KE)
            fo.did(tt(fix_sum[:, 0:D], bank(0)[:, 0:D], hsum[:, 0:D], ALU.add))
            fix_norm(0, fix_x)
            fo.do(ts(fix_sum[:, 0:D], fix_sum[:, 0:D], fix_s[:, 7:8], None, ALU.mult))
            fo.do(ts(fix_s[:, 8:9], fix_s[:, 11:12], fix_s[:, 7:8], fix_s[:, 7:8], ALU.mult, ALU.mult))
            fo.do(ts(fix_c[:], fix_c[:], 0.0, fix_s[:, 8:9], ALU.max, ALU.mult))
            fo.do(tt(fix_two[:, 0:D], fix_c[:], fix_sum[:, 0:D], ALU.add))
            at_step["fix a"] = fo.n
            dve.wait_ge(fix["pe"], 4)
            fo.did(ts(fix_g1[:], bank(3)[:, 0:D], fix_s[:, 7:8], None, ALU.mult))
            at_step["fix 0"] = fo.n
            assert fo.n == FIX_1_STEPS, fo.n

            o = Order(dve, sort)
            o.do(ts(pos[:], relf[:], float(R), float(SLOT_SKIP), ALU.is_equal, ALU.mult))
            for r in range(R):
                o.do(ts(tmp_a[:, 0:KE], relf[:], float(r), None, ALU.is_equal, ALU.add, accum_out=cnt[:, 0, r:r + 1]))
            at_step["counts"] = o.n
            dve.wait_ge(prep_pe, 3)
            totals, before = bank(1)[:, 0:R], bank(1)[:, R:2 * R]
            o.do(v.tensor_copy(cnti[:, 0, :], totals))
            o.do(ts(cnti[:, 1, :], cnti[:, 0, :], P - 1, None, ALU.add))
            o.do(ts(cnti[:, 0, :], cnti[:, 1, :], 7, None, ALU.logical_shift_right))
            o.do(v.tensor_copy(cnt[:, 1, :], cnti[:, 0, :]))
            o.do(v.tensor_tensor_scan(out=cnt[:, 2, :], data0=onesk[:, 0:R], data1=cnt[:, 1, :],
                                      initial=0.0, op0=ALU.mult, op1=ALU.add))
            o.do(tt(cnt[:, 3, :], cnt[:, 2, :], cnt[:, 1, :], ALU.subtract))
            o.do(stt(out=cnt[:, 5, :], in0=cnt[:, 3, :], scalar=float(P), in1=before, op0=ALU.mult, op1=ALU.add))
            o.do(ts(cnt[:, 4, :], cnt[:, 5, :], -1.0, None, ALU.add))

            def place(r, done):
                dve.wait_ge(sort, done)
                link(ts(tmp_b[:, 0:KE], relf[:], rel_no[:, bass.ds(r, 1)], None, ALU.is_equal), sort, done + 1)
                link(v.tensor_tensor_scan(out=tmp_a[:, 0:KE], data0=onesk[:], data1=tmp_b[:, 0:KE],
                                          initial=cnt[:, 4, bass.ds(r, 1)], op0=ALU.mult, op1=ALU.add), sort, done + 2)
                link(tt(tmp_a[:, 0:KE], tmp_a[:, 0:KE], tmp_b[:, 0:KE], ALU.mult), sort, done + 3)
                tt(pos[:], pos[:], tmp_a[:, 0:KE], ALU.add).then_inc(sort, 1)

            for r in range(GE, R):
                place(r, o.n)
                o.n += 4
            placed = o.n

            clear(2)

            def step_e2(g, q, u):
                dve.wait_ge(e2_got[q], 16 * GT * (u + 1))
                sum_group(e2, g, q, D)
                dve.wait_ge(e2_in[q], 32 * (u + 1))
                after(dve, e2_kept[q], 32 * u)
                after(dve, e2_sent[q], 16 * GT * u)
                dve.wait_ge(e2["run"], GT * (g + 1))
                x1 = eslot(4 + q)
                link(tt(cols(x1), rows_e[:, q, :, 0:D], cols(eslot(2 + q)), ALU.add), e2["rows"], 9 * g + 1)
                link(tt(cols(x1), cols(x1), wide(dinv_e[:, bass.ds(g * GT, GT)], GT), ALU.mult), e2["rows"], 9 * g + 2)
                link(tt(x1, x1, eslot(q), ALU.add), e2["rows"], 9 * g + 3)
                link(tt(cols(x1), cols(x1), b2_over(GT), ALU.add), e2["rows"], 9 * g + 4)
                centre(e2, g, estat[:], GT, x1, eslot(2 + q))
                place(g, placed + 4 * g)
                deviation(e2, g, estat[:], eslot(8))
                relu_times(eslot(6 + q), eslot(2 + q), estat[:, 4, :], GT).then_inc(e2["h"], 1)

            over_groups(dve, step_e2)

            dve.wait_ge(fix["pe"], 5)
            dve.wait_ge(e2["head"], KE)
            fo.do(tt(fix_sum[:, 0:D], bank(0)[:, 0:D], hsum[:, 0:D], ALU.add))
            fo.do(tt(fix_sum[:, 0:D], fix_sum[:, 0:D], fix_g1[:], ALU.add))
            fo.do(ts(fix_sum[:, 0:D], fix_sum[:, 0:D], fix_s[:, 7:8], None, ALU.mult))
            fo.do(tt(fix_x1[:], fix_sum[:, 0:D], fix_x[:], ALU.add))
            fo.do(tt(fix_x1[:], fix_x1[:], b2_sb[:], ALU.add))
            fix_norm(1, fix_x1)
            fo.did(ts(fix_h[:], fix_c[:], 0.0, fix_s[:, 11:12], ALU.max, ALU.mult))
            at_step["fix 1"] = fo.n

            o = Order(dve, sort)
            o.n = placed + 4 * GE
            o.wait()
            o.do(v.tensor_copy(tmp_i[:], pos[:]))
            o.did(ts(tmp_j[:], tmp_i[:], P - 1, None, ALU.bitwise_and))
            o.do(ts(dsafe[:], tmp_i[:], 7, None, ALU.logical_shift_right))
            o.did(stt(out=slot_row[:], in0=tmp_j[:], scalar=float(KS), in1=dsafe[:], op0=ALU.mult, op1=ALU.add))
            at_step["slot rows"] = o.n
            goes_on, ends = lo_key, hi_key
            o.did(v.tensor_copy(goes_on[:, 0:KE - 1], same[:, 1:KE]))
            o.do(v.memset(goes_on[:, KE - 1:KE], 1.0))
            o.do(ts(ends[:], goes_on[:], -1.0, 1.0, ALU.mult, ALU.add))

            dve.wait_ge(c_last, 16)

            def step_perm(s, q, u, kind):
                g = GE - 1 - s
                dve.wait_ge(c_hd[q], 16 * (u + 1))
                after(dve, c["hf"], GT * s)
                dve.sem_inc(waits_over["dve"], 1)
                link(tt(cols(eslot(2)), cols(eslot(q)), wide(ends[:, bass.ds(g * GT, GT)], GT), ALU.mult), c["tmp"], s + 1)
                after(dve, c_sent[q], 16 * GT * u)
                for j in range(GT):
                    k = GT - 1 - j
                    if j:
                        later = perm_rows[:, q, k + 1, D + 2:RW]
                    else:
                        later = h_last[:] if isinstance(s, int) and s == 0 else perm_rows[:, 1 - q, 0, D + 2:RW]
                    after(dve, c["hf"], GT * s + j)
                    stt(out=perm_rows[:, q, k, D + 2:RW], in0=later, scalar=goes_on[:, bass.ds(g * GT + k, 1)],
                        in1=cols(eslot(2))[:, k, :], op0=ALU.mult, op1=ALU.add).then_inc(c["hf"], 1)

            over_perm(dve, step_perm)

            o.did(v.tensor_copy(tile_rel[0:1, 0, :], tile_no[:]))
            o.do(v.memset(tile_rel[0:1, 1, :], 0.0))
            for r in range(R - 1):
                o.do(stt(out=tile_rel[0:1, 1, :], in0=tile_rel[0:1, 0, :], scalar=cnt[0:1, 2, r:r + 1],
                         in1=tile_rel[0:1, 1, :], op0=ALU.is_ge, op1=ALU.add))
            o.did(v.tensor_copy(tile_reli[:], tile_rel[0:1, 1, :]))
            at_step["tiles"] = o.n

            def rel_work(j, s, q, u):
                dve.wait_ge(rel_in[s], 16 * (u + 1))
                after(dve, rel_sent[s], 16 * GS * u)
                number = slot_w.bitcast(I32)[:, s, :, D + 1]
                link(ts(slot_e[:, s, :], number, 0.0, float(ROW_SKIP), ALU.is_equal, ALU.mult), rel["idx"], 2 * j + 1)
                link(tt(slot_idx[:, s, :], slot_e[:, s, :], number, ALU.add), rel["idx"], 2 * j + 2)
                made = bank(2 + q).rearrange("p (k f) -> p k f", f=P)
                dve.wait_ge(rel["tr"], j + 1)
                tt(slot_z[:, q], made[:, :, 0:D], slot_w[:, s, :, 0:D], ALU.add).then_inc(rel["z"], 1)
                dve.wait_ge(rel["th"], j + 1)
                link(tt(slot_q[:, q], slot_th[:, q], made[:, :, D:P], ALU.mult), rel["q"], j + 1)
                v.tensor_reduce(slot_w[:, s, :, WW - 1], slot_q[:, q], AX.X, ALU.add).then_inc(rel["att"], 1)

            over_slots(rel_work, dve)

            o = Order(dve, soft)
            dve.wait_ge(edges_in, 32)
            edge_rows = arena[:].rearrange("p (t w) -> p t w", w=MW)
            att, bwd, pen, mx, arg = lo_key, hi_key, tmp_a, pos, tmp_b
            o.did(v.tensor_copy(att[:], edge_rows[:, :, D]))
            o.do(ts(pen[:], same[:], -1.0, FAR, ALU.add, ALU.mult))
            o.did(v.memset(edge_rows[:, :, D], 1.0))
            o.do(v.tensor_tensor_scan(out=arg[:, 0:KE], data0=pen[:, 0:KE], data1=att[:], initial=-FAR,
                                      op0=ALU.add, op1=ALU.max))
            o.do(v.tensor_tensor_scan(out=bwd[:][:, ::-1], data0=pen[:, 1:KE + 1][:, ::-1], data1=arg[:, 0:KE][:, ::-1],
                                      initial=-FAR, op0=ALU.add, op1=ALU.max))
            o.did(ts(diag[:], ident[:], key[:, KE - 1:KE], None, ALU.mult))
            o.did(ts(diag_max[:, 0, :], ident[:], arg[:, KE - 1:KE], None, ALU.mult))
            o.did(ts(diag_max[:, 1, :], ident[:], bwd[:, 0:1], None, ALU.mult))
            at_step["last segments"] = o.n
            dve.wait_ge(soft_pe, 1)
            last_keys = bank(0)[:, 0:P]
            for n, k in enumerate((0, KE - 1)):
                o.did(ts(seen[:, 0:P], last_keys, key[:, k:k + 1], -1.0, ALU.is_equal, ALU.add))
                o.do(ts(seen[:, P:2 * P], first_row[:], key[:, k:k + 1], -1.0, ALU.is_equal, ALU.add))
                o.do(stt(out=seen, in0=seen, scalar=FAR, in1=bank(0)[:, P:3 * P], op0=ALU.mult, op1=ALU.add))
                o.do(v.tensor_reduce(smax[:, n:n + 1], seen, AX.X, ALU.max))
            for n, k in enumerate((0, KE - 1)):
                o.do(ts(arg[:, 0:KE], key[:, 0:KE], key[:, k:k + 1], -1.0, ALU.is_equal, ALU.add))
                o.do(ts(arg[:, 0:KE], arg[:, 0:KE], FAR, smax[:, n:n + 1], ALU.mult, ALU.add))
                o.do(tt(mx[:], arg[:, 0:KE], mx[:] if n else bwd[:], ALU.max))
            o.do(tt(arg[:, 0:KE], att[:], mx[:], ALU.subtract))
            at_step["exponents"] = o.n

            clear(3)

            def f_post(g, q, u, c):
                n, w = 4 * g + c, min(4, GT - 4 * c)
                at = slice(4 * c, 4 * c + w)
                dve.wait_ge(f["low"], n + 1)
                if c == 0:
                    after(dve, f_sent[q], 16 * GT * u)
                leaky = part(chain, (4 + c % 2) * MM, [MM])[:, 0:w * P].rearrange("p (k f) -> p k f", f=P)
                low = part(chain, (2 + c % 2) * MM, [MM])[:, 0:w * P].rearrange("p (k f) -> p k f", f=P)
                o_ps = bank(2 + c % 2)[:, 0:w * P].rearrange("p (k f) -> p k f", f=P)
                link(tt(leaky, o_ps, low, ALU.max), f["leaky"], n + 1)
                link(tt(halves[:, c % 2, 0:w, :], leaky[:, :, 0:D], leaky[:, :, D:P], ALU.add), f["half"], n + 1)
                tt(cols(eslot(7 + q))[:, at, :], halves[:, c % 2, 0:w, :], cols(eslot(2 + q))[:, at, :],
                   ALU.add).then_inc(f["out"], 1)

            def step_f(g, q, u):
                if known(g, 0, GE):
                    dve.wait_ge(f["weighted"], GT * (g + 1))
                    sum_group(f, g, q, MW)
                    dve.wait_ge(f["run"], GT * (g + 1))
                    link(ts(rden[:, 0, :], rows_e[:, q, :, D], TINY, None, ALU.max), f["rows"], 3 * g + 1)
                    link(v.reciprocal(rden[:, 1, :], rden[:, 0, :]), f["rows"], 3 * g + 2)
                    link(tt(cols(eslot(6)), rows_e[:, q, :, 0:D], wide(rden[:, 1, :], GT), ALU.mult), f["rows"], 3 * g + 3)
                    dve.wait_ge(f_in[q], 32 * (u + 1))
                    after(dve, f["turned"], 4 * g)
                    two = eslot(4, 2).rearrange("p (k f) -> p k f", f=P)
                    tt(two[:, :, 0:D], cols(eslot(q)), cols(eslot(6)), ALU.add).then_inc(f["two"], 1)
                    tt(two[:, :, D:P], cols(eslot(q)), cols(eslot(6)), ALU.mult).then_inc(f["two"], 1)
                if known(g, 1, GE + 1):
                    for c in range(4):
                        f_post(g - 1, 1 - q, u - (1 - q), c)

            over_groups(dve, step_f)
            step_f(GE, 0, GE // 2)

            dve.wait_ge(fix["pe"], 6)
            dve.wait_ge(f["head"], KE)
            fo.do(tt(fix_sum[:], bank(0)[:, 0:MW], hsum[:], ALU.add))
            fo.do(ts(fix_s[:, 8:9], fix_sum[:, D:MW], TINY, None, ALU.max))
            fo.do(v.reciprocal(fix_s[:, 9:10], fix_s[:, 8:9]))
            fo.do(ts(fix_c[:], fix_sum[:, 0:D], fix_s[:, 9:10], None, ALU.mult))
            fo.did(tt(fix_two[:, 0:D], fix_c[:], fix_h[:], ALU.add))
            fo.did(tt(fix_two[:, D:P], fix_c[:], fix_h[:], ALU.mult))
            at_step["fix operands"] = fo.n
            dve.wait_ge(fix["act"], 6)
            fo.do(tt(fix_hid[:], bank(3)[:, 0:P], fix_low[:], ALU.max))
            fo.do(tt(fix_q[:], fix_hid[:, 0:D], fix_hid[:, D:P], ALU.add))
            fo.did(tt(fix_out[:], fix_q[:], fix_x1[:], ALU.add))
            at_step["fix 2"] = fo.n

        @block.gpsimd
        def _(pool):
            pool.iota(iota_i, pattern=[[1, KN]], base=0, channel_multiplier=0).then_inc(consts, 1)
            pool.iota(eidi, pattern=[[1, KE]], base=1, channel_multiplier=KE).then_inc(consts, 1)
            pool.wait_ge(filled, 1)
            pool.affine_select(out=ident[:], in_=ones[:], compare_op=ALU.is_equal, fill=0.0, base=0,
                               pattern=[[1, P]], channel_multiplier=-1).then_inc(consts, 1)
            pool.affine_select(out=upper[:], in_=ones[:], compare_op=ALU.is_gt, fill=0.0, base=0,
                               pattern=[[1, P]], channel_multiplier=-1).then_inc(consts, 1)

            def alone():
                pool.sem_inc(waits_over["pool"], 1)

            def scatter(table, idx, of, bound, signal):
                pool.indirect_dma_start(out=table[:, :], out_offset=bass.IndirectOffsetOnAxis(ap=idx, axis=0),
                                        in_=of, in_offset=None, bounds_check=bound,
                                        oob_is_err=False).then_inc(signal, 16)

            def gather(to, table, idx, signal):
                pool.indirect_dma_start(out=to, out_offset=None, in_=table[:, :],
                                        in_offset=bass.IndirectOffsetOnAxis(ap=idx, axis=0)).then_inc(signal, 16)

            pool.wait_ge(prep, at_step["safe destinations"])

            def get_x(g, q, u):
                after(pool, x_kept[q], 16 * u)
                alone()
                pool.tensor_copy(src_idx[:, q, :], dsafe[:, bass.ds(g * GT, GT)]).then_inc(x_idx, 1)
                pool.wait_ge(x_idx, g + 1)
                alone()
                for k in range(GT):
                    gather(cols(eslot(q))[:, k, :], x, src_idx[:, q, k:k + 1], x_got[q])

            def keep_x(g, q, u):
                pool.wait_ge(x_got[q], 16 * GT * (u + 1))
                alone()
                pool.dma_start(group(xd_t, g), eslot(q)).then_inc(x_kept[q], 16)

            get_x(0, 0, 0)
            get_x(1, 1, 0)
            keep_x(0, 0, 0)
            with pool.Fori(1, GE // 2) as i:
                get_x(2 * i, 0, i)
                keep_x(2 * i - 1, 1, i - 1)
                get_x(2 * i + 1, 1, i)
                keep_x(2 * i, 0, i)
            keep_x(GE - 1, 1, GE // 2 - 1)

            all_landed(pool, a_g0, STORES)

            def get(s, idx_ready, sems_got, table, g, q, u):
                pool.wait_ge(idx_ready, g + 1)
                after(pool, s["head"], GT * (g - 1))
                alone()
                for k in range(GT):
                    gather(rows_g[:, q, k, 0:D], table, src_idx[:, q, k:k + 1], sems_got[q])

            def send(table, phase, sent, g, q, of):
                pool.wait_ge(out_idx_ready, phase * GE + g + 1)
                alone()
                for k in range(GT):
                    scatter(table, out_idx[:, q, k:k + 1], cols(of)[:, k, :], N - 1, sent[q])

            def send_fix(n, table, row):
                pool.wait_ge(fix["ve"], at_step[f"fix {n}"])
                scatter(table, fix_i[:, 0:1], row[:], N - 1, fix["sent"])

            def send_e1(g, q, u):
                pool.wait_ge(e1["g1"], 2 * (g + 1))
                send(g1_t, 0, e1_sent, g, q, eslot(7 + q))

            def step_e1(g, q, u):
                get(e1, e1_src, e1_got, g0_t, g, q, u)
                if known(g, 2, GE):
                    send_e1(g - 2, q, u - 1)

            get(e1, e1_src, e1_got, g0_t, 0, 0, 0)
            get(e1, e1_src, e1_got, g0_t, 1, 1, 0)
            all_landed(pool, a_g1, STORES)
            with pool.Fori(1, GE // 2) as i:
                step_e1(2 * i, 0, i)
                step_e1(2 * i + 1, 1, i)
            send_e1(GE - 2, 0, GE // 2 - 1)
            send_e1(GE - 1, 1, GE // 2 - 1)
            send_fix(0, g1_t, fix_g1)
            all_landed(pool, e1_sent, ALL)
            pool.wait_ge(fix["sent"], 16)

            def send_e2(g, q, u):
                pool.wait_ge(e2["h"], g + 1)
                send(h_t, 1, e2_sent, g, q, eslot(6 + q))

            get(e2, e2_src, e2_got, g1_t, 0, 0, 0)
            get(e2, e2_src, e2_got, g1_t, 1, 1, 0)
            all_landed(pool, b_h, STORES)
            send_e2(0, 0, 0)
            with pool.Fori(1, GE // 2) as i:
                get(e2, e2_src, e2_got, g1_t, 2 * i, 0, i)
                send_e2(2 * i - 1, 1, i - 1)
                get(e2, e2_src, e2_got, g1_t, 2 * i + 1, 1, i)
                send_e2(2 * i, 0, i)
            send_e2(GE - 1, 1, GE // 2 - 1)
            send_fix(1, h_t, fix_h)
            all_landed(pool, e2_kept, 32 * (GE // 2))
            scatter(hd_t, hd_i[:, 0:1], fix_h[:], EPAD - 1, fix["sent"])
            all_landed(pool, e2_sent, ALL)
            pool.wait_ge(fix["sent"], 48)

            gather(h_last[:], h_t, last_i[:, 0:1], c_last)

            def send_perm(s, q, u, kind):
                pool.wait_ge(c_ef[q], features_in(u, kind))
                pool.wait_ge(c_meta, s + 1)
                pool.wait_ge(out_idx_ready, 2 * GE + s + 1)
                pool.wait_ge(c["hf"], GT * (s + 1))
                alone()
                for k in range(GT):
                    scatter(slot_t, out_idx[:, q, k:k + 1], perm_rows[:, q, k, :], P * KS - 1, c_sent[q])

            over_perm(pool, send_perm)

            def rel_get(j, s, u):
                pool.wait_ge(rel_in[s], 16 * (u + 1))
                alone()
                for k in range(GS):
                    gather(slot_w[:, s, k, RW:RW + D], h_t, slot_w[:, s, k, D:D + 1].bitcast(I32), rel_got[s])

            def rel_send(j, s):
                pool.wait_ge(rel["idx"], 2 * j + 2)
                pool.wait_ge(rel["att"], j + 1)
                alone()
                for k in range(GS):
                    scatter(edge_t, slot_idx[:, s, k:k + 1], slot_w[:, s, k, RW:WW], EPAD, rel_sent[s])

            def step_rel(j, s, q, u):
                rel_get(j, s, u)
                if known(j, 2, NGS):
                    rel_send(j - 2, (s - 2) % SB)

            over_slots(step_rel, pool)
            for j in range(NGS - 2, NGS):
                rel_send(j, j % SB)

            all_landed(pool, b_out, [STORES[0] + 16, STORES[1]])

            def send_f(g, q, u):
                pool.wait_ge(f["out"], 4 * (g + 1))
                send(out, 3, f_sent, g, q, eslot(7 + q))

            over_groups(pool, send_f)
            send_fix(2, out, fix_out)
            all_landed(pool, f_sent, ALL)
            pool.wait_ge(fix["sent"], 64)

        @block.scalar
        def _(act):
            copy, activation = nc.scalar.copy, nc.scalar.activation
            act.wait_ge(deg_read, 1)
            activation(degs[:, 1, :], degs[:, 0, :], ACT.Sqrt).then_inc(deg_root, 1)

            def square(s, n, xc, sq):
                act.wait_ge(s["centered"], n + 1)
                buffers = 2 if s is A or s is B else 1
                after(act, s["rows"], row_steps(s, n - buffers, 3))
                activation(sq, xc, ACT.Square).then_inc(s["square"], 1)

            def root(s, n, st):
                act.wait_ge(s["rows"], row_steps(s, n, 4))
                activation(st[:, 3, :], st[:, 2, :], ACT.Sqrt).then_inc(s["std"], 1)

            def quad_a(b, q, u, z):
                n = 4 * b + z
                act.wait_ge(A["turned"], n + 1)
                after(act, A["h"], n - 1)
                copy(part(chain, z % 2 * MM, [MM]), bank(z % 2)).then_inc(A["at"], 1)
                act.wait_ge(A["h"], n + 1)
                after(act, A["u"], n - 1)
                activation(part(chain, 2 * MM + z % 2 * 2 * MM, [2 * MM]), bank(2 + z % 2 * 2, 2), ACT.Relu,
                           bias=b1_sb[:, 0:1]).then_inc(A["relu"], 1)
                act.wait_ge(A["u"], n + 1)
                if z == 0:
                    after(act, a_g1[q], 16 * u)
                    after(act, A["xu"], 2 * (b - 1))
                copy(slot(8 + q)[:, z * MM:(z + 1) * MM], bank(6 + z % 2)).then_inc(A["g1"], 1)

            def step_a(b, q, u):
                before = (b - 1, 1 - q, u - (1 - q))
                if known(b, 0, NB):
                    square(A, b, slot(2 + q), slot(4 + q))
                if known(b, 1, NB + 1):
                    quad_a(*before, 0)
                    quad_a(*before, 1)
                if known(b, 0, NB):
                    root(A, b, stat[:, q])
                if known(b, 1, NB + 1):
                    quad_a(*before, 2)
                    quad_a(*before, 3)

            over_blocks(act, step_a)
            act.wait_ge(prep, at_step["edge degrees"])
            activation(tmp_b[:, 0:KE], tmp_a[:, 0:KE], ACT.Sqrt).then_inc(prep_act, 1)
            act.wait_ge(prep, at_step["fix degrees"])
            activation(fix_s[:, 6:7], fix_s[:, 5:6], ACT.Sqrt).then_inc(prep_act, 1)

            def index(ring, of, g, q, signal):
                copy(ring[:, q, :], of[:, bass.ds(g * GT, GT)]).then_inc(signal, 1)

            all_landed(act, x_kept, 16 * (GE // 2))
            index(src_idx, meta[:, :, 0], 0, 0, e1_src)

            def e1_turn(g, c):
                n, w = 2 * g + c, (4 - c) * P
                act.wait_ge(e1["turned"], n + 1)
                after(act, e1["h"], n - 1)
                copy(part(chain, c * MM, [MM])[:, 0:w], bank(0)[:, 0:w]).then_inc(e1["at"], 1)

            def e1_relu(g, c):
                n, w = 2 * g + c, (4 - c) * P
                act.wait_ge(e1["h"], n + 1)
                after(act, e1["u"], n - 1)
                activation(part(chain, 2 * MM + c * 2 * MM, [2, MM])[:, :, 0:w], banks[:, 2:4, 0:w], ACT.Relu,
                           bias=b1_sb[:, 0:1]).then_inc(e1["relu"], 1)

            def b_turn(b, z):
                n = 4 * b + z
                act.wait_ge(B["turned"], n + 1)
                after(act, B["o"], n - 1)
                copy(part(arena, 10 * BW + z % 2 * MM, [MM]), bank((1, 7)[z % 2])).then_inc(B["t"], 1)

            def b_low(b, z):
                n = 4 * b + z
                act.wait_ge(B["o"], n + 1)
                after(act, B["leaky"], n - 1)
                nc.scalar.mul(part(arena, 10 * BW + (2 + z % 2) * MM, [MM]), bank(4 + z % 2), 0.01).then_inc(B["low"], 1)

            def step_e1(g, q, u):
                if known(g, 0, GE - 1):
                    after(act, e1_got[1 - q], 16 * GT * (u + q))
                    index(src_idx, meta[:, :, 0], g + 1, 1 - q, e1_src)
                if known(g, 1, GE + 1):
                    after(act, e1_sent[1 - q], 16 * GT * (u - (1 - q)))
                    index(out_idx, outi, g - 1, 1 - q, out_idx_ready)
                if known(g, 0, GE):
                    square(e1, g, eslot(2), eslot(3))
                if known(g, 0, NB):
                    square(B, g, slot(2 + q), slot(4 + q))
                if known(g, 0, GE):
                    root(e1, g, estat[:])
                if known(g, 0, NB):
                    root(B, g, stat[:, q])
                one, two = known(g, 1, GE + 1), known(g, 1, NB + 1)
                for name, c in (("e_turn", 0), ("b_turn", 0), ("e_relu", 0), ("b_low", 0), ("b_turn", 1), ("e_turn", 1),
                                ("b_low", 1), ("b_turn", 2), ("e_relu", 1), ("b_low", 2), ("b_turn", 3), ("b_low", 3)):
                    if name == "e_turn" and one:
                        e1_turn(g - 1, c)
                    if name == "e_relu" and one:
                        e1_relu(g - 1, c)
                    if name == "b_turn" and two:
                        b_turn(g - 1, c)
                    if name == "b_low" and two:
                        b_low(g - 1, c)

            over_both(act, step_e1)

            act.wait_ge(fix["ve"], at_step["variance 0"])
            activation(fix_s[:, 10:11], fix_s[:, 9:10], ACT.Sqrt).then_inc(fix["act"], 1)
            act.wait_ge(fix["pe"], 2)
            copy(fix_t[0:D, :], bank(1)[0:D, 0:P]).then_inc(fix["act"], 1)
            act.wait_ge(fix["pe"], 3)
            activation(fix_hid[:], bank(2)[:, 0:P], ACT.Relu, bias=b1_sb[:, 0:1]).then_inc(fix["act"], 1)

            all_landed(act, e1_sent, ALL)

            def step_e2(g, q, u):
                if known(g, 0, GE - 1):
                    after(act, e2_got[1 - q], 16 * GT * (u + q))
                    index(src_idx, meta[:, :, 0], g + 1, 1 - q, e2_src)
                after(act, e2_sent[q], 16 * GT * u)
                index(out_idx, outi, g, q, out_idx_ready)
                square(e2, g, eslot(2 + q), eslot(8))
                root(e2, g, estat[:])

            index(src_idx, meta[:, :, 0], 0, 0, e2_src)
            step_e2(0, 0, 0)
            step_e2(1, 1, 0)
            with act.Fori(1, GE // 2 - 1) as i:
                step_e2(2 * i, 0, i)
                step_e2(2 * i + 1, 1, i)
            step_e2(GE - 2, 0, GE // 2 - 1)
            step_e2(GE - 1, 1, GE // 2 - 1)

            act.wait_ge(fix["ve"], at_step["variance 1"])
            activation(fix_s[:, 10:11], fix_s[:, 9:10], ACT.Sqrt).then_inc(fix["act"], 1)

            all_landed(act, e2_sent, ALL)
            act.wait_ge(sort, at_step["slot rows"])

            def step_perm(s, q, u, kind):
                g = GE - 1 - s
                after(act, c_sent[q], 16 * GT * u)
                copy(perm_rows.bitcast(I32)[:, q, :, D:D + 2], meta[:, bass.ds(g * GT, GT), :]).then_inc(c_meta, 1)
                index(out_idx, slot_row, g, q, out_idx_ready)

            over_perm(act, step_perm)

            def rel_turn(j, q):
                act.wait_ge(rel["turned"], j + 1)
                after(act, rel["tr"], j - 1)
                copy(slot_ht[:, q], bank(q).rearrange("p (k s) -> p k s", s=P)).then_inc(rel["ht"], 1)

            def rel_tanh(j, q):
                act.wait_ge(rel["z"], j + 1)
                after(act, rel["q"], j - 1)
                activation(slot_th[:, q], slot_z[:, q], ACT.Tanh).then_inc(rel["th"], 1)

            def step_rel(j, s, q, u):
                if known(j, 0, NGS - 1):
                    rel_turn(j + 1, 1 - q)
                rel_tanh(j, q)

            rel_turn(0, 0)
            over_slots(step_rel, act)

            act.wait_ge(soft, at_step["exponents"])
            activation(tmp_a[:, 0:KE], tmp_b[:, 0:KE], ACT.Exp).then_inc(soft_exp, 1)
            act.wait_ge(soft_exp, 1)

            all_landed(act, c_sent, ALL)
            edge_rows = arena[:].rearrange("p (t w) -> p t w", w=MW)

            def weigh(g, q):
                after(act, f["head"], GT * (g - 1))
                for k in range(GT):
                    t = g * GT + k
                    activation(rows_g[:, q, k, :], edge_rows[:, bass.ds(t, 1), :].rearrange("p a w -> p (a w)"), ACT.Copy,
                               scale=tmp_a[:, bass.ds(t, 1)]).then_inc(f["weighted"], 1)

            def f_turned(g, c):
                n, w = 4 * g + c, min(4, GT - 4 * c) * P
                act.wait_ge(f["turned"], n + 1)
                after(act, f["o"], n - 1)
                copy(part(chain, c % 2 * MM, [MM])[:, 0:w], bank(c % 2)[:, 0:w]).then_inc(f["t"], 1)

            def f_low(g, c):
                n, w = 4 * g + c, min(4, GT - 4 * c) * P
                act.wait_ge(f["o"], n + 1)
                after(act, f["leaky"], n - 1)
                nc.scalar.mul(part(chain, (2 + c % 2) * MM, [MM])[:, 0:w], bank(2 + c % 2)[:, 0:w], 0.01).then_inc(f["low"], 1)

            def step_f(g, q, u):
                if known(g, 1, GE + 1):
                    f_turned(g - 1, 0)
                    for c in range(4):
                        if c < 3:
                            f_turned(g - 1, c + 1)
                        f_low(g - 1, c)
                if known(g, 0, GE - 1):
                    weigh(g + 1, 1 - q)
                if known(g, 0, GE):
                    after(act, f_sent[q], 16 * GT * u)
                    index(out_idx, outi, g, q, out_idx_ready)

            weigh(0, 0)
            step_f(0, 0, 0)
            step_f(1, 1, 0)
            with act.Fori(1, GE // 2 - 1) as i:
                step_f(2 * i, 0, i)
                step_f(2 * i + 1, 1, i)
            for g in range(GE - 2, GE + 1):
                step_f(g, g % 2, g // 2)
            act.wait_ge(fix["pe"], 7)
            copy(fix_t[:], bank(1)[:, 0:P]).then_inc(fix["act"], 1)
            act.wait_ge(fix["pe"], 8)
            nc.scalar.mul(fix_low[:], bank(3)[:, 0:P], 0.01).then_inc(fix["act"], 1)

        @block.tensor
        def _(pe):
            matmul, transpose = nc.tensor.matmul, nc.tensor.transpose
            pe.wait_ge(loaded, 16 * N_LOADS)
            pe.wait_ge(consts, 4)

            def count(t, k):
                pe.wait_ge(hot_made, 2 * (t + 1))
                first, last = isinstance(t, int) and t == 0, isinstance(t, int) and t == KE - 1
                matmul(banks[:, 0, 0:KN // 2], lo_hot[:, k % 4, :], hi_hot[:, k % 4, 0:KN // 2],
                       start=first, stop=last, skip_group_check=True)
                matmul(banks[:, 1, 0:KN // 2], lo_hot[:, k % 4, :], hi_hot[:, k % 4, KN // 2:KN],
                       start=first, stop=last, skip_group_check=True).then_inc(hot_used, 1)

            for k in range(8):
                count(k, k)
            with pe.Fori(1, KE // 8 - 1) as i:
                for k in range(8):
                    count(8 * i + k, k)
            for k in range(8):
                count(KE - 8 + k, k)

            def turn_a(b, q, z):
                n = 4 * b + z
                pe.wait_ge(A["g"], b + 1)
                after(pe, A["at"], n - 1)
                for k in range(4):
                    at = (8 * z + 2 * k) * D
                    ins = transpose(bank(z % 2)[:, k * P:(k + 1) * P], slot(6 + q)[:, at:at + P], ident[:])
                ins.then_inc(A["turned"], 1)

            def hidden(to, at, w):
                matmul(bank(to)[:, 0:w], w1_sb[0:D, :], at[0:D, 0:w], start=True, stop=True)
                return matmul(bank(to + 1)[:, 0:w], w1_sb[D:P, :], at[D:P, 0:w], start=True, stop=True)

            def output(to, hid, tiles):
                for k in range(tiles):
                    at = k % 2 * MM + k // 2 * P
                    ins = matmul(bank(to)[:, k * D:(k + 1) * D], hid[:, at:at + P], w2_sb[:], start=True, stop=True)
                return ins

            def hidden_a(n, z):
                pe.wait_ge(A["at"], n + 1)
                after(pe, A["relu"], n - 1)
                hidden(2 + z % 2 * 2, part(chain, z % 2 * MM, [MM]), MM).then_inc(A["h"], 1)

            def output_a(n, z):
                pe.wait_ge(A["relu"], n + 1)
                after(pe, A["g1"], n - 1)
                output(6 + z % 2, part(chain, 2 * MM + z % 2 * 2 * MM, [2 * MM]), 8).then_inc(A["u"], 1)

            def step_a(b, q, u):
                if known(b, 1, NB + 1):
                    for z in range(4):
                        n = 4 * (b - 1) + z
                        if z == 0:
                            turn_a(b - 1, 1 - q, z)
                        hidden_a(n, z)
                        if z < 3:
                            turn_a(b - 1, 1 - q, z + 1)
                        output_a(n, z)

            over_blocks(pe, step_a)

            pe.wait_ge(prep, at_step["first keys"])
            pe.wait_ge(A["at"], 4 * NB)
            matmul(bank(0)[:, 0:P], ones[:], diag[:], start=True, stop=True)
            transpose(bank(0)[:, P:2 * P], res_in[:], ident[:])
            transpose(bank(0)[:, 2 * P:3 * P], fix_two[:], ident[:]).then_inc(prep_pe, 1)
            pe.wait_ge(prep, at_step["carry"])
            matmul(bank(0)[:, 0:1], carry[:], fix_s[:, 2:3], start=True, stop=True).then_inc(prep_pe, 1)
            pe.wait_ge(prep, at_step["fix degrees"])

            def e1_turn(g, q, c):
                n, pairs = 2 * g + c, 4 - c
                pe.wait_ge(e1["a"], g + 1)
                after(pe, e1["at"], n)
                for k in range(pairs):
                    at = (8 * c + 2 * k) * D
                    ins = transpose(bank(0)[:, k * P:(k + 1) * P], eslot(5 + q)[:, at:at + P], ident[:])
                ins.then_inc(e1["turned"], 1)

            def e1_hidden(g, c):
                n = 2 * g + c
                pe.wait_ge(e1["at"], n + 1)
                after(pe, e1["relu"], n)
                hidden(2, part(chain, c * MM, [MM]), (4 - c) * P).then_inc(e1["h"], 1)

            def e1_output(g, c):
                n = 2 * g + c
                pe.wait_ge(e1["relu"], n + 1)
                after(pe, e1["g1"], n)
                output(6, part(chain, 2 * MM + c * 2 * MM, [2 * MM]), 8 - 2 * c).then_inc(e1["u"], 1)

            def b_turn(b, q, z):
                n = 4 * b + z
                pe.wait_ge(B["h"], b + 1)
                after(pe, B["t"], n - 1)
                for k in range(4):
                    at = (8 * z + 2 * k) * D
                    ins = transpose(bank((1, 7)[z % 2])[:, k * P:(k + 1) * P], slot(6 + q)[:, at:at + P], ident[:])
                ins.then_inc(B["turned"], 1)

            def b_residual(b, z):
                n = 4 * b + z
                pe.wait_ge(B["t"], n + 1)
                after(pe, B["leaky"], n - 1)
                t = part(arena, 10 * BW + z % 2 * MM, [MM])
                for k in range(4):
                    at = slice(k * P, (k + 1) * P)
                    ins = matmul(bank(4 + z % 2)[:, at], t[:, at], res1_sb[:], start=True, stop=True)
                ins.then_inc(B["o"], 1)

            def step_e1(g, q, u):
                one, two = known(g, 1, GE + 1), known(g, 1, NB + 1)
                for name, k in (("e_turn", 0), ("b_turn", 0), ("e_hidden", 0), ("b_res", 0), ("b_turn", 1), ("e_output", 0),
                                ("e_turn", 1), ("b_res", 1), ("b_turn", 2), ("e_hidden", 1), ("b_res", 2), ("b_turn", 3),
                                ("e_output", 1), ("b_res", 3)):
                    if name == "e_turn" and one:
                        e1_turn(g - 1, 1 - q, k)
                    if name == "e_hidden" and one:
                        e1_hidden(g - 1, k)
                    if name == "e_output" and one:
                        e1_output(g - 1, k)
                    if name == "b_turn" and two:
                        b_turn(g - 1, 1 - q, k)
                    if name == "b_res" and two:
                        b_residual(g - 1, k)

            over_both(pe, step_e1)

            def carried(s, width, n):
                pe.wait_ge(s["run"], KE)
                matmul(bank(0)[:, 0:width], carry[:], rows_e[:, 1, GT - 1, 0:width],
                       start=True, stop=True).then_inc(fix["pe"], 1)

            carried(e1, D, 0)
            pe.wait_ge(fix["ve"], at_step["fix a"])
            transpose(bank(1)[0:D, 0:P], fix_two[:, 0:D], ident[:]).then_inc(fix["pe"], 1)
            pe.wait_ge(fix["act"], 2)
            matmul(bank(2)[:, 0:P], w1_sb[0:D, :], fix_t[0:D, :], start=True, stop=True).then_inc(fix["pe"], 1)
            pe.wait_ge(fix["act"], 3)
            matmul(bank(3)[:, 0:D], fix_hid[:], w2_sb[:], start=True, stop=True).then_inc(fix["pe"], 1)

            pe.wait_ge(sort, at_step["counts"])
            matmul(bank(1)[:, 0:R], ones[:], cnt[:, 0, :], start=True, stop=True)
            matmul(bank(1)[:, R:2 * R], upper[:], cnt[:, 0, :], start=True, stop=True).then_inc(prep_pe, 1)
            carried(e2, D, 1)

            def rel_turn(j, s, q, u):
                pe.wait_ge(rel_got[s], 16 * GS * (u + 1))
                after(pe, rel["ht"], j - 1)
                for k in range(GS):
                    ins = transpose(bank(q)[:, k * P:(k + 1) * P], slot_w[:, s, k, D + 2:WW - 1], ident[:])
                ins.then_inc(rel["turned"], 1)

            def rel_project(j, q):
                number = [pe.value_load(tile_reli[0:1, bass.ds(j * GS + k, 1)], min_val=0, max_val=R - 1)
                          for k in range(GS)]
                pe.wait_ge(rel["ht"], j + 1)
                after(pe, rel["q"], j - 1)
                flat = rel_sb.rearrange("p r f -> p (r f)")
                for k in range(GS):
                    ins = matmul(bank(2 + q)[:, k * P:(k + 1) * P], slot_ht[:, q, k, :],
                                 flat[:, bass.ds(number[k] * P, P)], start=True, stop=True)
                ins.then_inc(rel["tr"], 1)

            pe.wait_ge(sort, at_step["tiles"])
            pe.wait_ge(rel_weights, 32)

            def step_rel(j, s, q, u):
                if known(j, 0, NGS - 1):
                    rel_turn(j + 1, (s + 1) % SB, 1 - q, u + (s + 1) // SB)
                rel_project(j, q)

            rel_turn(0, 0, 0, 0)
            over_slots(step_rel, pe)

            pe.wait_ge(soft, at_step["last segments"])
            for k, d in enumerate((diag[:], diag_max[:, 0, :], diag_max[:, 1, :])):
                ins = matmul(bank(0)[:, k * P:(k + 1) * P], ones[:], d, start=True, stop=True)
            ins.then_inc(soft_pe, 1)

            def f_turn(g, c):
                n = 4 * g + c
                pe.wait_ge(f["two"], 2 * (g + 1))
                after(pe, f["t"], n - 1)
                for k in range(min(4, GT - 4 * c)):
                    at = (4 * c + k) * P
                    ins = transpose(bank(c % 2)[:, k * P:(k + 1) * P], eslot(4, 2)[:, at:at + P], ident[:])
                ins.then_inc(f["turned"], 1)

            def f_residual(g, c):
                n = 4 * g + c
                pe.wait_ge(f["t"], n + 1)
                after(pe, f["leaky"], n - 1)
                for k in range(min(4, GT - 4 * c)):
                    at = slice(k * P, (k + 1) * P)
                    ins = matmul(bank(2 + c % 2)[:, at], part(chain, c % 2 * MM, [MM])[:, at], res_sb[:], start=True, stop=True)
                ins.then_inc(f["o"], 1)

            def step_f(g, q, u):
                f_turn(g, 0)
                for c in range(4):
                    if c < 3:
                        f_turn(g, c + 1)
                    f_residual(g, c)

            pe.wait_ge(soft_exp, 1)
            over_groups(pe, step_f)
            carried(f, MW, 2)
            pe.wait_ge(fix["ve"], at_step["fix operands"])
            transpose(bank(1)[:, 0:P], fix_two[:], ident[:]).then_inc(fix["pe"], 1)
            pe.wait_ge(fix["act"], 5)
            matmul(bank(3)[:, 0:P], fix_t[:], res_sb[:], start=True, stop=True).then_inc(fix["pe"], 1)


_INS = ["x", "src", "dst", "edge_attr_64", "edge_type_32", "L0_gnn_W1", "L0_gnn_b1", "L0_gnn_W2", "L0_gnn_b2",
        "L1_gnn_relation_weight", "L1_gnn_res_w1", "L1_gnn_res_w2"]


def kernel(**inputs):
    import numpy as _np
    import concourse.bacc as _bacc
    from concourse import mybir as _mybir
    from concourse.bass_utils import run_bass_kernel_spmd as _run

    nc = _bacc.Bacc("TRN2", target_bir_lowering=False, num_devices=1)
    arrays, args = {}, []
    for name in _INS:
        a = _np.ascontiguousarray(inputs[name])
        arrays[f"in_{name}"] = a
        args.append(nc.dram_tensor(f"in_{name}", a.shape, _mybir.dt.from_np(a.dtype), kind="ExternalInput").ap())
    args.append(nc.dram_tensor("result", (N, D), F32, kind="ExternalOutput").ap())
    build(nc, *args)
    return _run(nc, [arrays], core_ids=[0]).results[0]["result"]
```

```python
from contextlib import ExitStack

import concourse.bass as bass
from concourse import mybir

ALU = mybir.AluOpType
ACT = mybir.ActivationFunctionType
AX = mybir.AxisListType
F32 = mybir.dt.float32
F16 = mybir.dt.float16
I32 = mybir.dt.int32

P = 128
N = 100000
E = 50000
D = 64
HID = 128
R = 32
EPS = 1e-5

CB = 32
BROWS = P * CB
NB = -(-N // BROWS)
NPAD = NB * BROWS
KN = NB * CB
BW = CB * D
TAIL_P = (N - (NB - 1) * BROWS) // CB
TAIL_SPLIT = TAIL_P // 16 * 16

KE = 392
EFULL = E // KE
ETAIL = E - EFULL * KE
GT = 14
GE = KE // GT
EPAD = P * KE
ESPLIT = 112

MM = 512

KS = 424
GS = 4
NGS = KS // GS
SB = 4
RW = 2 * D + 2
MW = D + 1
WW = RW + MW

CQ = MM // D
QROWS = P * CQ
NQ = -(-N // QROWS)
Q_A = NB - 1
Q_TAIL_P = (N - (NQ - 1) * QROWS) // CQ

KEY_PAD = 1 << 20
SKIP = 1 << 20
SLOT_SKIP = 1 << 23
ROW_SKIP = 1 << 21
FAR = 1e30
TINY = 1e-30
GW = GT * D


def after(eng, sem, value):
    if isinstance(value, int) and value <= 0:
        return
    eng.wait_ge(sem, value)


def known(value, at_least, below):
    return not isinstance(value, int) or at_least <= value < below


class Order:

    def __init__(self, eng, sem):
        self.eng, self.sem, self.n = eng, sem, 0

    def did(self, ins):
        ins.then_inc(self.sem, 1)
        self.n += 1

    def wait(self):
        self.eng.wait_ge(self.sem, self.n)

    def do(self, ins):
        self.did(ins)
        self.wait()


def build(nc, x, src, dst, eattr, etype, w1, b1, w2, b2, relw, rw1, rw2, out):
    with ExitStack() as ctx:
        def sb(name, shape, dt=F32):
            return ctx.enter_context(nc.sbuf_tensor(name, shape, dt))

        def sem(name):
            return ctx.enter_context(nc.semaphore(name))

        def sem2(name):
            return [sem(name + "_even"), sem(name + "_odd")]

        def sems(prefix, names):
            return {k: sem(f"{prefix}_{k}") for k in names.split()}

        g0_t = nc.dram_tensor("g0_by_node", (NPAD, D), F32).ap()
        g1_t = nc.dram_tensor("g1_by_node", (NQ * QROWS, D), F32).ap()
        x1_t = nc.dram_tensor("x1_by_node", (NPAD, D), F32).ap()
        h_t = nc.dram_tensor("h_by_node", (NPAD, D), F32).ap()
        a_t = nc.dram_tensor("layer_input_of_destination", (EPAD, D), F32).ap()
        xd_t = nc.dram_tensor("x_of_destination", (EPAD, D), F32).ap()
        g1d_t = nc.dram_tensor("g1_of_destination", (EPAD, D), F32).ap()
        x1d_t = nc.dram_tensor("x1_of_destination", (EPAD, D), F32).ap()
        hd_t = nc.dram_tensor("h_of_destination", (EPAD, D), F32).ap()
        slot_t = nc.dram_tensor("slot_rows", (P * KS, RW), F32).ap()
        edge_t = nc.dram_tensor("edge_rows", (1 + EPAD, MW), F32).ap()

        ident = sb("ident", [P, P])
        upper = sb("upper", [P, P])
        ones = sb("ones", [P, P])
        diag = sb("diag", [P, P])
        first_row = sb("first_row", [P, P])
        carry = sb("carry", [P, P])
        dsti = sb("dsti", [P, KE + 1], I32)
        dsafe = sb("dsafe", [P, KE], I32)
        meta = sb("meta", [P, KE, 2], I32)
        relf = sb("relf", [P, KE])
        key = sb("key", [P, KE + 1])
        same = sb("same", [P, KE + 1])
        head = sb("head", [P, KE])
        outi = sb("outi", [P, KE], I32)
        slot_row = sb("slot_row", [P, KE], I32)
        dinv_e = sb("dinv_e", [P, KE])
        dinv2_e = sb("dinv2_e", [P, KE])
        tmp_a = sb("tmp_a", [P, KE + 1])
        tmp_b = sb("tmp_b", [P, KE + 1])
        tmp_i = sb("tmp_i", [P, KE], I32)
        tmp_j = sb("tmp_j", [P, KE], I32)
        lo_key = sb("lo_key", [P, KE])
        hi_key = sb("hi_key", [P, KE])
        pos = sb("pos", [P, KE])
        onesk = sb("onesk", [P, KE])
        cnt = sb("cnt", [P, 6, R])
        cnti = sb("cnti", [P, 2, R], I32)
        rel_no = sb("rel_no", [P, R])
        tile_no = sb("tile_no", [1, KS])
        tile_reli = sb("tile_reli", [1, KS], I32)
        w1_sb = sb("w1_sb", [P, HID])
        w2_sb = sb("w2_sb", [P, D])
        b1_sb = sb("b1_sb", [P, 1])
        b2_sb = sb("b2_sb", [P, D])
        res_in = sb("res_in", [P, P])
        res_sb = sb("res_sb", [P, P])
        res1_sb = sb("res1_sb", [P, P])
        stat = sb("stat", [P, 2, 6, CB])
        estat = sb("estat", [P, 6, GT])
        rden = sb("rden", [P, 2, GT])
        smax = sb("smax", [P, 2])
        src_idx = sb("src_idx", [P, 2, GT], I32)
        out_idx = sb("out_idx", [P, 2, GT], I32)
        slot_idx = sb("slot_idx", [P, SB, GS], I32)
        slot_e = sb("slot_e", [P, SB, GS])
        fix_i = sb("fix_i", [P, 1], I32)
        fix_s = sb("fix_s", [P, 12])
        hd_i = sb("hd_i", [P, 1], I32)
        last_i = sb("last_i", [P, 1], I32)
        hsum = sb("hsum", [P, MW])
        fix_sum = sb("fix_sum", [P, MW])
        fix_x = sb("fix_x", [P, D])
        fix_c = sb("fix_c", [P, D])
        fix_q = sb("fix_q", [P, D])
        fix_g1 = sb("fix_g1", [P, D])
        fix_x1 = sb("fix_x1", [P, D])
        fix_h = sb("fix_h", [P, D])
        fix_two = sb("fix_two", [P, P])
        fix_t = sb("fix_t", [P, P])
        fix_hid = sb("fix_hid", [P, P])
        fix_low = sb("fix_low", [P, P])
        fix_out = sb("fix_out", [P, D])
        h_last = sb("h_last", [P, D])
        gbuf = sb("gbuf", [P, 2 * GT * MW])
        rbuf = sb("rbuf", [P, 2 * GT * MW])
        ebuf = sb("ebuf", [P, 9 * GW])
        chain = sb("chain", [P, 6 * MM])
        halves = sb("halves", [P, 2, 4, D])
        arena = sb("arena", [P, KE * MW])
        banks = ctx.enter_context(nc.psum_tensor("banks", [P, 8, MM], F32))

        def part(buffer, at, shape, dt=F32):
            n = 1
            for k in shape:
                n *= k
            words = buffer[:, at:at + (n + 1) // 2] if dt == F16 else buffer[:, at:at + n]
            words = words if dt == F32 else words.bitcast(dt)
            if len(shape) == 1:
                return words
            if len(shape) == 2:
                return words.rearrange("p (a b) -> p a b", b=shape[1])
            return words.rearrange("p (a b c) -> p a b c", b=shape[1], c=shape[2])

        iota_h = part(arena, 8 * BW, [KN], F16)
        lo_hot = part(arena, 8 * BW + KN // 2, [4, P], F16)
        hi_hot = part(arena, 8 * BW + KN // 2 + 2 * P, [4, KN], F16)
        degs = part(arena, 8 * BW + KN // 2 + 2 * P + 2 * KN, [2, KN])
        ZW = KS * RW // 16
        zero = part(arena, 10 * BW, [ZW])
        iota_i = part(arena, 10 * BW + ZW, [KN], I32)
        eidi = part(arena, 10 * BW + ZW + KN, [KE], I32)
        rows_e = part(rbuf, 0, [2, GT, MW])
        rows_g = part(gbuf, 0, [2, GT, MW])
        perm_rows = part(arena, 0, [2, GT, RW])
        slot_w = part(arena, 2 * GT * RW, [SB, GS, WW])
        srci = part(ebuf, 3 * GW, [KE], I32)
        dinv = part(ebuf, 2 * GW, [KN])
        rel_sb = part(arena, 2 * GT * RW + SB * GS * WW, [R, P])
        tile_rel = part(ebuf, 3 * GW, [2, KS])
        slot_ht = part(ebuf, 0, [2, GS, P])
        slot_z = part(ebuf, 2 * GS * P, [2, GS, D])
        slot_th = part(ebuf, 3 * GS * P, [2, GS, D])
        slot_q = part(ebuf, 4 * GS * P, [2, GS, D])
        diag_max = part(chain, 0, [2, P])
        seen = part(chain, 2 * P, [2 * P])

        def quad_buffer(k):
            return part(arena, 8 * BW + k * MM, [MM])

        def slot(k):
            return arena[:, k * BW:(k + 1) * BW]

        def eslot(k, n=1):
            return ebuf[:, k * GW:(k + n) * GW]

        def cols(ap):
            return ap.rearrange("p (c f) -> p c f", f=D)

        def bank(k, n=1):
            return banks[:, k:k + n, :].rearrange("p a b -> p (a b)")

        def wide(ap, c, f=D):
            return ap.unsqueeze(2).to_broadcast([P, c, f])

        def b2_over(c):
            return b2_sb[:].unsqueeze(1).to_broadcast([P, c, D])

        filled, loaded, consts = sem("filled"), sem("inputs_loaded"), sem("pool_constants")
        prep, prep_pe, prep_act = sem("prep_steps"), sem("prep_products"), sem("prep_roots")
        zeroed, cleared = sem("zeros_stored"), sem("sums_cleared")
        waits_over = {e: sem("waits_over_" + e) for e in ("pool", "sp", "dve")}
        x_idx, x_got, x_kept = sem("xd_idx"), sem2("xd_here"), sem2("xd_stored")
        hot_made, hot_used, deg_read = sem("one_hots_made"), sem("one_hots_used"), sem("degree_read")
        deg_root, out_idx_ready = sem("degree_root"), sem("out_idx_ready")
        A = sems("a", "rows centered square std g")
        a_in, a_g0 = sem2("a_x_loaded"), sem2("a_g0_stored")
        Q = sems("quad", "turned at h relu u g1 x1")
        q_g0, q_x, q_g1, q_x1 = (sem2("quad_" + k) for k in ("g0_loaded", "x_loaded", "g1_stored", "x1_stored"))
        B = sems("b", "rows centered square std h turned t o low leaky out")
        b_in, b_h, b_out = sem2("b_x1_loaded"), sem2("b_h_stored"), sem2("b_out_stored")
        e1 = sems("e1", "rows centered square std run head a turned at h relu u g1")
        e1_src = sem("e1_src_idx")
        e1_in, e1_got, e1_sent, e1_kept = (sem2("e1_" + k) for k in ("loaded", "rows_here", "rows_sent", "stored"))
        e2 = sems("e2", "run head rows centered square std h")
        e2_src = sem("e2_src_idx")
        e2_in, e2_got, e2_sent, e2_kept = (sem2("e2_" + k) for k in ("loaded", "rows_here", "rows_sent", "stored"))
        sort = sem("sort_steps")
        c = sems("perm", "tmp hf")
        c_meta = sem("perm_meta")
        c_ef, c_hd, c_sent = (sem2("perm_" + k) for k in ("features", "hd_loaded", "sent"))
        rel = sems("rel", "idx turned ht tr z th q att")
        rel_in, rel_got, rel_sent = ([sem(f"rel_{k}_{n}") for n in range(SB)] for k in ("loaded", "rows_here", "sent"))
        edges_in, soft, soft_pe, soft_exp = sem("edges_loaded"), sem("softmax_steps"), sem("softmax_rows"), sem("weights_ready")
        f = sems("f", "weighted run head rows two turned t o low leaky half out")
        f_in, f_sent = sem2("f_loaded"), sem2("f_sent")
        fix_in = sem("fix_loaded")
        fix = sems("fix", "ve act pe sent")
        for s, steps, first in ((A, 6, 0), (B, 5, 0), (e1, 8, 0), (e2, 9, 4)):
            s["steps"], s["first"] = steps, first
        at_step = {}
        ALL = 16 * GT * (GE // 2)
        ALL_QUADS = 16 * (NQ // 2)
        STORES = [16 * (NB // 2 + 1), 16 * (NB // 2)]
        FIX_1_STEPS = 13
        N_LOADS = 9 + 3 + 9

        block = ctx.enter_context(nc.Block())

        def row_steps(s, n, k):
            return s["steps"] * n + s["first"] + k

        def over_groups(eng, step):
            step(0, 0, 0)
            step(1, 1, 0)
            with eng.Fori(1, GE // 2) as i:
                step(2 * i, 0, i)
                step(2 * i + 1, 1, i)

        def over_quads(eng, step):
            first = Q_A + 2 * GE
            with eng.Fori(first // 2, NQ // 2 - 1) as i:
                step(2 * i, 0, i)
                step(2 * i + 1, 1, i)
            for n in range(NQ - 2, NQ):
                step(n, n % 2, n // 2)

        def over_both(eng, step):
            step(0, 0, 0)
            step(1, 1, 0)
            with eng.Fori(1, NB // 2) as i:
                step(2 * i, 0, i)
                step(2 * i + 1, 1, i)
            for g in range(NB - 1, GE):
                step(g, g % 2, g // 2)

        def over_slots(step, eng):
            for j in range(SB):
                step(j, j, j % 2, 0)
            with eng.Fori(1, NGS // SB) as i:
                for s in range(SB):
                    step(SB * i + s, s, s % 2, i)
            for j in range(NGS // SB * SB, NGS):
                step(j, j % SB, j % 2, j // SB)

        def over_perm(eng, step):
            whole = ETAIL // GT
            s0 = GE - 1 - whole
            assert s0 % 2 == 0
            step(0, 0, 0, "none")
            step(1, 1, 0, "none")
            with eng.Fori(1, s0 // 2) as i:
                step(2 * i, 0, i, "none")
                step(2 * i + 1, 1, i, "none")
            step(s0, 0, s0 // 2, "part")
            step(s0 + 1, 1, s0 // 2, "whole")
            with eng.Fori(s0 // 2 + 1, GE // 2) as i:
                step(2 * i, 0, i, "whole")
                step(2 * i + 1, 1, i, "whole")

        def features_in(u, kind):
            u0 = (GE - 1 - ETAIL // GT) // 2
            return 32 * (u + 1) if kind == "none" else 32 * u0 + 48 * (u + 1 - u0)

        def group(table, g):
            return table.rearrange("(p t) f -> p (t f)", p=P)[:, bass.ds(g * GW, GW)]

        def rows(table, b, parts=P, first=0):
            if isinstance(b, int):
                at = b * BROWS + first * CB
                return table[at:at + parts * CB, :].rearrange("(p c) f -> p (c f)", c=CB)
            return table[bass.ds(b * BROWS, BROWS), :].rearrange("(p c) f -> p (c f)", c=CB)

        def quad_rows(table, n):
            return table[bass.ds(n * QROWS, QROWS), :].rearrange("(p c) f -> p (c f)", c=CQ)

        def move_block(eng, dram, here, b, signal, store):
            parts = [(0, P)]
            if isinstance(b, int) and b == NB - 1 and dram.shape[0] == N:
                parts = [(0, TAIL_SPLIT), (TAIL_SPLIT, TAIL_P)]
            for lo, hi in parts:
                there, mine = rows(dram, b, hi - lo, lo), here[lo:hi, :]
                eng.dma_start(there if store else mine, mine if store else there).then_inc(signal, 16)

        def all_landed(eng, signals, counts):
            for q in range(2):
                eng.wait_ge(signals[q], counts[q] if isinstance(counts, list) else counts)

        @block.sync
        def _(sp):
            count = [0]

            def load(to, of):
                sp.dma_start(to, of).then_inc(loaded, 16)
                count[0] += 1

            def load_edges(tile, vec):
                full = vec[0:EFULL * KE].rearrange("(p t) -> p t", t=KE)
                load(tile[0:ESPLIT, 0:KE], full[0:ESPLIT, :])
                load(tile[ESPLIT:EFULL, 0:KE], full[ESPLIT:EFULL, :])
                load(tile[EFULL:P, 0:ETAIL], vec[EFULL * KE:E].unsqueeze(0))

            sp.wait_ge(filled, 1)
            load_edges(dsti, dst)
            load_edges(tmp_j, etype)
            load_edges(srci, src)
            ctx.enter_context(nc.allow_non_contiguous_dma(reason="one number in each partition"))
            later = dst[KE:EFULL * KE].rearrange("(p t) -> p t", t=KE)
            load(dsti[0:ESPLIT, KE:KE + 1], later[0:ESPLIT, 0:1])
            load(dsti[ESPLIT:EFULL - 1, KE:KE + 1], later[ESPLIT:EFULL - 1, 0:1])
            load(dsti[EFULL - 1:EFULL, KE:KE + 1], dst[EFULL * KE:EFULL * KE + 1].unsqueeze(0))
            load(w1_sb[0:D, :], w1)
            load(w1_sb[D:P, :], w1)
            load(w2_sb[:], w2)
            load(b1_sb[:], b1.unsqueeze(1))
            load(b2_sb[:], b2.partition_broadcast(P))
            load(res_in[0:D, 0:D], rw1)
            load(res_in[D:P, D:P], rw2)
            load(fix_two[0:D, 0:D], rw1)
            load(fix_two[D:P, D:P], rw1)
            assert count[0] == N_LOADS, count[0]
            lanes = slot_t.rearrange("(l s) w -> l (s w)", l=P)
            for k in range(16):
                sp.dma_start(lanes[:, k * ZW:(k + 1) * ZW], zero).then_inc(zeroed, 16)
            pads = edge_t[E + 1:EPAD + 1, :].rearrange("(l s) w -> l (s w)", s=2)
            sp.dma_start(pads, zero[0:(EPAD - E) // 2, 0:2 * MW]).then_inc(zeroed, 16)
            rest = x1_t[NQ * QROWS:NPAD, :].rearrange("(p c) f -> p (c f)", p=P)
            sp.dma_start(rest, zero[:, 0:(NPAD - NQ * QROWS) // P * D]).then_inc(zeroed, 16)
            sp.wait_ge(zeroed, 16 * 18)

            def load_a(b, q):
                after(sp, A["centered"], b - 1)
                move_block(sp, x, slot(q), b, a_in[q], store=False)

            def load_g0(n, q):
                after(sp, Q["turned"], n - 1)
                sp.dma_start(quad_buffer(q), quad_rows(g0_t, n)).then_inc(q_g0[q], 16)

            def keep_quad(n, q):
                sp.wait_ge(Q["x1"], 2 * (n + 1))
                sp.dma_start(quad_rows(g1_t, n), quad_buffer(2 + q)).then_inc(q_g1[q], 16)
                sp.dma_start(quad_rows(x1_t, n), quad_buffer(6 + q)).then_inc(q_x1[q], 16)

            def quad(n, q):
                if known(n, 2, NQ):
                    keep_quad(n - 2, q)
                if isinstance(n, int) and n == NQ - 1:
                    for lo, hi in ((0, Q_TAIL_P // 16 * 16), (Q_TAIL_P // 16 * 16, Q_TAIL_P)):
                        at = n * QROWS
                        sp.dma_start(quad_buffer(4 + q)[lo:hi, :], x[at + lo * CQ:at + hi * CQ, :].rearrange(
                            "(p c) f -> p (c f)", c=CQ)).then_inc(q_x[q], 16)
                else:
                    sp.dma_start(quad_buffer(4 + q), quad_rows(x, n)).then_inc(q_x[q], 16)

            def step_a(b, q, u):
                if known(b, 1, NB):
                    if isinstance(b, int) and b == 1:
                        sp.wait_ge(a_g0[0], 16)
                        load_g0(0, 0)
                        load_g0(1, 1)
                    else:
                        sp.wait_ge(a_g0[q], 16 * u)
                        sp.sem_inc(waits_over["sp"], 1)
                    load_g0(b + 1, 1 - q)
                if known(b, 0, NB - 1):
                    load_a(b + 1, 1 - q)
                sp.wait_ge(A["g"], b + 1)
                move_block(sp, g0_t, slot(6 + q), b, a_g0[q], store=True)
                if known(b, 1, NB):
                    quad(b - 1, 1 - q)

            load_a(0, 0)
            for b in range(4):
                step_a(b, b % 2, b // 2)
            with sp.Fori(2, NB // 2 - 1) as i:
                step_a(2 * i, 0, i)
                step_a(2 * i + 1, 1, i)
            for b in range(NB - 3, NB):
                step_a(b, b % 2, b // 2)
            all_landed(sp, a_g0, STORES)
            all_landed(sp, x_kept, 16 * (GE // 2))

            def load_e1(g, q):
                after(sp, e1["centered"], g - 1)
                sp.dma_start(eslot(q), group(xd_t, g)).then_inc(e1_in[q], 16)

            def step_e1(g, q, u):
                n = Q_A + 2 * g
                load_g0(n + 2, 0)
                if known(g, 0, GE - 1):
                    load_e1(g + 1, 1 - q)
                quad(n, 0)
                load_g0(n + 3, 1)
                sp.wait_ge(e1["a"], g + 1)
                sp.dma_start(group(a_t, g), eslot(5 + q)).then_inc(e1_kept[q], 16)
                quad(n + 1, 1)

            load_e1(0, 0)
            sp.dma_start(fix_x[:], xd_t.rearrange("(p t) f -> p (t f)", p=P)[:, 0:D]).then_inc(fix_in, 16)
            step_e1(0, 0, 0)
            step_e1(1, 1, 0)
            with sp.Fori(1, GE // 2 - 1) as i:
                step_e1(2 * i, 0, i)
                step_e1(2 * i + 1, 1, i)
            step_e1(GE - 2, 0, GE // 2 - 1)
            step_e1(GE - 1, 1, GE // 2 - 1)

            def step_quad(n, q, u):
                if known(n, 0, NQ - 2):
                    load_g0(n + 2, q)
                quad(n, q)

            over_quads(sp, step_quad)
            keep_quad(NQ - 2, 0)
            keep_quad(NQ - 1, 1)
            all_landed(sp, q_x1, ALL_QUADS)
            all_landed(sp, e1_kept, 16 * (GE // 2))

            def load_a_rows(g, q):
                after(sp, e1["turned"], 2 * (g - 1))
                sp.dma_start(eslot(5 + q), group(a_t, g)).then_inc(e1_in[q], 16)

            def load_b(b, q):
                after(sp, B["out"], 4 * (b - 1))
                move_block(sp, x1_t, slot(q), b, b_in[q], store=False)

            def keep_g1(g, q):
                sp.wait_ge(e1["g1"], 2 * (g + 1))
                sp.dma_start(group(g1d_t, g), eslot(7 + q)).then_inc(e1_kept[q], 16)

            def step_b(g, q, u):
                if known(g, 0, GE - 1):
                    load_a_rows(g + 1, 1 - q)
                if known(g, 1, GE):
                    keep_g1(g - 1, 1 - q)
                if known(g, 0, NB):
                    sp.wait_ge(B["h"], g + 1)
                    move_block(sp, h_t, slot(6 + q), g, b_h[q], store=True)
                if known(g, 0, NB - 1):
                    load_b(g + 1, 1 - q)
                if known(g, 1, NB + 1):
                    sp.wait_ge(B["out"], 4 * g)
                    move_block(sp, out, slot(9 - q), g - 1, b_out[1 - q], store=True)

            load_a_rows(0, 0)
            load_b(0, 0)
            over_both(sp, step_b)
            keep_g1(GE - 1, 1)
            all_landed(sp, e1_kept, 32 * (GE // 2))

            sp.wait_ge(fix["ve"], FIX_1_STEPS)

            sp.wait_ge(cleared, 3)
            sp.dma_start(rel_sb[0:D, :, 0:D], relw.rearrange("r d e -> d r e")).then_inc(loaded, 16)
            sp.dma_start(rel_sb[D:P, :, D:P], relw.rearrange("r d e -> d r e")).then_inc(loaded, 16)

            def load_e2(g, q):
                after(sp, e2["h"], g - 1)
                sp.dma_start(eslot(q), group(xd_t, g)).then_inc(e2_in[q], 16)
                sp.dma_start(eslot(2 + q), group(g1d_t, g)).then_inc(e2_in[q], 16)

            def step_e2(g, q, u):
                if known(g, 0, GE - 1):
                    load_e2(g + 1, 1 - q)
                sp.wait_ge(e2["h"], g + 1)
                sp.dma_start(group(x1d_t, g), eslot(4 + q)).then_inc(e2_kept[q], 16)
                sp.dma_start(group(hd_t, g), eslot(6 + q)).then_inc(e2_kept[q], 16)

            load_e2(0, 0)
            step_e2(0, 0, 0)
            step_e2(1, 1, 0)
            with sp.Fori(1, GE // 2 - 1) as i:
                step_e2(2 * i, 0, i)
                step_e2(2 * i + 1, 1, i)
            step_e2(GE - 2, 0, GE // 2 - 1)
            step_e2(GE - 1, 1, GE // 2 - 1)
            all_landed(sp, e2_kept, 32 * (GE // 2))

            sp.wait_ge(fix["sent"], 48)

            by_edge = eattr[0:EFULL * KE, :].rearrange("(p t) f -> p t f", t=KE)

            def load_perm(s, q, u, kind):
                g = GE - 1 - s
                after(sp, c["tmp"], s - 1)
                sp.sem_inc(waits_over["sp"], 1)
                sp.dma_start(eslot(q), group(hd_t, g)).then_inc(c_hd[q], 16)
                after(sp, c_sent[q], 16 * GT * u)
                for lo, hi in ((0, ESPLIT), (ESPLIT, EFULL)):
                    sp.dma_start(perm_rows[lo:hi, q, :, 0:D], by_edge[lo:hi, bass.ds(g * GT, GT), :]).then_inc(c_ef[q], 16)
                if kind == "whole":
                    sp.dma_start(perm_rows[EFULL:P, q, :, 0:D],
                                 eattr[bass.ds(g * GT + EFULL * KE, GT), :].unsqueeze(0)).then_inc(c_ef[q], 16)
                if kind == "part":
                    left = ETAIL % GT
                    sp.dma_start(perm_rows[EFULL:P, q, 0:left, 0:D], eattr[E - left:E, :].unsqueeze(0)).then_inc(c_ef[q], 16)

            over_perm(sp, load_perm)
            all_landed(sp, c_sent, ALL)

            def load_slots(j, s, q, u):
                after(sp, rel_sent[s], 16 * GS * u)
                by_lane = slot_t.rearrange("(l s) w -> l s w", l=P)
                sp.dma_start(slot_w[:, s, :, 0:RW], by_lane[:, bass.ds(j * GS, GS), :]).then_inc(rel_in[s], 16)

            over_slots(load_slots, sp)

            for s in range(SB):
                sp.wait_ge(rel_sent[s], 16 * GS * ((NGS - s + SB - 1) // SB))
            all_landed(sp, b_out, [STORES[0] + 16, STORES[1]])
            edge_view = edge_t[1:EPAD + 1, :].rearrange("(p t) w -> p (t w)", p=P)
            half = KE // 2 * MW
            for k in range(2):
                sp.dma_start(arena[:, k * half:(k + 1) * half],
                             edge_view[:, k * half:(k + 1) * half]).then_inc(edges_in, 16)

            def load_f(g, q, u):
                after(sp, f["out"], 4 * (g - 1))
                sp.dma_start(eslot(q), group(hd_t, g)).then_inc(f_in[q], 16)
                sp.dma_start(eslot(2 + q), group(x1d_t, g)).then_inc(f_in[q], 16)

            over_groups(sp, load_f)

        @block.vector
        def _(dve):
            v = nc.vector
            tt, ts, stt = v.tensor_tensor, v.tensor_scalar, v.scalar_tensor_tensor

            def link(ins, signal, n):
                ins.then_inc(signal, 1)
                dve.wait_ge(signal, n)

            o = Order(dve, prep)
            o.did(v.memset(dsti[:], KEY_PAD))
            o.did(v.memset(srci, 0))
            o.did(v.memset(tmp_j[:], R))
            o.did(v.memset(ones[:], 1.0))
            o.did(v.memset(zero, 0.0))
            o.did(v.memset(res_in[:], 0.0))
            o.did(v.memset(fix_two[:], 0.0))
            o.wait()
            v.memset(tmp_b[:], 0.0).then_inc(filled, 1)
            o.did(v.memset(onesk[:], 1.0))
            o.did(v.memset(same[:], 0.0))
            dve.wait_ge(loaded, 16 * N_LOADS)
            dve.wait_ge(consts, 4)
            o.do(v.tensor_copy(key[:], dsti[:]))
            o.do(ts(dsafe[:], key[:, 0:KE], float(N - 1), None, ALU.min))
            at_step["safe destinations"] = o.n
            o.did(ts(tmp_i[:], dsti[:, 0:KE], 5, P - 1, ALU.logical_shift_right, ALU.bitwise_and))
            o.did(ts(outi[:], dsti[:, 0:KE], CB - 1, None, ALU.bitwise_and))
            o.did(ts(slot_row[:], dsti[:, 0:KE], 12, None, ALU.logical_shift_right))
            o.did(v.tensor_copy(iota_h, iota_i))
            o.did(v.tensor_copy(relf[:], tmp_j[:]))
            o.did(v.tensor_copy(rel_no[:], iota_i[:, 0:R]))
            o.did(v.tensor_copy(tile_no[:], iota_i[0:1, 0:KS]))
            o.did(v.tensor_copy(meta[:, :, 0], srci))
            o.did(v.tensor_copy(meta[:, :, 1], eidi))
            o.wait()
            o.did(v.tensor_copy(lo_key[:], tmp_i[:]))
            o.do(stt(out=hi_key[:], in0=slot_row[:], scalar=float(CB), in1=outi[:], op0=ALU.mult, op1=ALU.add))

            def hot(t, k):
                after(dve, hot_used, t - 3)
                ts(lo_hot[:, k % 4, :], iota_h[:, 0:P], lo_key[:, bass.ds(t, 1)], None,
                   ALU.is_equal).then_inc(hot_made, 1)
                ts(hi_hot[:, k % 4, :], iota_h, hi_key[:, bass.ds(t, 1)], None,
                   ALU.is_equal).then_inc(hot_made, 1)

            for k in range(8):
                hot(k, k)
            with dve.Fori(1, KE // 8) as i:
                for k in range(8):
                    hot(8 * i + k, k)
            dve.wait_ge(hot_used, KE)
            ts(degs[:, 0, :].rearrange("p (a c) -> p a c", a=2), banks[:, 0:2, 0:KN // 2], 1.0, None,
               ALU.add).then_inc(deg_read, 1)
            dve.wait_ge(deg_root, 1)
            o.do(v.reciprocal(dinv, degs[:, 1, :]))

            o.did(tt(same[:, 1:KE], key[:, 1:KE], key[:, 0:KE - 1], ALU.is_equal))
            o.did(ts(head[:], key[:, 0:KE], key[:, 0:1], None, ALU.is_equal))
            o.did(tt(tmp_a[:, 0:KE], key[:, 1:KE + 1], key[:, 0:KE], ALU.is_equal))
            o.did(ts(diag[:], ident[:], key[:, 0:1], None, ALU.mult))
            at_step["first keys"] = o.n
            o.wait()
            o.do(tt(tmp_b[:, 0:KE], tmp_a[:, 0:KE], head[:], ALU.max))
            o.did(stt(out=outi[:], in0=tmp_b[:, 0:KE], scalar=float(SKIP), in1=key[:, 0:KE], op0=ALU.mult, op1=ALU.add))
            o.do(tt(fix_s[:, 0:1], key[:, KE:KE + 1], key[:, 0:1], ALU.is_equal))
            o.did(stt(out=fix_i[:], in0=fix_s[:, 0:1], scalar=float(SKIP), in1=key[:, 0:1], op0=ALU.mult, op1=ALU.add))
            o.did(ts(last_i[:], key[:, KE - 1:KE], float(N - 1), None, ALU.min))
            o.do(v.tensor_tensor_scan(out=tmp_a[:, 0:KE], data0=same[:, 0:KE], data1=onesk[:], initial=0.0,
                                      op0=ALU.mult, op1=ALU.add))
            o.do(v.tensor_copy(fix_s[:, 2:3], tmp_a[:, KE - 1:KE]))
            o.do(ts(tmp_a[:, 0:KE], tmp_a[:, 0:KE], 1.0, None, ALU.add))
            at_step["edge degrees"] = o.n
            o.do(v.tensor_reduce(fix_s[:, 3:4], head[:], AX.X, ALU.add))
            o.did(stt(out=hd_i[:], in0=fix_s[:, 3:4], scalar=-2.0, in1=meta[:, 0:1, 1], op0=ALU.add, op1=ALU.add))
            dve.wait_ge(prep_pe, 1)
            o.did(v.tensor_copy(first_row[:], bank(0)[:, 0:P]))
            o.did(v.tensor_copy(res_sb[:], bank(0)[:, P:2 * P]))
            o.did(v.tensor_copy(res1_sb[:], bank(0)[:, 2 * P:3 * P]))
            o.wait()
            o.do(stt(out=carry[:], in0=first_row[:], scalar=key[:, KE - 1:KE], in1=upper[:], op0=ALU.is_equal, op1=ALU.mult))
            at_step["carry"] = o.n
            dve.wait_ge(prep_act, 1)
            o.do(v.reciprocal(dinv_e[:], tmp_b[:, 0:KE]))
            o.do(tt(dinv2_e[:], dinv_e[:], dinv_e[:], ALU.mult))
            dve.wait_ge(prep_pe, 2)
            o.do(tt(fix_s[:, 4:5], bank(0)[:, 0:1], fix_s[:, 3:4], ALU.add))
            o.do(ts(fix_s[:, 5:6], fix_s[:, 4:5], 1.0, None, ALU.add))
            at_step["fix degrees"] = o.n
            dve.wait_ge(prep_act, 2)
            o.do(v.reciprocal(fix_s[:, 7:8], fix_s[:, 6:7]))

            def centre(s, n, st, c, xin, xc):
                link(v.tensor_reduce(st[:, 0, :], cols(xin), AX.X, ALU.add), s["rows"], row_steps(s, n, 1))
                link(ts(st[:, 1, :], st[:, 0, :], 1.0 / D, None, ALU.mult), s["rows"], row_steps(s, n, 2))
                tt(cols(xc), cols(xin), wide(st[:, 1, :], c), ALU.subtract).then_inc(s["centered"], 1)

            def deviation(s, n, st, sq):
                dve.wait_ge(s["square"], n + 1)
                link(v.tensor_reduce(st[:, 5, :], cols(sq), AX.X, ALU.add), s["rows"], row_steps(s, n, 3))
                ts(st[:, 2, :], st[:, 5, :], 1.0 / D, EPS, ALU.mult, ALU.add).then_inc(s["rows"], 1)
                dve.wait_ge(s["std"], n + 1)
                link(v.reciprocal(st[:, 4, :], st[:, 3, :]), s["rows"], row_steps(s, n, 5))

            def relu_times(to, xc, factor, c):
                return stt(out=cols(to), in0=cols(xc), scalar=0.0, in1=wide(factor, c), op0=ALU.max, op1=ALU.mult)

            def quad(n, q, u):
                dve.wait_ge(Q["g1"], n + 1)
                dve.wait_ge(q_x[q], 16 * (u + 1) + (16 if isinstance(n, int) and n == NQ - 1 else 0))
                after(dve, q_x1[q], 16 * u)
                link(tt(quad_buffer(6 + q), quad_buffer(2 + q), quad_buffer(4 + q), ALU.add), Q["x1"], 2 * n + 1)
                tt(cols(quad_buffer(6 + q)), cols(quad_buffer(6 + q)), b2_over(CQ), ALU.add).then_inc(Q["x1"], 1)

            def step_a(b, q, u):
                st = stat[:, q]
                dve.wait_ge(a_in[q], 16 * (u + 1) + (16 if isinstance(b, int) and b == NB - 1 else 0))
                centre(A, b, st, CB, slot(q), slot(2 + q))
                if known(b, 3, NB):
                    quad(b - 3, 1 - q, u - (2 - q))
                deviation(A, b, st, slot(4 + q))
                link(tt(st[:, 5, :], st[:, 4, :], dinv[:, bass.ds(b * CB, CB)], ALU.mult), A["rows"], row_steps(A, b, 6))
                after(dve, a_g0[q], 16 * u)
                relu_times(slot(6 + q), slot(2 + q), st[:, 5, :], CB).then_inc(A["g"], 1)

            for b in range(6):
                step_a(b, b % 2, b // 2)
            with dve.Fori(3, NB // 2) as i:
                step_a(2 * i, 0, i)
                step_a(2 * i + 1, 1, i)
            step_a(NB - 1, 0, NB // 2)

            def sum_group(s, g, q, width):
                for k in range(GT):
                    t = g * GT + k
                    former = rows_e[:, q, k - 1, 0:width] if k else rows_e[:, 1 - q, GT - 1, 0:width]
                    after(dve, s["run"], t)
                    stt(out=rows_e[:, q, k, 0:width], in0=former, scalar=same[:, bass.ds(t, 1)],
                        in1=rows_g[:, q, k, 0:width], op0=ALU.mult, op1=ALU.add).then_inc(s["run"], 1)
                    after(dve, s["head"], t)
                    stt(out=hsum[:, 0:width], in0=rows_g[:, q, k, 0:width], scalar=head[:, bass.ds(t, 1)],
                        in1=hsum[:, 0:width], op0=ALU.mult, op1=ALU.add).then_inc(s["head"], 1)

            def clear(n):
                v.memset(rows_e[:, 1, GT - 1, :], 0.0).then_inc(cleared, 1)
                v.memset(hsum[:], 0.0).then_inc(cleared, 1)
                dve.wait_ge(cleared, n)

            clear(2)

            def step_e1(g, q, u):
                n = Q_A + 2 * g
                dve.wait_ge(e1_in[q], 16 * (u + 1))
                centre(e1, g, estat[:], GT, eslot(q), eslot(2))
                quad(n - 2, 0, Q_A // 2 + g - 1)
                deviation(e1, g, estat[:], eslot(3))
                link(tt(estat[:, 5, :], estat[:, 4, :], dinv2_e[:, bass.ds(g * GT, GT)], ALU.mult), e1["rows"], row_steps(e1, g, 6))
                relu_times(eslot(4), eslot(2), estat[:, 5, :], GT).then_inc(e1["rows"], 1)
                dve.wait_ge(e1_got[q], 16 * GT * (u + 1))
                sum_group(e1, g, q, D)
                dve.wait_ge(e1["rows"], row_steps(e1, g, 7))
                dve.wait_ge(e1["run"], GT * (g + 1))
                after(dve, e1_kept[q], 16 * u)
                link(tt(cols(eslot(5 + q)), rows_e[:, q, :, 0:D], wide(dinv_e[:, bass.ds(g * GT, GT)], GT), ALU.mult),
                     e1["rows"], row_steps(e1, g, 8))
                tt(eslot(5 + q), eslot(5 + q), eslot(4), ALU.add).then_inc(e1["a"], 1)
                quad(n - 1, 1, Q_A // 2 + g - 1)

            over_groups(dve, step_e1)

            o = Order(dve, sort)
            o.do(ts(pos[:], relf[:], float(R), float(SLOT_SKIP), ALU.is_equal, ALU.mult))
            for r in range(R):
                o.do(ts(tmp_a[:, 0:KE], relf[:], float(r), None, ALU.is_equal, ALU.add, accum_out=cnt[:, 0, r:r + 1]))
            at_step["counts"] = o.n
            over_quads(dve, lambda n, q, u: quad(n - 2, q, u - 1))
            quad(NQ - 2, 0, NQ // 2 - 1)
            quad(NQ - 1, 1, NQ // 2 - 1)

            dve.wait_ge(prep_pe, 3)
            totals, before = bank(1)[:, 0:R], bank(1)[:, R:2 * R]
            o.do(v.tensor_copy(cnti[:, 0, :], totals))
            o.do(ts(cnti[:, 1, :], cnti[:, 0, :], P - 1, None, ALU.add))
            o.do(ts(cnti[:, 0, :], cnti[:, 1, :], 7, None, ALU.logical_shift_right))
            o.do(v.tensor_copy(cnt[:, 1, :], cnti[:, 0, :]))
            o.do(v.tensor_tensor_scan(out=cnt[:, 2, :], data0=onesk[:, 0:R], data1=cnt[:, 1, :],
                                      initial=0.0, op0=ALU.mult, op1=ALU.add))
            o.do(tt(cnt[:, 3, :], cnt[:, 2, :], cnt[:, 1, :], ALU.subtract))
            at_step["totals read"] = o.n + 1
            o.do(stt(out=cnt[:, 5, :], in0=cnt[:, 3, :], scalar=float(P), in1=before, op0=ALU.mult, op1=ALU.add))
            o.do(ts(cnt[:, 4, :], cnt[:, 5, :], -1.0, None, ALU.add))

            def place(r, done):
                dve.wait_ge(sort, done)
                link(ts(tmp_b[:, 0:KE], relf[:], rel_no[:, bass.ds(r, 1)], None, ALU.is_equal), sort, done + 1)
                link(v.tensor_tensor_scan(out=tmp_a[:, 0:KE], data0=onesk[:], data1=tmp_b[:, 0:KE],
                                          initial=cnt[:, 4, bass.ds(r, 1)], op0=ALU.mult, op1=ALU.add), sort, done + 2)
                link(tt(tmp_a[:, 0:KE], tmp_a[:, 0:KE], tmp_b[:, 0:KE], ALU.mult), sort, done + 3)
                tt(pos[:], pos[:], tmp_a[:, 0:KE], ALU.add).then_inc(sort, 1)

            for r in range(GE, R):
                place(r, o.n)
                o.n += 4
            placed = o.n

            def e1_keep(g, q, u, c):
                n, w = 2 * g + c, 8 - 2 * c
                dve.wait_ge(e1["u"], n + 1)
                if c == 0:
                    after(dve, e1_sent[q], 16 * GT * u)
                    after(dve, e1_kept[q], 16 * (GE // 2 + u))
                tt(cols(eslot(7 + q))[:, 8 * c:8 * c + w, :], cols(bank(6 + c)[:, 0:w * D]),
                   wide(dinv_e[:, bass.ds(g * GT + 8 * c, w)], w), ALU.mult).then_inc(e1["g1"], 1)

            def quad_b(b, q, u, z):
                n = 4 * b + z
                at = slice(8 * z, 8 * z + 8)
                low, leaky = part(arena, 10 * BW + (2 + z % 2) * MM, [MM]), part(arena, 11 * BW + z % 2 * MM, [MM])
                dve.wait_ge(B["low"], n + 1)
                if z == 0:
                    after(dve, b_out[q], 16 * u)
                link(tt(leaky, bank(4 + z % 2), low, ALU.max), B["leaky"], n + 1)
                tt(cols(slot(8 + q))[:, at, :], cols(leaky), cols(slot(q))[:, at, :], ALU.add).then_inc(B["out"], 1)

            def step_b(g, q, u):
                st = stat[:, q]
                before = (g - 1, 1 - q, u - (1 - q))
                if known(g, 0, NB):
                    dve.wait_ge(b_in[q], 16 * (u + 1))
                    centre(B, g, st, CB, slot(q), slot(2 + q))
                if known(g, 1, NB + 1):
                    quad_b(*before, 0)
                if known(g, 1, GE):
                    e1_keep(*before, 1)
                if known(g, 1, NB + 1):
                    quad_b(*before, 1)
                if known(g, 0, NB):
                    deviation(B, g, st, slot(4 + q))
                    after(dve, b_h[q], 16 * u)
                    relu_times(slot(6 + q), slot(2 + q), st[:, 4, :], CB).then_inc(B["h"], 1)
                if known(g, 1, NB + 1):
                    quad_b(*before, 2)
                e1_keep(g, q, u, 0)
                if known(g, 1, NB + 1):
                    quad_b(*before, 3)

            over_both(dve, step_b)
            e1_keep(GE - 1, 1, GE // 2 - 1, 1)
            dve.wait_ge(B["square"], NB)
            v.memset(rel_sb, 0.0).then_inc(cleared, 1)
            fo = Order(dve, fix["ve"])

            def fix_norm(n, xin):
                fo.do(v.tensor_reduce(fix_s[:, 8:9], xin[:], AX.X, ALU.add))
                fo.do(ts(fix_s[:, 9:10], fix_s[:, 8:9], 1.0 / D, None, ALU.mult))
                fo.do(ts(fix_c[:], xin[:], fix_s[:, 9:10], None, ALU.subtract))
                fo.do(tt(fix_q[:], fix_c[:], fix_c[:], ALU.mult))
                fo.do(v.tensor_reduce(fix_s[:, 8:9], fix_q[:], AX.X, ALU.add))
                fo.do(ts(fix_s[:, 9:10], fix_s[:, 8:9], 1.0 / D, EPS, ALU.mult, ALU.add))
                at_step[f"variance {n}"] = fo.n
                dve.wait_ge(fix["act"], 3 * n + 1)
                fo.do(v.reciprocal(fix_s[:, 11:12], fix_s[:, 10:11]))

            dve.wait_ge(fix_in, 16)
            dve.wait_ge(fix["pe"], 1)
            dve.wait_ge(e1["head"], KE)
            fo.did(tt(fix_sum[:, 0:D], bank(0)[:, 0:D], hsum[:, 0:D], ALU.add))
            fix_norm(0, fix_x)
            fo.do(ts(fix_sum[:, 0:D], fix_sum[:, 0:D], fix_s[:, 7:8], None, ALU.mult))
            fo.do(ts(fix_s[:, 8:9], fix_s[:, 11:12], fix_s[:, 7:8], fix_s[:, 7:8], ALU.mult, ALU.mult))
            fo.do(ts(fix_c[:], fix_c[:], 0.0, fix_s[:, 8:9], ALU.max, ALU.mult))
            fo.do(tt(fix_two[:, 0:D], fix_c[:], fix_sum[:, 0:D], ALU.add))
            at_step["fix a"] = fo.n
            dve.wait_ge(fix["pe"], 4)
            fo.did(ts(fix_g1[:], bank(3)[:, 0:D], fix_s[:, 7:8], None, ALU.mult))
            at_step["fix 0"] = fo.n
            assert fo.n == FIX_1_STEPS, fo.n

            clear(5)

            def step_e2(g, q, u):
                dve.wait_ge(e2_got[q], 16 * GT * (u + 1))
                sum_group(e2, g, q, D)
                dve.wait_ge(e2_in[q], 32 * (u + 1))
                after(dve, e2_kept[q], 32 * u)
                after(dve, e2_sent[q], 16 * GT * u)
                dve.wait_ge(e2["run"], GT * (g + 1))
                x1 = eslot(4 + q)
                link(tt(cols(x1), rows_e[:, q, :, 0:D], cols(eslot(2 + q)), ALU.add), e2["rows"], 9 * g + 1)
                link(tt(cols(x1), cols(x1), wide(dinv_e[:, bass.ds(g * GT, GT)], GT), ALU.mult), e2["rows"], 9 * g + 2)
                link(tt(x1, x1, eslot(q), ALU.add), e2["rows"], 9 * g + 3)
                link(tt(cols(x1), cols(x1), b2_over(GT), ALU.add), e2["rows"], 9 * g + 4)
                centre(e2, g, estat[:], GT, x1, eslot(2 + q))
                place(g, placed + 4 * g)
                deviation(e2, g, estat[:], eslot(8))
                relu_times(eslot(6 + q), eslot(2 + q), estat[:, 4, :], GT).then_inc(e2["h"], 1)

            over_groups(dve, step_e2)

            dve.wait_ge(fix["pe"], 5)
            dve.wait_ge(e2["head"], KE)
            fo.do(tt(fix_sum[:, 0:D], bank(0)[:, 0:D], hsum[:, 0:D], ALU.add))
            fo.do(tt(fix_sum[:, 0:D], fix_sum[:, 0:D], fix_g1[:], ALU.add))
            fo.do(ts(fix_sum[:, 0:D], fix_sum[:, 0:D], fix_s[:, 7:8], None, ALU.mult))
            fo.do(tt(fix_x1[:], fix_sum[:, 0:D], fix_x[:], ALU.add))
            fo.do(tt(fix_x1[:], fix_x1[:], b2_sb[:], ALU.add))
            fix_norm(1, fix_x1)
            fo.did(ts(fix_h[:], fix_c[:], 0.0, fix_s[:, 11:12], ALU.max, ALU.mult))
            at_step["fix 1"] = fo.n

            o = Order(dve, sort)
            o.n = placed + 4 * GE
            o.wait()
            o.do(v.tensor_copy(tmp_i[:], pos[:]))
            o.did(ts(tmp_j[:], tmp_i[:], P - 1, None, ALU.bitwise_and))
            o.do(ts(dsafe[:], tmp_i[:], 7, None, ALU.logical_shift_right))
            o.did(stt(out=slot_row[:], in0=tmp_j[:], scalar=float(KS), in1=dsafe[:], op0=ALU.mult, op1=ALU.add))
            at_step["slot rows"] = o.n
            goes_on, ends = lo_key, hi_key
            o.did(v.tensor_copy(goes_on[:, 0:KE - 1], same[:, 1:KE]))
            o.do(v.memset(goes_on[:, KE - 1:KE], 1.0))
            o.do(ts(ends[:], goes_on[:], -1.0, 1.0, ALU.mult, ALU.add))

            dve.wait_ge(fix["sent"], 64)

            def step_perm(s, q, u, kind):
                g = GE - 1 - s
                dve.wait_ge(c_hd[q], 16 * (u + 1))
                after(dve, c["hf"], GT * s)
                dve.sem_inc(waits_over["dve"], 1)
                link(tt(cols(eslot(2)), cols(eslot(q)), wide(ends[:, bass.ds(g * GT, GT)], GT), ALU.mult), c["tmp"], s + 1)
                after(dve, c_sent[q], 16 * GT * u)
                for j in range(GT):
                    k = GT - 1 - j
                    if j:
                        later = perm_rows[:, q, k + 1, D + 2:RW]
                    else:
                        later = h_last[:] if isinstance(s, int) and s == 0 else perm_rows[:, 1 - q, 0, D + 2:RW]
                    after(dve, c["hf"], GT * s + j)
                    stt(out=perm_rows[:, q, k, D + 2:RW], in0=later, scalar=goes_on[:, bass.ds(g * GT + k, 1)],
                        in1=cols(eslot(2))[:, k, :], op0=ALU.mult, op1=ALU.add).then_inc(c["hf"], 1)

            over_perm(dve, step_perm)

            o.did(v.tensor_copy(tile_rel[0:1, 0, :], tile_no[:]))
            o.do(v.memset(tile_rel[0:1, 1, :], 0.0))
            for r in range(R - 1):
                o.do(stt(out=tile_rel[0:1, 1, :], in0=tile_rel[0:1, 0, :], scalar=cnt[0:1, 2, r:r + 1],
                         in1=tile_rel[0:1, 1, :], op0=ALU.is_ge, op1=ALU.add))
            o.did(v.tensor_copy(tile_reli[:], tile_rel[0:1, 1, :]))
            at_step["tiles"] = o.n

            def rel_work(j, s, q, u):
                dve.wait_ge(rel_in[s], 16 * (u + 1))
                after(dve, rel_sent[s], 16 * GS * u)
                number = slot_w.bitcast(I32)[:, s, :, D + 1]
                link(ts(slot_e[:, s, :], number, 0.0, float(ROW_SKIP), ALU.is_equal, ALU.mult), rel["idx"], 2 * j + 1)
                link(tt(slot_idx[:, s, :], slot_e[:, s, :], number, ALU.add), rel["idx"], 2 * j + 2)
                made = bank(2 + q).rearrange("p (k f) -> p k f", f=P)
                dve.wait_ge(rel["tr"], j + 1)
                tt(slot_z[:, q], made[:, :, 0:D], slot_w[:, s, :, 0:D], ALU.add).then_inc(rel["z"], 1)
                dve.wait_ge(rel["th"], j + 1)
                link(tt(slot_q[:, q], slot_th[:, q], made[:, :, D:P], ALU.mult), rel["q"], j + 1)
                v.tensor_reduce(slot_w[:, s, :, WW - 1], slot_q[:, q], AX.X, ALU.add).then_inc(rel["att"], 1)

            over_slots(rel_work, dve)

            o = Order(dve, soft)
            dve.wait_ge(edges_in, 32)
            edge_rows = arena[:].rearrange("p (t w) -> p t w", w=MW)
            att, bwd, pen, mx, arg = lo_key, hi_key, tmp_a, pos, tmp_b
            o.did(v.tensor_copy(att[:], edge_rows[:, :, D]))
            o.do(ts(pen[:], same[:], -1.0, FAR, ALU.add, ALU.mult))
            o.did(v.memset(edge_rows[:, :, D], 1.0))
            o.do(v.tensor_tensor_scan(out=arg[:, 0:KE], data0=pen[:, 0:KE], data1=att[:], initial=-FAR,
                                      op0=ALU.add, op1=ALU.max))
            o.do(v.tensor_tensor_scan(out=bwd[:][:, ::-1], data0=pen[:, 1:KE + 1][:, ::-1], data1=arg[:, 0:KE][:, ::-1],
                                      initial=-FAR, op0=ALU.add, op1=ALU.max))
            o.did(ts(diag[:], ident[:], key[:, KE - 1:KE], None, ALU.mult))
            o.did(ts(diag_max[:, 0, :], ident[:], arg[:, KE - 1:KE], None, ALU.mult))
            o.did(ts(diag_max[:, 1, :], ident[:], bwd[:, 0:1], None, ALU.mult))
            at_step["last segments"] = o.n
            dve.wait_ge(soft_pe, 1)
            last_keys = bank(0)[:, 0:P]
            for n, k in enumerate((0, KE - 1)):
                o.did(ts(seen[:, 0:P], last_keys, key[:, k:k + 1], -1.0, ALU.is_equal, ALU.add))
                o.do(ts(seen[:, P:2 * P], first_row[:], key[:, k:k + 1], -1.0, ALU.is_equal, ALU.add))
                o.do(stt(out=seen, in0=seen, scalar=FAR, in1=bank(0)[:, P:3 * P], op0=ALU.mult, op1=ALU.add))
                o.do(v.tensor_reduce(smax[:, n:n + 1], seen, AX.X, ALU.max))
            for n, k in enumerate((0, KE - 1)):
                o.do(ts(arg[:, 0:KE], key[:, 0:KE], key[:, k:k + 1], -1.0, ALU.is_equal, ALU.add))
                o.do(ts(arg[:, 0:KE], arg[:, 0:KE], FAR, smax[:, n:n + 1], ALU.mult, ALU.add))
                o.do(tt(mx[:], arg[:, 0:KE], mx[:] if n else bwd[:], ALU.max))
            o.do(tt(arg[:, 0:KE], att[:], mx[:], ALU.subtract))
            at_step["exponents"] = o.n

            clear(7)

            def f_post(g, q, u, c):
                n, w = 4 * g + c, min(4, GT - 4 * c)
                at = slice(4 * c, 4 * c + w)
                dve.wait_ge(f["low"], n + 1)
                if c == 0:
                    after(dve, f_sent[q], 16 * GT * u)
                leaky = part(chain, (4 + c % 2) * MM, [MM])[:, 0:w * P].rearrange("p (k f) -> p k f", f=P)
                low = part(chain, (2 + c % 2) * MM, [MM])[:, 0:w * P].rearrange("p (k f) -> p k f", f=P)
                o_ps = bank(2 + c % 2)[:, 0:w * P].rearrange("p (k f) -> p k f", f=P)
                link(tt(leaky, o_ps, low, ALU.max), f["leaky"], n + 1)
                link(tt(halves[:, c % 2, 0:w, :], leaky[:, :, 0:D], leaky[:, :, D:P], ALU.add), f["half"], n + 1)
                tt(cols(eslot(7 + q))[:, at, :], halves[:, c % 2, 0:w, :], cols(eslot(2 + q))[:, at, :],
                   ALU.add).then_inc(f["out"], 1)

            def step_f(g, q, u):
                if known(g, 0, GE):
                    dve.wait_ge(f["weighted"], GT * (g + 1))
                    sum_group(f, g, q, MW)
                    dve.wait_ge(f["run"], GT * (g + 1))
                    link(ts(rden[:, 0, :], rows_e[:, q, :, D], TINY, None, ALU.max), f["rows"], 3 * g + 1)
                    link(v.reciprocal(rden[:, 1, :], rden[:, 0, :]), f["rows"], 3 * g + 2)
                    link(tt(cols(eslot(6)), rows_e[:, q, :, 0:D], wide(rden[:, 1, :], GT), ALU.mult), f["rows"], 3 * g + 3)
                    dve.wait_ge(f_in[q], 32 * (u + 1))
                    after(dve, f["turned"], 4 * g)
                    two = eslot(4, 2).rearrange("p (k f) -> p k f", f=P)
                    tt(two[:, :, 0:D], cols(eslot(q)), cols(eslot(6)), ALU.add).then_inc(f["two"], 1)
                    tt(two[:, :, D:P], cols(eslot(q)), cols(eslot(6)), ALU.mult).then_inc(f["two"], 1)
                if known(g, 1, GE + 1):
                    for c in range(4):
                        f_post(g - 1, 1 - q, u - (1 - q), c)

            over_groups(dve, step_f)
            step_f(GE, 0, GE // 2)

            dve.wait_ge(fix["pe"], 6)
            dve.wait_ge(f["head"], KE)
            fo.do(tt(fix_sum[:], bank(0)[:, 0:MW], hsum[:], ALU.add))
            fo.do(ts(fix_s[:, 8:9], fix_sum[:, D:MW], TINY, None, ALU.max))
            fo.do(v.reciprocal(fix_s[:, 9:10], fix_s[:, 8:9]))
            fo.do(ts(fix_c[:], fix_sum[:, 0:D], fix_s[:, 9:10], None, ALU.mult))
            fo.did(tt(fix_two[:, 0:D], fix_c[:], fix_h[:], ALU.add))
            fo.did(tt(fix_two[:, D:P], fix_c[:], fix_h[:], ALU.mult))
            at_step["fix operands"] = fo.n
            dve.wait_ge(fix["act"], 6)
            fo.do(tt(fix_hid[:], bank(3)[:, 0:P], fix_low[:], ALU.max))
            fo.do(tt(fix_q[:], fix_hid[:, 0:D], fix_hid[:, D:P], ALU.add))
            fo.did(tt(fix_out[:], fix_q[:], fix_x1[:], ALU.add))
            at_step["fix 2"] = fo.n

        @block.gpsimd
        def _(pool):
            pool.iota(iota_i, pattern=[[1, KN]], base=0, channel_multiplier=0).then_inc(consts, 1)
            pool.iota(eidi, pattern=[[1, KE]], base=1, channel_multiplier=KE).then_inc(consts, 1)
            pool.wait_ge(filled, 1)
            pool.affine_select(out=ident[:], in_=ones[:], compare_op=ALU.is_equal, fill=0.0, base=0,
                               pattern=[[1, P]], channel_multiplier=-1).then_inc(consts, 1)
            pool.affine_select(out=upper[:], in_=ones[:], compare_op=ALU.is_gt, fill=0.0, base=0,
                               pattern=[[1, P]], channel_multiplier=-1).then_inc(consts, 1)

            def alone():
                pool.sem_inc(waits_over["pool"], 1)

            def scatter(table, idx, of, bound, signal):
                pool.indirect_dma_start(out=table[:, :], out_offset=bass.IndirectOffsetOnAxis(ap=idx, axis=0),
                                        in_=of, in_offset=None, bounds_check=bound,
                                        oob_is_err=False).then_inc(signal, 16)

            def gather(to, table, idx, signal):
                pool.indirect_dma_start(out=to, out_offset=None, in_=table[:, :],
                                        in_offset=bass.IndirectOffsetOnAxis(ap=idx, axis=0)).then_inc(signal, 16)

            pool.wait_ge(prep, at_step["safe destinations"])

            def get_x(g, q, u):
                after(pool, x_kept[q], 16 * u)
                alone()
                pool.tensor_copy(src_idx[:, q, :], dsafe[:, bass.ds(g * GT, GT)]).then_inc(x_idx, 1)
                pool.wait_ge(x_idx, g + 1)
                alone()
                for k in range(GT):
                    gather(cols(eslot(q))[:, k, :], x, src_idx[:, q, k:k + 1], x_got[q])

            def keep_x(g, q, u):
                pool.wait_ge(x_got[q], 16 * GT * (u + 1))
                alone()
                pool.dma_start(group(xd_t, g), eslot(q)).then_inc(x_kept[q], 16)

            get_x(0, 0, 0)
            get_x(1, 1, 0)
            keep_x(0, 0, 0)
            with pool.Fori(1, GE // 2) as i:
                get_x(2 * i, 0, i)
                keep_x(2 * i - 1, 1, i - 1)
                get_x(2 * i + 1, 1, i)
                keep_x(2 * i, 0, i)
            keep_x(GE - 1, 1, GE // 2 - 1)

            all_landed(pool, a_g0, STORES)

            def get(s, idx_ready, sems_got, table, g, q, u):
                pool.wait_ge(idx_ready, g + 1)
                after(pool, s["head"], GT * (g - 1))
                alone()
                for k in range(GT):
                    gather(rows_g[:, q, k, 0:D], table, src_idx[:, q, k:k + 1], sems_got[q])

            def send(table, phase, sent, g, q, of):
                pool.wait_ge(out_idx_ready, phase * GE + g + 1)
                alone()
                for k in range(GT):
                    scatter(table, out_idx[:, q, k:k + 1], cols(of)[:, k, :], N - 1, sent[q])

            def send_fix(n, table, row):
                pool.wait_ge(fix["ve"], at_step[f"fix {n}"])
                scatter(table, fix_i[:, 0:1], row[:], N - 1, fix["sent"])

            over_groups(pool, lambda g, q, u: get(e1, e1_src, e1_got, g0_t, g, q, u))

            all_landed(pool, q_g1, ALL_QUADS)

            def send_g1(g, q, u):
                pool.wait_ge(e1["g1"], 2 * (g + 1))
                send(g1_t, 0, e1_sent, g, q, eslot(7 + q))

            over_groups(pool, send_g1)
            send_fix(0, g1_t, fix_g1)
            all_landed(pool, e1_sent, ALL)
            pool.wait_ge(fix["sent"], 16)

            def send_e2(g, q, u):
                pool.wait_ge(e2["h"], g + 1)
                send(h_t, 1, e2_sent, g, q, eslot(6 + q))

            get(e2, e2_src, e2_got, g1_t, 0, 0, 0)
            get(e2, e2_src, e2_got, g1_t, 1, 1, 0)
            all_landed(pool, b_h, STORES)
            send_e2(0, 0, 0)
            with pool.Fori(1, GE // 2) as i:
                get(e2, e2_src, e2_got, g1_t, 2 * i, 0, i)
                send_e2(2 * i - 1, 1, i - 1)
                get(e2, e2_src, e2_got, g1_t, 2 * i + 1, 1, i)
                send_e2(2 * i, 0, i)
            send_e2(GE - 1, 1, GE // 2 - 1)
            send_fix(1, h_t, fix_h)
            all_landed(pool, e2_kept, 32 * (GE // 2))
            scatter(hd_t, hd_i[:, 0:1], fix_h[:], EPAD - 1, fix["sent"])
            all_landed(pool, e2_sent, ALL)
            pool.wait_ge(fix["sent"], 48)

            gather(h_last[:], h_t, last_i[:, 0:1], fix["sent"])

            def send_perm(s, q, u, kind):
                pool.wait_ge(c_ef[q], features_in(u, kind))
                pool.wait_ge(c_meta, s + 1)
                pool.wait_ge(out_idx_ready, 2 * GE + s + 1)
                pool.wait_ge(c["hf"], GT * (s + 1))
                alone()
                for k in range(GT):
                    scatter(slot_t, out_idx[:, q, k:k + 1], perm_rows[:, q, k, :], P * KS - 1, c_sent[q])

            over_perm(pool, send_perm)

            def rel_get(j, s, u):
                pool.wait_ge(rel_in[s], 16 * (u + 1))
                alone()
                for k in range(GS):
                    gather(slot_w[:, s, k, RW:RW + D], h_t, slot_w[:, s, k, D:D + 1].bitcast(I32), rel_got[s])

            def rel_send(j, s):
                pool.wait_ge(rel["idx"], 2 * j + 2)
                pool.wait_ge(rel["att"], j + 1)
                alone()
                for k in range(GS):
                    scatter(edge_t, slot_idx[:, s, k:k + 1], slot_w[:, s, k, RW:WW], EPAD, rel_sent[s])

            def step_rel(j, s, q, u):
                rel_get(j, s, u)
                if known(j, 2, NGS):
                    rel_send(j - 2, (s - 2) % SB)

            over_slots(step_rel, pool)
            for j in range(NGS - 2, NGS):
                rel_send(j, j % SB)

            all_landed(pool, b_out, [STORES[0] + 16, STORES[1]])

            def send_f(g, q, u):
                pool.wait_ge(f["out"], 4 * (g + 1))
                send(out, 3, f_sent, g, q, eslot(7 + q))

            over_groups(pool, send_f)
            send_fix(2, out, fix_out)
            all_landed(pool, f_sent, ALL)
            pool.wait_ge(fix["sent"], 80)

        @block.scalar
        def _(act):
            copy, activation = nc.scalar.copy, nc.scalar.activation
            act.wait_ge(deg_read, 1)
            activation(degs[:, 1, :], degs[:, 0, :], ACT.Sqrt).then_inc(deg_root, 1)

            def square(s, n, xc, sq):
                act.wait_ge(s["centered"], n + 1)
                buffers = 2 if s is A or s is B else 1
                after(act, s["rows"], row_steps(s, n - buffers, 3))
                activation(sq, xc, ACT.Square).then_inc(s["square"], 1)

            def root(s, n, st):
                act.wait_ge(s["rows"], row_steps(s, n, 4))
                activation(st[:, 3, :], st[:, 2, :], ACT.Sqrt).then_inc(s["std"], 1)

            act.wait_ge(prep, at_step["edge degrees"])
            activation(tmp_b[:, 0:KE], tmp_a[:, 0:KE], ACT.Sqrt).then_inc(prep_act, 1)
            act.wait_ge(prep, at_step["fix degrees"])
            activation(fix_s[:, 6:7], fix_s[:, 5:6], ACT.Sqrt).then_inc(prep_act, 1)

            def index(ring, of, g, q, signal):
                copy(ring[:, q, :], of[:, bass.ds(g * GT, GT)]).then_inc(signal, 1)

            def quad_turned(n, q):
                act.wait_ge(Q["turned"], n + 1)
                after(act, Q["h"], n - 1)
                copy(part(chain, q * MM, [MM]), bank(q)).then_inc(Q["at"], 1)

            def quad_hidden(n, q):
                act.wait_ge(Q["h"], n + 1)
                after(act, Q["u"], n - 1)
                activation(part(chain, 2 * MM + q * 2 * MM, [2 * MM]), bank(2 + q * 2, 2), ACT.Relu,
                           bias=b1_sb[:, 0:1]).then_inc(Q["relu"], 1)

            def quad_u(n, q, u):
                act.wait_ge(Q["u"], n + 1)
                after(act, q_g1[q], 16 * u)
                after(act, Q["x1"], 2 * (n - 1))
                copy(quad_buffer(2 + q), bank(6 + q)).then_inc(Q["g1"], 1)

            def quad(n, q, u, between=None):
                if known(n, 0, NQ - 1):
                    quad_turned(n + 1, 1 - q)
                if between:
                    between()
                quad_hidden(n, q)
                if known(n, 1, NQ):
                    quad_u(n - 1, 1 - q, u - (1 - q))

            def step_a(b, q, u):
                square(A, b, slot(2 + q), slot(4 + q))
                if isinstance(b, int) and b == 1:
                    quad_turned(0, 0)
                if known(b, 1, NB):
                    quad(b - 1, 1 - q, u - (1 - q), lambda: root(A, b, stat[:, q]))
                else:
                    root(A, b, stat[:, q])

            for b in range(4):
                step_a(b, b % 2, b // 2)
            with act.Fori(2, NB // 2) as i:
                step_a(2 * i, 0, i)
                step_a(2 * i + 1, 1, i)
            step_a(NB - 1, 0, NB // 2)

            all_landed(act, x_kept, 16 * (GE // 2))
            index(src_idx, meta[:, :, 0], 0, 0, e1_src)

            def step_e1(g, q, u):
                n, half = Q_A + 2 * g, Q_A // 2 + g
                if known(g, 0, GE - 1):
                    after(act, e1_got[1 - q], 16 * GT * (u + q))
                    index(src_idx, meta[:, :, 0], g + 1, 1 - q, e1_src)
                quad(n, 0, half, lambda: square(e1, g, eslot(2), eslot(3)))
                quad(n + 1, 1, half, lambda: root(e1, g, estat[:]))

            step_e1(0, 0, 0)
            step_e1(1, 1, 0)
            with act.Fori(1, GE // 2 - 1) as i:
                step_e1(2 * i, 0, i)
                step_e1(2 * i + 1, 1, i)
            step_e1(GE - 2, 0, GE // 2 - 1)
            step_e1(GE - 1, 1, GE // 2 - 1)
            over_quads(act, quad)
            quad_u(NQ - 1, 1, NQ // 2 - 1)

            def e1_turn(g, c):
                n, w = 2 * g + c, (4 - c) * P
                act.wait_ge(e1["turned"], n + 1)
                after(act, e1["h"], n - 1)
                copy(part(chain, c * MM, [MM])[:, 0:w], bank(0)[:, 0:w]).then_inc(e1["at"], 1)

            def e1_relu(g, c):
                n, w = 2 * g + c, (4 - c) * P
                act.wait_ge(e1["h"], n + 1)
                after(act, e1["u"], n - 1)
                activation(part(chain, 2 * MM + c * 2 * MM, [2, MM])[:, :, 0:w], banks[:, 2:4, 0:w], ACT.Relu,
                           bias=b1_sb[:, 0:1]).then_inc(e1["relu"], 1)

            def b_turn(b, z):
                n = 4 * b + z
                act.wait_ge(B["turned"], n + 1)
                after(act, B["o"], n - 1)
                copy(part(arena, 10 * BW + z % 2 * MM, [MM]), bank(1)).then_inc(B["t"], 1)

            def b_low(b, z):
                n = 4 * b + z
                act.wait_ge(B["o"], n + 1)
                after(act, B["leaky"], n - 1)
                nc.scalar.mul(part(arena, 10 * BW + (2 + z % 2) * MM, [MM]), bank(4 + z % 2), 0.01).then_inc(B["low"], 1)

            def step_b(g, q, u):
                after(act, e1_sent[q], 16 * GT * u)
                index(out_idx, outi, g, q, out_idx_ready)
                two, three = known(g, 1, NB + 1), known(g, 0, NB)
                e1_turn(g, 0)
                for name, c in (("b_turn", 0), ("e_relu", 0), ("b_low", 0), ("square", 0), ("b_turn", 1), ("b_low", 1), ("root", 0),
                                ("e_turn", 1), ("b_turn", 2), ("b_low", 2), ("e_relu", 1), ("b_turn", 3), ("b_low", 3)):
                    if name == "e_turn":
                        e1_turn(g, c)
                    if name == "e_relu":
                        e1_relu(g, c)
                    if name == "b_turn" and two:
                        b_turn(g - 1, c)
                    if name == "b_low" and two:
                        b_low(g - 1, c)
                    if name == "square" and three:
                        square(B, g, slot(2 + q), slot(4 + q))
                    if name == "root" and three:
                        root(B, g, stat[:, q])

            over_both(act, step_b)

            act.wait_ge(fix["ve"], at_step["variance 0"])
            activation(fix_s[:, 10:11], fix_s[:, 9:10], ACT.Sqrt).then_inc(fix["act"], 1)
            act.wait_ge(fix["pe"], 2)
            copy(fix_t[0:D, :], bank(1)[0:D, 0:P]).then_inc(fix["act"], 1)
            act.wait_ge(fix["pe"], 3)
            activation(fix_hid[:], bank(2)[:, 0:P], ACT.Relu, bias=b1_sb[:, 0:1]).then_inc(fix["act"], 1)

            all_landed(act, e1_sent, ALL)

            def step_e2(g, q, u):
                if known(g, 0, GE - 1):
                    after(act, e2_got[1 - q], 16 * GT * (u + q))
                    index(src_idx, meta[:, :, 0], g + 1, 1 - q, e2_src)
                after(act, e2_sent[q], 16 * GT * u)
                index(out_idx, outi, g, q, out_idx_ready)
                square(e2, g, eslot(2 + q), eslot(8))
                root(e2, g, estat[:])

            index(src_idx, meta[:, :, 0], 0, 0, e2_src)
            step_e2(0, 0, 0)
            step_e2(1, 1, 0)
            with act.Fori(1, GE // 2 - 1) as i:
                step_e2(2 * i, 0, i)
                step_e2(2 * i + 1, 1, i)
            step_e2(GE - 2, 0, GE // 2 - 1)
            step_e2(GE - 1, 1, GE // 2 - 1)

            act.wait_ge(fix["ve"], at_step["variance 1"])
            activation(fix_s[:, 10:11], fix_s[:, 9:10], ACT.Sqrt).then_inc(fix["act"], 1)

            all_landed(act, e2_sent, ALL)
            act.wait_ge(sort, at_step["slot rows"])

            def step_perm(s, q, u, kind):
                g = GE - 1 - s
                after(act, c_sent[q], 16 * GT * u)
                copy(perm_rows.bitcast(I32)[:, q, :, D:D + 2], meta[:, bass.ds(g * GT, GT), :]).then_inc(c_meta, 1)
                index(out_idx, slot_row, g, q, out_idx_ready)

            over_perm(act, step_perm)

            def rel_turn(j, q):
                act.wait_ge(rel["turned"], j + 1)
                after(act, rel["tr"], j - 1)
                copy(slot_ht[:, q], bank(q).rearrange("p (k s) -> p k s", s=P)).then_inc(rel["ht"], 1)

            def rel_tanh(j, q):
                act.wait_ge(rel["z"], j + 1)
                after(act, rel["q"], j - 1)
                activation(slot_th[:, q], slot_z[:, q], ACT.Tanh).then_inc(rel["th"], 1)

            def step_rel(j, s, q, u):
                if known(j, 0, NGS - 1):
                    rel_turn(j + 1, 1 - q)
                rel_tanh(j, q)

            rel_turn(0, 0)
            over_slots(step_rel, act)

            act.wait_ge(soft, at_step["exponents"])
            activation(tmp_a[:, 0:KE], tmp_b[:, 0:KE], ACT.Exp).then_inc(soft_exp, 1)
            act.wait_ge(soft_exp, 1)

            all_landed(act, c_sent, ALL)
            edge_rows = arena[:].rearrange("p (t w) -> p t w", w=MW)

            def weigh(g, q):
                after(act, f["head"], GT * (g - 1))
                for k in range(GT):
                    t = g * GT + k
                    activation(rows_g[:, q, k, :], edge_rows[:, bass.ds(t, 1), :].rearrange("p a w -> p (a w)"), ACT.Copy,
                               scale=tmp_a[:, bass.ds(t, 1)]).then_inc(f["weighted"], 1)

            def f_turned(g, c):
                n, w = 4 * g + c, min(4, GT - 4 * c) * P
                act.wait_ge(f["turned"], n + 1)
                after(act, f["o"], n - 1)
                copy(part(chain, c % 2 * MM, [MM])[:, 0:w], bank(c % 2)[:, 0:w]).then_inc(f["t"], 1)

            def f_low(g, c):
                n, w = 4 * g + c, min(4, GT - 4 * c) * P
                act.wait_ge(f["o"], n + 1)
                after(act, f["leaky"], n - 1)
                nc.scalar.mul(part(chain, (2 + c % 2) * MM, [MM])[:, 0:w], bank(2 + c % 2)[:, 0:w], 0.01).then_inc(f["low"], 1)

            def step_f(g, q, u):
                if known(g, 1, GE + 1):
                    f_turned(g - 1, 0)
                    for c in range(4):
                        if c < 3:
                            f_turned(g - 1, c + 1)
                        f_low(g - 1, c)
                if known(g, 0, GE - 1):
                    weigh(g + 1, 1 - q)
                if known(g, 0, GE):
                    after(act, f_sent[q], 16 * GT * u)
                    index(out_idx, outi, g, q, out_idx_ready)

            weigh(0, 0)
            step_f(0, 0, 0)
            step_f(1, 1, 0)
            with act.Fori(1, GE // 2 - 1) as i:
                step_f(2 * i, 0, i)
                step_f(2 * i + 1, 1, i)
            for g in range(GE - 2, GE + 1):
                step_f(g, g % 2, g // 2)
            act.wait_ge(fix["pe"], 7)
            copy(fix_t[:], bank(1)[:, 0:P]).then_inc(fix["act"], 1)
            act.wait_ge(fix["pe"], 8)
            nc.scalar.mul(fix_low[:], bank(3)[:, 0:P], 0.01).then_inc(fix["act"], 1)

        @block.tensor
        def _(pe):
            matmul, transpose = nc.tensor.matmul, nc.tensor.transpose
            pe.wait_ge(loaded, 16 * N_LOADS)
            pe.wait_ge(consts, 4)

            def count(t, k):
                pe.wait_ge(hot_made, 2 * (t + 1))
                first, last = isinstance(t, int) and t == 0, isinstance(t, int) and t == KE - 1
                matmul(banks[:, 0, 0:KN // 2], lo_hot[:, k % 4, :], hi_hot[:, k % 4, 0:KN // 2],
                       start=first, stop=last, skip_group_check=True)
                matmul(banks[:, 1, 0:KN // 2], lo_hot[:, k % 4, :], hi_hot[:, k % 4, KN // 2:KN],
                       start=first, stop=last, skip_group_check=True).then_inc(hot_used, 1)

            for k in range(8):
                count(k, k)
            with pe.Fori(1, KE // 8 - 1) as i:
                for k in range(8):
                    count(8 * i + k, k)
            for k in range(8):
                count(KE - 8 + k, k)

            pe.wait_ge(prep, at_step["first keys"])
            matmul(bank(0)[:, 0:P], ones[:], diag[:], start=True, stop=True)
            transpose(bank(0)[:, P:2 * P], res_in[:], ident[:])
            transpose(bank(0)[:, 2 * P:3 * P], fix_two[:], ident[:]).then_inc(prep_pe, 1)
            pe.wait_ge(prep, at_step["carry"])
            matmul(bank(0)[:, 0:1], carry[:], fix_s[:, 2:3], start=True, stop=True).then_inc(prep_pe, 1)
            pe.wait_ge(prep, at_step["fix degrees"])

            def hidden(to, at, w):
                matmul(bank(to)[:, 0:w], w1_sb[0:D, :], at[0:D, 0:w], start=True, stop=True)
                return matmul(bank(to + 1)[:, 0:w], w1_sb[D:P, :], at[D:P, 0:w], start=True, stop=True)

            def output(to, hid, tiles):
                for k in range(tiles):
                    at = k % 2 * MM + k // 2 * P
                    ins = matmul(bank(to)[:, k * D:(k + 1) * D], hid[:, at:at + P], w2_sb[:], start=True, stop=True)
                return ins

            def quad_turn(n, q, u):
                pe.wait_ge(q_g0[q], 16 * (u + 1))
                after(pe, Q["at"], n - 1)
                for k in range(CQ // 2):
                    ins = transpose(bank(q)[:, k * P:(k + 1) * P], quad_buffer(q)[:, k * P:(k + 1) * P], ident[:])
                ins.then_inc(Q["turned"], 1)

            def quad_output(n, q):
                pe.wait_ge(Q["relu"], n + 1)
                after(pe, Q["g1"], n - 1)
                output(6 + q, part(chain, 2 * MM + q * 2 * MM, [2 * MM]), CQ).then_inc(Q["u"], 1)

            def quad(n, q, u):
                if known(n, 0, NQ - 1):
                    quad_turn(n + 1, 1 - q, u + q)
                pe.wait_ge(Q["at"], n + 1)
                after(pe, Q["relu"], n - 1)
                hidden(2 + q * 2, part(chain, q * MM, [MM]), MM).then_inc(Q["h"], 1)
                if known(n, 1, NQ):
                    quad_output(n - 1, 1 - q)

            quad_turn(0, 0, 0)
            for n in range(4):
                quad(n, n % 2, n // 2)
            with pe.Fori(2, NQ // 2 - 1) as i:
                quad(2 * i, 0, i)
                quad(2 * i + 1, 1, i)
            quad(NQ - 2, 0, NQ // 2 - 1)
            quad(NQ - 1, 1, NQ // 2 - 1)
            quad_output(NQ - 1, 1)
            pe.wait_ge(Q["g1"], NQ)

            pe.wait_ge(sort, at_step["counts"])
            matmul(bank(1)[:, 0:R], ones[:], cnt[:, 0, :], start=True, stop=True)
            matmul(bank(1)[:, R:2 * R], upper[:], cnt[:, 0, :], start=True, stop=True).then_inc(prep_pe, 1)
            pe.wait_ge(sort, at_step["totals read"])

            def e1_turn(g, q, u, c):
                n, pairs = 2 * g + c, 4 - c
                pe.wait_ge(e1_in[q], 16 * (GE // 2 + u + 1))
                after(pe, e1["at"], n)
                for k in range(pairs):
                    at = (8 * c + 2 * k) * D
                    ins = transpose(bank(0)[:, k * P:(k + 1) * P], eslot(5 + q)[:, at:at + P], ident[:])
                ins.then_inc(e1["turned"], 1)

            def e1_hidden(g, c):
                n = 2 * g + c
                pe.wait_ge(e1["at"], n + 1)
                after(pe, e1["relu"], n)
                hidden(2, part(chain, c * MM, [MM]), (4 - c) * P).then_inc(e1["h"], 1)

            def e1_output(g, c):
                n = 2 * g + c
                pe.wait_ge(e1["relu"], n + 1)
                after(pe, e1["g1"], n - 1)
                output(6 + c, part(chain, 2 * MM + c * 2 * MM, [2 * MM]), 8 - 2 * c).then_inc(e1["u"], 1)

            def b_turn(b, q, z):
                n = 4 * b + z
                pe.wait_ge(B["h"], b + 1)
                after(pe, B["t"], n)
                for k in range(4):
                    at = (8 * z + 2 * k) * D
                    ins = transpose(bank(1)[:, k * P:(k + 1) * P], slot(6 + q)[:, at:at + P], ident[:])
                ins.then_inc(B["turned"], 1)

            def b_residual(b, z):
                n = 4 * b + z
                pe.wait_ge(B["t"], n + 1)
                after(pe, B["leaky"], n - 1)
                t = part(arena, 10 * BW + z % 2 * MM, [MM])
                for k in range(4):
                    at = slice(k * P, (k + 1) * P)
                    ins = matmul(bank(4 + z % 2)[:, at], t[:, at], res1_sb[:], start=True, stop=True)
                ins.then_inc(B["o"], 1)

            def step_b(g, q, u):
                two = known(g, 1, NB + 1)
                for name, k in (("e_turn", 0), ("b_turn", 0), ("e_hidden", 0), ("b_res", 0), ("b_turn", 1), ("e_output", 0),
                                ("b_res", 1), ("e_turn", 1), ("b_turn", 2), ("b_res", 2), ("e_hidden", 1), ("b_turn", 3),
                                ("b_res", 3), ("e_output", 1)):
                    if name == "e_turn":
                        e1_turn(g, q, u, k)
                    if name == "e_hidden":
                        e1_hidden(g, k)
                    if name == "e_output":
                        e1_output(g, k)
                    if name == "b_turn" and two:
                        b_turn(g - 1, 1 - q, k)
                    if name == "b_res" and two:
                        b_residual(g - 1, k)

            over_both(pe, step_b)

            def carried(s, width, n):
                pe.wait_ge(s["run"], KE)
                matmul(bank(0)[:, 0:width], carry[:], rows_e[:, 1, GT - 1, 0:width],
                       start=True, stop=True).then_inc(fix["pe"], 1)

            carried(e1, D, 0)
            pe.wait_ge(fix["ve"], at_step["fix a"])
            transpose(bank(1)[0:D, 0:P], fix_two[:, 0:D], ident[:]).then_inc(fix["pe"], 1)
            pe.wait_ge(fix["act"], 2)
            matmul(bank(2)[:, 0:P], w1_sb[0:D, :], fix_t[0:D, :], start=True, stop=True).then_inc(fix["pe"], 1)
            pe.wait_ge(fix["act"], 3)
            matmul(bank(3)[:, 0:D], fix_hid[:], w2_sb[:], start=True, stop=True).then_inc(fix["pe"], 1)

            carried(e2, D, 1)

            def rel_turn(j, s, q, u):
                pe.wait_ge(rel_got[s], 16 * GS * (u + 1))
                after(pe, rel["ht"], j - 1)
                for k in range(GS):
                    ins = transpose(bank(q)[:, k * P:(k + 1) * P], slot_w[:, s, k, D + 2:WW - 1], ident[:])
                ins.then_inc(rel["turned"], 1)

            def rel_project(j, q):
                number = [pe.value_load(tile_reli[0:1, bass.ds(j * GS + k, 1)], min_val=0, max_val=R - 1)
                          for k in range(GS)]
                pe.wait_ge(rel["ht"], j + 1)
                after(pe, rel["q"], j - 1)
                flat = rel_sb.rearrange("p r f -> p (r f)")
                for k in range(GS):
                    ins = matmul(bank(2 + q)[:, k * P:(k + 1) * P], slot_ht[:, q, k, :],
                                 flat[:, bass.ds(number[k] * P, P)], start=True, stop=True)
                ins.then_inc(rel["tr"], 1)

            pe.wait_ge(sort, at_step["tiles"])
            pe.wait_ge(loaded, 16 * (N_LOADS + 2))

            def step_rel(j, s, q, u):
                if known(j, 0, NGS - 1):
                    rel_turn(j + 1, (s + 1) % SB, 1 - q, u + (s + 1) // SB)
                rel_project(j, q)

            rel_turn(0, 0, 0, 0)
            over_slots(step_rel, pe)

            pe.wait_ge(soft, at_step["last segments"])
            for k, d in enumerate((diag[:], diag_max[:, 0, :], diag_max[:, 1, :])):
                ins = matmul(bank(0)[:, k * P:(k + 1) * P], ones[:], d, start=True, stop=True)
            ins.then_inc(soft_pe, 1)

            def f_turn(g, c):
                n = 4 * g + c
                pe.wait_ge(f["two"], 2 * (g + 1))
                after(pe, f["t"], n - 1)
                for k in range(min(4, GT - 4 * c)):
                    at = (4 * c + k) * P
                    ins = transpose(bank(c % 2)[:, k * P:(k + 1) * P], eslot(4, 2)[:, at:at + P], ident[:])
                ins.then_inc(f["turned"], 1)

            def f_residual(g, c):
                n = 4 * g + c
                pe.wait_ge(f["t"], n + 1)
                after(pe, f["leaky"], n - 1)
                for k in range(min(4, GT - 4 * c)):
                    at = slice(k * P, (k + 1) * P)
                    ins = matmul(bank(2 + c % 2)[:, at], part(chain, c % 2 * MM, [MM])[:, at], res_sb[:], start=True, stop=True)
                ins.then_inc(f["o"], 1)

            def step_f(g, q, u):
                f_turn(g, 0)
                for c in range(4):
                    if c < 3:
                        f_turn(g, c + 1)
                    f_residual(g, c)

            pe.wait_ge(soft_exp, 1)
            over_groups(pe, step_f)
            carried(f, MW, 2)
            pe.wait_ge(fix["ve"], at_step["fix operands"])
            transpose(bank(1)[:, 0:P], fix_two[:], ident[:]).then_inc(fix["pe"], 1)
            pe.wait_ge(fix["act"], 5)
            matmul(bank(3)[:, 0:P], fix_t[:], res_sb[:], start=True, stop=True).then_inc(fix["pe"], 1)


_INS = ["x", "src", "dst", "edge_attr_64", "edge_type_32", "L0_gnn_W1", "L0_gnn_b1", "L0_gnn_W2", "L0_gnn_b2",
        "L1_gnn_relation_weight", "L1_gnn_res_w1", "L1_gnn_res_w2"]


def kernel(**inputs):
    import numpy as _np
    import concourse.bacc as _bacc
    from concourse import mybir as _mybir
    from concourse.bass_utils import run_bass_kernel_spmd as _run

    nc = _bacc.Bacc("TRN2", target_bir_lowering=False, num_devices=1)
    arrays, args = {}, []
    for name in _INS:
        a = _np.ascontiguousarray(inputs[name])
        arrays[f"in_{name}"] = a
        args.append(nc.dram_tensor(f"in_{name}", a.shape, _mybir.dt.from_np(a.dtype), kind="ExternalInput").ap())
    args.append(nc.dram_tensor("result", (N, D), F32, kind="ExternalOutput").ap())
    build(nc, *args)
    return _run(nc, [arrays], core_ids=[0]).results[0]["result"]
```
